# Optimizing a Trainium2 kernel written in Bass

```python
import numpy as np
import jax
import jax.numpy as jnp

def _softmax(x, axis=-1):
    return jax.nn.softmax(x, axis=axis)

def _gelu(x):
    return jax.nn.gelu(x, approximate=True)

def _silu(x):
    return jax.nn.silu(x)

def _sigmoid(x):
    return jax.nn.sigmoid(x)

def _layernorm(x, axis=-1, eps=1e-05):
    m = jnp.mean(x, axis=axis, keepdims=True)
    v = jnp.var(x, axis=axis, keepdims=True)
    return (x - m) / jnp.sqrt(v + eps)

def _scatter_add(tgt, idx, src, axis=0):
    return tgt.at[idx].add(src)

def _segment_sum(src, seg, n):
    return jax.ops.segment_sum(src, seg, n)
kernel_name = 'mk_flamingo_gated_d4_seqx_r4_acd38b'

def setup_inputs(seed: int=0):
    np.random.seed(seed)
    _w = jnp.asarray

    def _rec_inputs():
        import jax
        import jax.numpy as jnp
        _rk = jax.random.key(seed)
        x = -0.0005146 + 1 * jax.random.normal(jax.random.fold_in(_rk, 1), (16, 100, 256), jnp.float32)
        _lenS = 100 - jax.random.randint(jax.random.fold_in(_rk, 7), (16,), 0, max(1, 100 // 4) + 1, jnp.int32)
        _lenS2 = 361 - jax.random.randint(jax.random.fold_in(_rk, 8), (16,), 0, max(1, 361 // 4) + 1, jnp.int32)
        _ctx_768P = jax.random.normal(jax.random.fold_in(_rk, 11), (16, 16, 192), jnp.float32)
        _ctx_768c = jax.random.dirichlet(jax.random.fold_in(_rk, 511), 0.3 * jnp.ones((16,), jnp.float32), (16, 361))
        _ctx_768t = jnp.einsum('bsk,bkd->bsd', _ctx_768c, _ctx_768P)
        _ctx_768t = _ctx_768t * jax.lax.rsqrt(jnp.mean(jnp.square(_ctx_768t)) + 1e-12) * 0.953939
        ctx_768 = -0.00040386 + 0.999972 * (_ctx_768t + 0.3 * jax.random.normal(jax.random.fold_in(_rk, 611), (16, 361, 192), jnp.float32))
        _validS = jnp.arange(100)[None, :] < _lenS[:, None]
        _validS2 = jnp.arange(361)[None, :] < _lenS2[:, None]
        _causal = jnp.tril(jnp.ones((100, 100), dtype=bool))
        mask_BxS2_bk0 = jnp.logical_not(jnp.broadcast_to(_validS2[:, :], (16, 361)))
        _g = jax.random.normal(jax.random.fold_in(_rk, 9001), (2, 4), jnp.float32)
        _g = jnp.sign(_g) * jnp.maximum(jnp.abs(_g), 1.0) + (_g == 0) * 1.0
        g_xattn = _g[0]
        g_ffn = _g[1]
        return (x, ctx_768, mask_BxS2_bk0, g_xattn, g_ffn)
    x, ctx_768, mask_BxS2_bk0, g_xattn, g_ffn = _rec_inputs()

    def _L0_xattn_setup():
        import jax, jax.numpy as jnp
        import numpy as np
        DIM_IN, DIM_LAT, DIM_HEAD = (192, 256, 64)
        INNER = max(DIM_LAT, DIM_IN)
        HEADS = INNER // DIM_HEAD
        SCALE = DIM_HEAD ** (-0.5)
        RMS_EPS = 1e-08
        LN_EPS = 1e-05

        def layernorm(x, g, b):
            mu = jnp.mean(x, axis=-1, keepdims=True)
            var = jnp.mean((x - mu) ** 2, axis=-1, keepdims=True)
            return (x - mu) * jax.lax.rsqrt(var + LN_EPS) * g + b

        def rmsnorm(x, gamma):
            norm = jnp.sqrt(jnp.sum(x * x, axis=-1, keepdims=True)) * x.shape[-1] ** (-0.5)
            return x / jnp.maximum(norm, RMS_EPS) * gamma
        key = jax.random.key(seed)
        ks = jax.random.split(key, 12)
        b, n, m = (4, 1024, 128)
        x = jax.random.normal(ks[0], (b, n, DIM_IN), jnp.float32)
        latents = jax.random.normal(ks[1], (b, m, DIM_LAT), jnp.float32)
        mask = jax.random.randint(ks[2], (b, n), 0, 2).astype(bool)
        s = lambda k, sh, fan: jax.random.normal(k, sh, jnp.float32) * fan ** (-0.5)
        return {'x': x, 'latents': latents, 'mask': mask, 'ln_x_g': jnp.ones((DIM_IN,), jnp.float32), 'ln_x_b': jnp.zeros((DIM_IN,), jnp.float32), 'ln_l_g': jnp.ones((DIM_LAT,), jnp.float32), 'ln_l_b': jnp.zeros((DIM_LAT,), jnp.float32), 'qn_g': jnp.ones((DIM_HEAD,), jnp.float32), 'kn_g': jnp.ones((DIM_HEAD,), jnp.float32), 'Wq': s(ks[3], (INNER, DIM_LAT), DIM_LAT), 'Wkv': s(ks[4], (2 * INNER, DIM_IN), DIM_IN), 'Wlkv': s(ks[5], (2 * INNER, DIM_LAT), DIM_LAT), 'Wo': s(ks[6], (DIM_LAT, INNER), INNER), 'bo': jnp.zeros((DIM_LAT,), jnp.float32)}
    _L0_xattn_all = _L0_xattn_setup()
    _L0_xattn_in = {k: v for k, v in _L0_xattn_all.items() if k in ('ln_x_g', 'ln_x_b', 'ln_l_g', 'ln_l_b', 'qn_g', 'kn_g', 'Wq', 'Wkv', 'Wlkv', 'Wo', 'bo')}
    del _L0_xattn_all

    def _L0_ffn_setup():
        import jax, jax.numpy as jnp
        import numpy as np
        DIM = 256
        HIDDEN = 1024
        E = 8
        B, S = (2, 1024)
        key = jax.random.key(seed)
        ks = jax.random.split(key, 8)
        sd = 1.0 / np.sqrt(DIM)
        sh = 1.0 / np.sqrt(HIDDEN)
        return {'x': jax.random.normal(ks[0], (B, S, DIM), dtype=jnp.float32), 'router_w': jax.random.uniform(ks[1], (DIM, E), jnp.float32, -sd, sd), 'router_b': jax.random.uniform(ks[2], (E,), jnp.float32, -sd, sd), 'w1': jax.random.uniform(ks[3], (E, DIM, 2 * HIDDEN), jnp.float32, -sd, sd), 'b1': jax.random.uniform(ks[4], (E, 2 * HIDDEN), jnp.float32, -sd, sd), 'w2': jax.random.uniform(ks[5], (E, HIDDEN, DIM), jnp.float32, -sh, sh), 'b2': jax.random.uniform(ks[6], (E, DIM), jnp.float32, -sh, sh)}
    _L0_ffn_all = _L0_ffn_setup()
    _L0_ffn_in = {k: v for k, v in _L0_ffn_all.items() if k in ('router_w', 'router_b', 'w1', 'b1', 'w2', 'b2')}
    del _L0_ffn_all

    def _L1_xattn_setup():
        import jax, jax.numpy as jnp
        import numpy as np
        QUERY_DIM = 256
        CONTEXT_DIM = 192
        HEADS = 8
        DIM_HEAD = 64
        INNER = HEADS * DIM_HEAD
        key = jax.random.key(seed)
        ks = jax.random.split(key, 7)
        B, S, L = (8, 1024, 77)
        x = jax.random.normal(ks[0], (B, S, QUERY_DIM), dtype=jnp.float32)
        context = jax.random.normal(ks[1], (B, L, CONTEXT_DIM), dtype=jnp.float32)
        Wq = jax.random.normal(ks[2], (QUERY_DIM, INNER), dtype=jnp.float32) * QUERY_DIM ** (-0.5)
        Wk = jax.random.normal(ks[3], (CONTEXT_DIM, INNER), dtype=jnp.float32) * CONTEXT_DIM ** (-0.5)
        Wv = jax.random.normal(ks[4], (CONTEXT_DIM, INNER), dtype=jnp.float32) * CONTEXT_DIM ** (-0.5)
        Wo = jax.random.normal(ks[5], (INNER, QUERY_DIM), dtype=jnp.float32) * INNER ** (-0.5)
        bo = jax.random.normal(ks[6], (QUERY_DIM,), dtype=jnp.float32) * 0.01
        return {'x': x, 'context': context, 'Wq': Wq, 'Wk': Wk, 'Wv': Wv, 'Wo': Wo, 'bo': bo}
    _L1_xattn_all = _L1_xattn_setup()
    _L1_xattn_in = {k: v for k, v in _L1_xattn_all.items() if k in ('Wq', 'Wk', 'Wv', 'Wo', 'bo')}
    del _L1_xattn_all

    def _L1_ffn_setup():
        import jax, jax.numpy as jnp
        import numpy as np
        D_MODEL = 256
        EXPERT_DIM = 128
        N_EXPERTS = 8
        TOP_K = 2

        def _sq_relu(h):
            return jnp.square(jax.nn.relu(h))
        key = jax.random.key(seed)
        ks = jax.random.split(key, 6)
        s = 0.02
        x = jax.random.normal(ks[0], (2, 512, D_MODEL), dtype=jnp.float32)
        Ws1 = jax.random.normal(ks[1], (D_MODEL, EXPERT_DIM), dtype=jnp.float32) * s
        Ws2 = jax.random.normal(ks[2], (EXPERT_DIM, D_MODEL), dtype=jnp.float32) * s
        W1 = jax.random.normal(ks[3], (N_EXPERTS, D_MODEL, EXPERT_DIM), dtype=jnp.float32) * s
        W2 = jax.random.normal(ks[4], (N_EXPERTS, EXPERT_DIM, D_MODEL), dtype=jnp.float32) * s
        Wr = jax.random.normal(ks[5], (D_MODEL, N_EXPERTS), dtype=jnp.float32) * s
        return {'x': x, 'Ws1': Ws1, 'Ws2': Ws2, 'W1': W1, 'W2': W2, 'Wr': Wr}
    _L1_ffn_all = _L1_ffn_setup()
    _L1_ffn_in = {k: v for k, v in _L1_ffn_all.items() if k in ('Ws1', 'Ws2', 'W1', 'W2', 'Wr')}
    del _L1_ffn_all

    def _L2_xattn_setup():
        import jax, jax.numpy as jnp
        import numpy as np
        DIM_Q = 256
        DIM_KV = 192
        N_HEADS = 4

        def _split_heads(x):
            b, l, d = x.shape
            return x.reshape(b, l, N_HEADS, d // N_HEADS).transpose(0, 2, 1, 3)
        key = jax.random.key(seed)
        ks = jax.random.split(key, 7)
        b, lq, lkv = (4, 512, 512)
        q = jax.random.normal(ks[0], (b, lq, DIM_Q), dtype=jnp.float32)
        kv = jax.random.normal(ks[1], (b, lkv, DIM_KV), dtype=jnp.float32)
        s_q = 1.0 / np.sqrt(DIM_Q)
        s_kv = 1.0 / np.sqrt(DIM_KV)
        Wq = jax.random.normal(ks[2], (DIM_Q, DIM_Q), dtype=jnp.float32) * s_q
        Wk = jax.random.normal(ks[3], (DIM_Q, DIM_KV), dtype=jnp.float32) * s_kv
        Wv = jax.random.normal(ks[4], (DIM_Q, DIM_KV), dtype=jnp.float32) * s_kv
        Wo = jax.random.normal(ks[5], (DIM_Q, DIM_Q), dtype=jnp.float32) * s_q
        bo = jax.random.normal(ks[6], (DIM_Q,), dtype=jnp.float32) * 0.01
        return {'q': q, 'kv': kv, 'Wq': Wq, 'Wk': Wk, 'Wv': Wv, 'Wo': Wo, 'bo': bo}
    _L2_xattn_all = _L2_xattn_setup()
    _L2_xattn_in = {k: v for k, v in _L2_xattn_all.items() if k in ('Wq', 'Wk', 'Wv', 'Wo', 'bo')}
    del _L2_xattn_all

    def _L2_ffn_setup():
        import jax, jax.numpy as jnp
        import numpy as np
        D_MODEL = 256
        N_EXPERTS = 8
        TOP_K = 2
        B, S = (4, 512)
        key = jax.random.key(seed)
        k_x, k_g, k_w = jax.random.split(key, 3)
        x = jax.random.normal(k_x, (B, S, D_MODEL), dtype=jnp.float32)
        gate_w = jax.random.normal(k_g, (N_EXPERTS, D_MODEL), dtype=jnp.float32) * (1.0 / np.sqrt(D_MODEL))
        bound = float(np.sqrt(6.0 / (D_MODEL + D_MODEL)))
        weight = jax.random.uniform(k_w, (N_EXPERTS, D_MODEL, D_MODEL), dtype=jnp.float32, minval=-bound, maxval=bound)
        return {'x': x, 'gate_w': gate_w, 'weight': weight}
    _L2_ffn_all = _L2_ffn_setup()
    _L2_ffn_in = {k: v for k, v in _L2_ffn_all.items() if k in ('gate_w', 'weight')}
    del _L2_ffn_all

    def _L3_xattn_setup():
        import jax, jax.numpy as jnp
        import numpy as np
        EPS = 1e-05

        def layernorm(x, g, b):
            mu = jnp.mean(x, axis=-1, keepdims=True)
            var = jnp.mean(jnp.square(x - mu), axis=-1, keepdims=True)
            return (x - mu) * jax.lax.rsqrt(var + EPS) * g + b
        key = jax.random.key(seed)
        ks = jax.random.split(key, 12)
        B, L1, L2 = (8, 512, 512)
        D1, D2, E = (256, 192, 256)
        s1, s2, se = (D1 ** (-0.5), D2 ** (-0.5), E ** (-0.5))
        return {'modality1': jax.random.normal(ks[0], (B, L1, D1), jnp.float32), 'modality2': jax.random.normal(ks[1], (B, L2, D2), jnp.float32), 'ln1_g': jnp.ones((D1,), jnp.float32), 'ln1_b': jnp.zeros((D1,), jnp.float32), 'ln2_g': jnp.ones((D2,), jnp.float32), 'ln2_b': jnp.zeros((D2,), jnp.float32), 'Wq': jax.random.normal(ks[2], (D1, E), jnp.float32) * s1, 'bq': jax.random.normal(ks[3], (E,), jnp.float32) * 0.01, 'Wk': jax.random.normal(ks[4], (D2, E), jnp.float32) * s2, 'bk': jax.random.normal(ks[5], (E,), jnp.float32) * 0.01, 'Wv': jax.random.normal(ks[6], (D2, E), jnp.float32) * s2, 'bv': jax.random.normal(ks[7], (E,), jnp.float32) * 0.01, 'Wo': jax.random.normal(ks[8], (E, D1), jnp.float32) * se, 'bo': jax.random.normal(ks[9], (D1,), jnp.float32) * 0.01}
    _L3_xattn_all = _L3_xattn_setup()
    _L3_xattn_in = {k: v for k, v in _L3_xattn_all.items() if k in ('ln1_g', 'ln1_b', 'ln2_g', 'ln2_b', 'Wq', 'bq', 'Wk', 'bk', 'Wv', 'bv', 'Wo', 'bo')}
    del _L3_xattn_all

    def _L3_ffn_setup():
        import jax, jax.numpy as jnp
        import numpy as np
        B, T, D = (8, 1024, 256)
        NUM_SLOTS = 64
        TOP_K = 8
        DQ = D // 4
        DH = D // 2

        def _forward(x, slot_init, w1, b1, w2, b2, tau, Wih, Whh, bih, bhh, wq, bq, wk, bk, wv, bv, ln_g, ln_b, wvp, bvp, wo, bo):
            Bx, Tx, Dx = x.shape
            S = jnp.broadcast_to(slot_init[None], (Bx, NUM_SLOTS, Dx)).astype(x.dtype)
            slot_mean = jnp.broadcast_to(S.mean(axis=1, keepdims=True), (Bx, Tx, Dx))
            ctx = jnp.concatenate([x, slot_mean], axis=-1)
            h = jax.nn.gelu(ctx @ w1 + b1, approximate=False)
            route_logits = (h @ w2 + b2) / (jnp.abs(tau) + 0.1)
            topk_vals, topk_idx = jax.lax.top_k(route_logits, TOP_K)
            topk_w = jax.nn.softmax(topk_vals, axis=-1)
            alpha = (jax.nn.one_hot(topk_idx, NUM_SLOTS, dtype=x.dtype) * topk_w[..., None]).sum(axis=-2)
            slot_input = jnp.einsum('bts,btd->bsd', alpha, x)
            denom = alpha.sum(axis=1) + 1e-08
            si = slot_input / denom[..., None]
            gi = si @ Wih.T + bih
            gh = S @ Whh.T + bhh
            i_r, i_z, i_n = jnp.split(gi, 3, axis=-1)
            h_r, h_z, h_n = jnp.split(gh, 3, axis=-1)
            r = jax.nn.sigmoid(i_r + h_r)
            z = jax.nn.sigmoid(i_z + h_z)
            n = jnp.tanh(i_n + r * h_n)
            S_new = (1.0 - z) * n + z * S
            q = S_new @ wq + bq
            k = S_new @ wk + bk
            v = S_new @ wv + bv
            scale = DQ ** (-0.5)
            attn = jax.nn.softmax(jnp.einsum('bsq,btq->bst', q, k) * scale, axis=-1)
            S_comm = jnp.einsum('bst,btd->bsd', attn, v)
            y = S_new + S_comm
            mu = y.mean(axis=-1, keepdims=True)
            var = y.var(axis=-1, keepdims=True)
            y = (y - mu) * jax.lax.rsqrt(var + 1e-05) * ln_g + ln_b
            slot_values = y @ wvp + bvp
            out = jnp.einsum('bts,bsd->btd', alpha, slot_values)
            return out @ wo + bo
        key = jax.random.key(seed)
        ks = jax.random.split(key, 24)
        n = lambda k, shp, s=0.02: jax.random.normal(k, shp, dtype=jnp.float32) * s
        return {'x': jax.random.normal(ks[0], (B, T, D), dtype=jnp.float32), 'slot_init': n(ks[1], (NUM_SLOTS, D)), 'w1': n(ks[2], (2 * D, DH)), 'b1': jnp.zeros((DH,)), 'w2': n(ks[3], (DH, NUM_SLOTS)), 'b2': jnp.zeros((NUM_SLOTS,)), 'tau': jnp.ones((1,)), 'Wih': n(ks[4], (3 * D, D)), 'Whh': n(ks[5], (3 * D, D)), 'bih': jnp.zeros((3 * D,)), 'bhh': jnp.zeros((3 * D,)), 'wq': n(ks[6], (D, DQ)), 'bq': jnp.zeros((DQ,)), 'wk': n(ks[7], (D, DQ)), 'bk': jnp.zeros((DQ,)), 'wv': n(ks[8], (D, D)), 'bv': jnp.zeros((D,)), 'ln_g': jnp.ones((D,)), 'ln_b': jnp.zeros((D,)), 'wvp': n(ks[9], (D, D)), 'bvp': jnp.zeros((D,)), 'wo': n(ks[10], (D, D)), 'bo': jnp.zeros((D,))}
    _L3_ffn_all = _L3_ffn_setup()
    _L3_ffn_in = {k: v for k, v in _L3_ffn_all.items() if k in ('slot_init', 'w1', 'b1', 'w2', 'b2', 'tau', 'Wih', 'Whh', 'bih', 'bhh', 'wq', 'bq', 'wk', 'bk', 'wv', 'bv', 'ln_g', 'ln_b', 'wvp', 'bvp', 'wo', 'bo')}
    del _L3_ffn_all
    return {'x': x, 'ctx_768': ctx_768, 'mask_BxS2_bk0': mask_BxS2_bk0, 'g_xattn': g_xattn, 'g_ffn': g_ffn, 'L0_xattn_ln_x_g': _L0_xattn_in['ln_x_g'], 'L0_xattn_ln_x_b': _L0_xattn_in['ln_x_b'], 'L0_xattn_ln_l_g': _L0_xattn_in['ln_l_g'], 'L0_xattn_ln_l_b': _L0_xattn_in['ln_l_b'], 'L0_xattn_qn_g': _L0_xattn_in['qn_g'], 'L0_xattn_kn_g': _L0_xattn_in['kn_g'], 'L0_xattn_Wq': _L0_xattn_in['Wq'], 'L0_xattn_Wkv': _L0_xattn_in['Wkv'], 'L0_xattn_Wlkv': _L0_xattn_in['Wlkv'], 'L0_xattn_Wo': _L0_xattn_in['Wo'], 'L0_xattn_bo': _L0_xattn_in['bo'], 'L0_ffn_router_w': _L0_ffn_in['router_w'], 'L0_ffn_router_b': _L0_ffn_in['router_b'], 'L0_ffn_w1': _L0_ffn_in['w1'], 'L0_ffn_b1': _L0_ffn_in['b1'], 'L0_ffn_w2': _L0_ffn_in['w2'], 'L0_ffn_b2': _L0_ffn_in['b2'], 'L1_xattn_Wq': _L1_xattn_in['Wq'], 'L1_xattn_Wk': _L1_xattn_in['Wk'], 'L1_xattn_Wv': _L1_xattn_in['Wv'], 'L1_xattn_Wo': _L1_xattn_in['Wo'], 'L1_xattn_bo': _L1_xattn_in['bo'], 'L1_ffn_Ws1': _L1_ffn_in['Ws1'], 'L1_ffn_Ws2': _L1_ffn_in['Ws2'], 'L1_ffn_W1': _L1_ffn_in['W1'], 'L1_ffn_W2': _L1_ffn_in['W2'], 'L1_ffn_Wr': _L1_ffn_in['Wr'], 'L2_xattn_Wq': _L2_xattn_in['Wq'], 'L2_xattn_Wk': _L2_xattn_in['Wk'], 'L2_xattn_Wv': _L2_xattn_in['Wv'], 'L2_xattn_Wo': _L2_xattn_in['Wo'], 'L2_xattn_bo': _L2_xattn_in['bo'], 'L2_ffn_gate_w': _L2_ffn_in['gate_w'], 'L2_ffn_weight': _L2_ffn_in['weight'], 'L3_xattn_ln1_g': _L3_xattn_in['ln1_g'], 'L3_xattn_ln1_b': _L3_xattn_in['ln1_b'], 'L3_xattn_ln2_g': _L3_xattn_in['ln2_g'], 'L3_xattn_ln2_b': _L3_xattn_in['ln2_b'], 'L3_xattn_Wq': _L3_xattn_in['Wq'], 'L3_xattn_bq': _L3_xattn_in['bq'], 'L3_xattn_Wk': _L3_xattn_in['Wk'], 'L3_xattn_bk': _L3_xattn_in['bk'], 'L3_xattn_Wv': _L3_xattn_in['Wv'], 'L3_xattn_bv': _L3_xattn_in['bv'], 'L3_xattn_Wo': _L3_xattn_in['Wo'], 'L3_xattn_bo': _L3_xattn_in['bo'], 'L3_ffn_slot_init': _L3_ffn_in['slot_init'], 'L3_ffn_w1': _L3_ffn_in['w1'], 'L3_ffn_b1': _L3_ffn_in['b1'], 'L3_ffn_w2': _L3_ffn_in['w2'], 'L3_ffn_b2': _L3_ffn_in['b2'], 'L3_ffn_tau': _L3_ffn_in['tau'], 'L3_ffn_Wih': _L3_ffn_in['Wih'], 'L3_ffn_Whh': _L3_ffn_in['Whh'], 'L3_ffn_bih': _L3_ffn_in['bih'], 'L3_ffn_bhh': _L3_ffn_in['bhh'], 'L3_ffn_wq': _L3_ffn_in['wq'], 'L3_ffn_bq': _L3_ffn_in['bq'], 'L3_ffn_wk': _L3_ffn_in['wk'], 'L3_ffn_bk': _L3_ffn_in['bk'], 'L3_ffn_wv': _L3_ffn_in['wv'], 'L3_ffn_bv': _L3_ffn_in['bv'], 'L3_ffn_ln_g': _L3_ffn_in['ln_g'], 'L3_ffn_ln_b': _L3_ffn_in['ln_b'], 'L3_ffn_wvp': _L3_ffn_in['wvp'], 'L3_ffn_bvp': _L3_ffn_in['bvp'], 'L3_ffn_wo': _L3_ffn_in['wo'], 'L3_ffn_bo': _L3_ffn_in['bo']}

def reference(x, ctx_768, mask_BxS2_bk0, g_xattn, g_ffn, L0_xattn_ln_x_g, L0_xattn_ln_x_b, L0_xattn_ln_l_g, L0_xattn_ln_l_b, L0_xattn_qn_g, L0_xattn_kn_g, L0_xattn_Wq, L0_xattn_Wkv, L0_xattn_Wlkv, L0_xattn_Wo, L0_xattn_bo, L0_ffn_router_w, L0_ffn_router_b, L0_ffn_w1, L0_ffn_b1, L0_ffn_w2, L0_ffn_b2, L1_xattn_Wq, L1_xattn_Wk, L1_xattn_Wv, L1_xattn_Wo, L1_xattn_bo, L1_ffn_Ws1, L1_ffn_Ws2, L1_ffn_W1, L1_ffn_W2, L1_ffn_Wr, L2_xattn_Wq, L2_xattn_Wk, L2_xattn_Wv, L2_xattn_Wo, L2_xattn_bo, L2_ffn_gate_w, L2_ffn_weight, L3_xattn_ln1_g, L3_xattn_ln1_b, L3_xattn_ln2_g, L3_xattn_ln2_b, L3_xattn_Wq, L3_xattn_bq, L3_xattn_Wk, L3_xattn_bk, L3_xattn_Wv, L3_xattn_bv, L3_xattn_Wo, L3_xattn_bo, L3_ffn_slot_init, L3_ffn_w1, L3_ffn_b1, L3_ffn_w2, L3_ffn_b2, L3_ffn_tau, L3_ffn_Wih, L3_ffn_Whh, L3_ffn_bih, L3_ffn_bhh, L3_ffn_wq, L3_ffn_bq, L3_ffn_wk, L3_ffn_bk, L3_ffn_wv, L3_ffn_bv, L3_ffn_ln_g, L3_ffn_ln_b, L3_ffn_wvp, L3_ffn_bvp, L3_ffn_wo, L3_ffn_bo):
    import jax
    import jax.numpy as jnp

    def _L0_xattn_ref(x, latents, mask, ln_x_g, ln_x_b, ln_l_g, ln_l_b, qn_g, kn_g, Wq, Wkv, Wlkv, Wo, bo):
        import jax, jax.numpy as jnp
        import numpy as np
        DIM_IN, DIM_LAT, DIM_HEAD = (192, 256, 64)
        INNER = max(DIM_LAT, DIM_IN)
        HEADS = INNER // DIM_HEAD
        SCALE = DIM_HEAD ** (-0.5)
        RMS_EPS = 1e-08
        LN_EPS = 1e-05

        def layernorm(x, g, b):
            mu = jnp.mean(x, axis=-1, keepdims=True)
            var = jnp.mean((x - mu) ** 2, axis=-1, keepdims=True)
            return (x - mu) * jax.lax.rsqrt(var + LN_EPS) * g + b

        def rmsnorm(x, gamma):
            norm = jnp.sqrt(jnp.sum(x * x, axis=-1, keepdims=True)) * x.shape[-1] ** (-0.5)
            return x / jnp.maximum(norm, RMS_EPS) * gamma
        b, n, _ = x.shape
        m = latents.shape[1]
        xn = layernorm(x, ln_x_g, ln_x_b)
        ln = layernorm(latents, ln_l_g, ln_l_b)
        q = ln @ Wq.T
        kv = jnp.concatenate([xn @ Wkv.T, ln @ Wlkv.T], axis=1)
        k, v = (kv[..., :INNER], kv[..., INNER:])
        split_heads = lambda t: t.reshape(t.shape[0], t.shape[1], HEADS, DIM_HEAD).transpose(0, 2, 1, 3)
        q, k, v = (split_heads(q), split_heads(k), split_heads(v))
        qn = rmsnorm(q, qn_g) * SCALE
        kn = rmsnorm(k, kn_g)
        attn = jnp.einsum('bhid,bhjd->bhij', qn, kn)
        full_mask = jnp.pad(mask, ((0, 0), (0, m)), constant_values=True)
        attn = jnp.where(full_mask[:, None, None, :], attn, -jnp.finfo(attn.dtype).max)
        attn = jax.nn.softmax(attn, axis=-1)
        out = jnp.einsum('bhij,bhjd->bhid', attn, v)
        out = out.transpose(0, 2, 1, 3).reshape(b, m, INNER)
        return out @ Wo.T + bo

    def _L0_ffn_ref(x, router_w, router_b, w1, b1, w2, b2):
        import jax, jax.numpy as jnp
        import numpy as np
        DIM = 256
        HIDDEN = 1024
        E = 8
        B, S = (2, 1024)
        logits = jnp.einsum('bsd,de->bse', x, router_w) + router_b
        probs = jax.nn.softmax(logits, axis=-1)
        top1 = jnp.argmax(probs, axis=-1)
        out = jnp.zeros_like(x)
        for i in range(E):
            h = jnp.einsum('bsd,df->bsf', x, w1[i]) + b1[i]
            a, g = jnp.split(h, 2, axis=-1)
            y = jnp.einsum('bsh,hd->bsd', a * jax.nn.sigmoid(g), w2[i]) + b2[i]
            out = out + jnp.where((top1 == i)[..., None], y, 0.0)
        return out

    def _L1_xattn_ref(x, context, Wq, Wk, Wv, Wo, bo):
        import jax, jax.numpy as jnp
        import numpy as np
        QUERY_DIM = 256
        CONTEXT_DIM = 192
        HEADS = 8
        DIM_HEAD = 64
        INNER = HEADS * DIM_HEAD
        B, S, _ = x.shape
        L = context.shape[1]
        scale = DIM_HEAD ** (-0.5)
        q = (x @ Wq).reshape(B, S, HEADS, DIM_HEAD).transpose(0, 2, 1, 3)
        k = (context @ Wk).reshape(B, L, HEADS, DIM_HEAD).transpose(0, 2, 1, 3)
        v = (context @ Wv).reshape(B, L, HEADS, DIM_HEAD).transpose(0, 2, 1, 3)
        attn = jnp.einsum('bhsd,bhld->bhsl', q, k) * scale
        attn = jax.nn.softmax(attn, axis=-1)
        out = jnp.einsum('bhsl,bhld->bhsd', attn, v)
        out = out.transpose(0, 2, 1, 3).reshape(B, S, INNER)
        return out @ Wo + bo

    def _L1_ffn_ref(x, Ws1, Ws2, W1, W2, Wr):
        import jax, jax.numpy as jnp
        import numpy as np
        D_MODEL = 256
        EXPERT_DIM = 128
        N_EXPERTS = 8
        TOP_K = 2

        def _sq_relu(h):
            return jnp.square(jax.nn.relu(h))
        shape = x.shape
        xf = x.reshape(-1, D_MODEL)
        out_shared = _sq_relu(xf @ Ws1) @ Ws2
        logits = xf @ Wr
        top_vals, top_idx = jax.lax.top_k(logits, TOP_K)
        rw = jax.nn.softmax(top_vals.astype(jnp.float32), axis=-1).astype(x.dtype)
        onehot = jax.nn.one_hot(top_idx, N_EXPERTS, dtype=x.dtype)
        prob = jnp.einsum('tk,tke->te', rw, onehot)
        prob = jnp.trunc(prob)
        h = _sq_relu(jnp.einsum('td,edf->tef', xf, W1))
        y = jnp.einsum('tef,efd->ted', h, W2)
        out_routed = jnp.einsum('ted,te->td', y, prob)
        return (out_shared + out_routed).reshape(shape)

    def _L2_xattn_ref(q, kv, Wq, Wk, Wv, Wo, bo):
        import jax, jax.numpy as jnp
        import numpy as np
        DIM_Q = 256
        DIM_KV = 192
        N_HEADS = 4

        def _split_heads(x):
            b, l, d = x.shape
            return x.reshape(b, l, N_HEADS, d // N_HEADS).transpose(0, 2, 1, 3)
        qp = q @ Wq.T
        kp = kv @ Wk.T
        vp = kv @ Wv.T
        qh, kh, vh = (_split_heads(qp), _split_heads(kp), _split_heads(vp))
        scale = (DIM_Q // N_HEADS) ** (-0.5)
        scores = jnp.einsum('bhqd,bhkd->bhqk', qh, kh) * scale
        attn = jax.nn.softmax(scores, axis=-1)
        ctx = jnp.einsum('bhqk,bhkd->bhqd', attn, vh)
        b, h, lq, hd = ctx.shape
        ctx = ctx.transpose(0, 2, 1, 3).reshape(b, lq, h * hd)
        return ctx @ Wo.T + bo

    def _L2_ffn_ref(x, gate_w, weight):
        import jax, jax.numpy as jnp
        import numpy as np
        D_MODEL = 256
        N_EXPERTS = 8
        TOP_K = 2
        B, S = (4, 512)
        logits = jnp.einsum('bsd,ed->bse', x, gate_w)
        topk_vals, topk_idx = jax.lax.top_k(logits, TOP_K)
        topk_weights = jax.nn.softmax(topk_vals, axis=-1)
        one_hot = jax.nn.one_hot(topk_idx, N_EXPERTS, dtype=x.dtype)
        weights_full = jnp.einsum('bsk,bske->bse', topk_weights, one_hot)
        expert_out = jnp.einsum('bsd,edh->bseh', x, weight)
        out = jnp.einsum('bse,bseh->bsh', weights_full, expert_out)
        return out

    def _L3_xattn_ref(modality1, modality2, ln1_g, ln1_b, ln2_g, ln2_b, Wq, bq, Wk, bk, Wv, bv, Wo, bo):
        import jax, jax.numpy as jnp
        import numpy as np
        EPS = 1e-05

        def layernorm(x, g, b):
            mu = jnp.mean(x, axis=-1, keepdims=True)
            var = jnp.mean(jnp.square(x - mu), axis=-1, keepdims=True)
            return (x - mu) * jax.lax.rsqrt(var + EPS) * g + b
        E = Wq.shape[1]
        scaling = E ** (-0.5)
        x1 = layernorm(modality1, ln1_g, ln1_b)
        x2 = layernorm(modality2, ln2_g, ln2_b)
        q = x1 @ Wq + bq
        k = x2 @ Wk + bk
        v = x2 @ Wv + bv
        scores = jnp.einsum('bqe,bke->bqk', q, k) * scaling
        attn = jax.nn.softmax(scores, axis=-1)
        ctx = jnp.einsum('bqk,bke->bqe', attn, v)
        return ctx @ Wo + bo

    def _L3_ffn_ref(x, slot_init, w1, b1, w2, b2, tau, Wih, Whh, bih, bhh, wq, bq, wk, bk, wv, bv, ln_g, ln_b, wvp, bvp, wo, bo):
        import jax, jax.numpy as jnp
        import numpy as np
        B, T, D = (8, 1024, 256)
        NUM_SLOTS = 64
        TOP_K = 8
        DQ = D // 4
        DH = D // 2

        def _forward(x, slot_init, w1, b1, w2, b2, tau, Wih, Whh, bih, bhh, wq, bq, wk, bk, wv, bv, ln_g, ln_b, wvp, bvp, wo, bo):
            Bx, Tx, Dx = x.shape
            S = jnp.broadcast_to(slot_init[None], (Bx, NUM_SLOTS, Dx)).astype(x.dtype)
            slot_mean = jnp.broadcast_to(S.mean(axis=1, keepdims=True), (Bx, Tx, Dx))
            ctx = jnp.concatenate([x, slot_mean], axis=-1)
            h = jax.nn.gelu(ctx @ w1 + b1, approximate=False)
            route_logits = (h @ w2 + b2) / (jnp.abs(tau) + 0.1)
            topk_vals, topk_idx = jax.lax.top_k(route_logits, TOP_K)
            topk_w = jax.nn.softmax(topk_vals, axis=-1)
            alpha = (jax.nn.one_hot(topk_idx, NUM_SLOTS, dtype=x.dtype) * topk_w[..., None]).sum(axis=-2)
            slot_input = jnp.einsum('bts,btd->bsd', alpha, x)
            denom = alpha.sum(axis=1) + 1e-08
            si = slot_input / denom[..., None]
            gi = si @ Wih.T + bih
            gh = S @ Whh.T + bhh
            i_r, i_z, i_n = jnp.split(gi, 3, axis=-1)
            h_r, h_z, h_n = jnp.split(gh, 3, axis=-1)
            r = jax.nn.sigmoid(i_r + h_r)
            z = jax.nn.sigmoid(i_z + h_z)
            n = jnp.tanh(i_n + r * h_n)
            S_new = (1.0 - z) * n + z * S
            q = S_new @ wq + bq
            k = S_new @ wk + bk
            v = S_new @ wv + bv
            scale = DQ ** (-0.5)
            attn = jax.nn.softmax(jnp.einsum('bsq,btq->bst', q, k) * scale, axis=-1)
            S_comm = jnp.einsum('bst,btd->bsd', attn, v)
            y = S_new + S_comm
            mu = y.mean(axis=-1, keepdims=True)
            var = y.var(axis=-1, keepdims=True)
            y = (y - mu) * jax.lax.rsqrt(var + 1e-05) * ln_g + ln_b
            slot_values = y @ wvp + bvp
            out = jnp.einsum('bts,bsd->btd', alpha, slot_values)
            return out @ wo + bo
        return _forward(x, slot_init, w1, b1, w2, b2, tau, Wih, Whh, bih, bhh, wq, bq, wk, bk, wv, bv, ln_g, ln_b, wvp, bvp, wo, bo)
    x = x + jnp.tanh(g_xattn[0]) * _L0_xattn_ref(ctx_768, _layernorm(x, axis=-1), mask_BxS2_bk0, L0_xattn_ln_x_g, L0_xattn_ln_x_b, L0_xattn_ln_l_g, L0_xattn_ln_l_b, L0_xattn_qn_g, L0_xattn_kn_g, L0_xattn_Wq, L0_xattn_Wkv, L0_xattn_Wlkv, L0_xattn_Wo, L0_xattn_bo)
    x = x + jnp.tanh(g_ffn[0]) * _L0_ffn_ref(_layernorm(x, axis=-1), L0_ffn_router_w, L0_ffn_router_b, L0_ffn_w1, L0_ffn_b1, L0_ffn_w2, L0_ffn_b2)
    x = x + jnp.tanh(g_xattn[1]) * _L1_xattn_ref(_layernorm(x, axis=-1), ctx_768, L1_xattn_Wq, L1_xattn_Wk, L1_xattn_Wv, L1_xattn_Wo, L1_xattn_bo)
    x = x + jnp.tanh(g_ffn[1]) * _L1_ffn_ref(_layernorm(x, axis=-1), L1_ffn_Ws1, L1_ffn_Ws2, L1_ffn_W1, L1_ffn_W2, L1_ffn_Wr)
    x = x + jnp.tanh(g_xattn[2]) * _L2_xattn_ref(_layernorm(x, axis=-1), ctx_768, L2_xattn_Wq, L2_xattn_Wk, L2_xattn_Wv, L2_xattn_Wo, L2_xattn_bo)
    x = x + jnp.tanh(g_ffn[2]) * _L2_ffn_ref(_layernorm(x, axis=-1), L2_ffn_gate_w, L2_ffn_weight)
    x = x + jnp.tanh(g_xattn[3]) * _L3_xattn_ref(_layernorm(x, axis=-1), ctx_768, L3_xattn_ln1_g, L3_xattn_ln1_b, L3_xattn_ln2_g, L3_xattn_ln2_b, L3_xattn_Wq, L3_xattn_bq, L3_xattn_Wk, L3_xattn_bk, L3_xattn_Wv, L3_xattn_bv, L3_xattn_Wo, L3_xattn_bo)
    x = x + jnp.tanh(g_ffn[3]) * _L3_ffn_ref(_layernorm(x, axis=-1), L3_ffn_slot_init, L3_ffn_w1, L3_ffn_b1, L3_ffn_w2, L3_ffn_b2, L3_ffn_tau, L3_ffn_Wih, L3_ffn_Whh, L3_ffn_bih, L3_ffn_bhh, L3_ffn_wq, L3_ffn_bq, L3_ffn_wk, L3_ffn_bk, L3_ffn_wv, L3_ffn_bv, L3_ffn_ln_g, L3_ffn_ln_b, L3_ffn_wvp, L3_ffn_bvp, L3_ffn_wo, L3_ffn_bo)
    return x

_drawn_inputs = setup_inputs


def setup_inputs(seed=0):
    import zlib

    import numpy as np

    out = dict(_drawn_inputs(seed))
    spreads = {'L0_xattn_ln_x_g': (1.0, 0.2),
     'L0_xattn_ln_x_b': (0.0, 0.1),
     'L0_xattn_ln_l_g': (1.0, 0.2),
     'L0_xattn_ln_l_b': (0.0, 0.1),
     'L0_xattn_qn_g': (1.0, 0.2),
     'L0_xattn_kn_g': (1.0, 0.2),
     'L0_xattn_bo': (0.0, 0.1),
     'L3_xattn_ln1_g': (1.0, 0.6),
     'L3_xattn_ln1_b': (0.0, 0.721),
     'L3_xattn_ln2_g': (1.0, 0.2),
     'L3_xattn_ln2_b': (0.0, 0.1),
     'L3_ffn_b1': (0.0, 2.0),
     'L3_ffn_b2': (0.0, 2.0),
     'L3_ffn_bih': (0.0, 0.394),
     'L3_ffn_bhh': (0.0, 0.704),
     'L3_ffn_bq': (0.0, 2.0),
     'L3_ffn_bk': (0.0, 2.0),
     'L3_ffn_bv': (0.0, 0.345),
     'L3_ffn_ln_g': (1.0, 0.6),
     'L3_ffn_ln_b': (0.0, 0.8),
     'L3_ffn_bvp': (0.0, 0.448),
     'L3_ffn_bo': (0.0, 0.1)}
    factors = {'g_ffn': 8.0,
     'L3_xattn_bq': 64.0,
     'L3_xattn_bk': 64.0,
     'L3_xattn_bv': 8.0,
     'L3_xattn_bo': 8.0,
     'L3_ffn_slot_init': 22.178,
     'L3_ffn_w1': 33.614,
     'L3_ffn_w2': 29.054,
     'L3_ffn_Whh': 30.786,
     'L3_ffn_wq': 64.0,
     'L3_ffn_wk': 64.0,
     'L3_ffn_wv': 6.414}
    for name, (base, spread) in spreads.items():
        noise = np.random.default_rng([zlib.crc32(name.encode()), seed]).standard_normal(out[name].shape)
        drawn = base * np.exp(spread * noise) if base else spread * noise
        out[name] = jnp.asarray(drawn.astype(out[name].dtype))
    for name, factor in factors.items():
        out[name] = (out[name] * factor).astype(out[name].dtype)
    return out
```

```python
from contextlib import ExitStack

import concourse.bass as bass
from concourse import mybir

ALU = mybir.AluOpType
ACT = mybir.ActivationFunctionType
F32 = mybir.dt.float32
U8 = mybir.dt.uint8
U32 = mybir.dt.uint32
AXX = mybir.AxisListType.X

B, T, D = 16, 100, 256
NC, DC = 361, 192
P = 128
NCH = 3
LAST = NC - (NCH - 1) * P
NKP = NCH * P
CW = (P, DC - P)
LN_EPS = 1e-5
FAR = -1.0e30

HEADS = (4, 8, 4, 1)
HWID = (64, 64, 64, 256)
KEYS = (NKP + P, NC, NC, NC)
CHUNKS = (NCH + 1, NCH, NCH, NCH)
GROUPS = (
    ((0, 1, 2), (3, 4, 5), (6, 7), (8, 9, 10)),
    ((0,), (1, 2), (3,), (4,), (5,), (6,), (7,), (8,)),
    ((0, 1), (2, 3), (4, 5), (6,)),
    ((0, 1, 2, 3, 4, 5, 6, 7, 8),),
)
STEPS = tuple(sum(len(g) for g in gs) for gs in GROUPS)
NORMS = (2, 1, 1, 2)
MAXES = (2, 1, 1, 1)
E0, HID0 = 8, 1024
E1, HID1 = 8, 128
E2 = 8
NS, TOPS, DQ = 64, 8, 64
BUILT = (0, 1, 2, 3, 4, 5, 6, 7)
WORK = 24600


class Named:

    def __init__(self, **by_name):
        self.by_name = by_name

    def __getattr__(self, name):
        return self.by_name[name]


def signals(nc, ctx, phase, names):
    return Named(**{n: ctx.enter_context(nc.semaphore(f"{phase}_{n}")) for n in names.split()})


class Signal:

    def __init__(self, sem, before):
        self.sem, self.before = sem, before


def raised_by_attention(L):
    H, own_ctx = HEADS[L], L in (0, 3)
    per_batch = {"ln_ctx": 10 * own_ctx, "rstd_ctx": own_ctx, "ln_x": 4 * NORMS[L], "rstd_x": NORMS[L],
                 "proj": STEPS[L], "copied": STEPS[L], "mask_row": L == 0, "qk_rms": 4 * (L == 0), "rqk": L == 0,
                 "scores": H, "maxed": MAXES[L] * H, "exped": H, "probs_turned": H, "probs_copied": H, "pv": H,
                 "o_scaled": 2, "o_turned": 1, "o_copied": 1, "out": 1, "resid": 2}
    counts = {n: B * int(c) for n, c in per_batch.items()}
    counts.update(ctx_in0=16 * B, ctx_in1=16 * B, mask_in0=8 * B * (L == 0), mask_in1=8 * B * (L == 0), cleared=1)
    return counts


def wait_for(eng, signal, count):
    if isinstance(count, int) and count <= 0:
        return
    eng.wait_ge(signal.sem, signal.before + count)


def apart(eng):
    eng.nop(nofuse=True)


def wait_count(eng, sem, count):
    if isinstance(count, int) and count <= 0:
        return
    eng.wait_ge(sem, count)


def pipelined(eng, prepare, attend, finish):
    prepare(0, 0)
    attend(0, 0, True)
    attend(1, 1, True)
    with eng.Fori(1, B // 2 - 1) as i:
        attend(2 * i, 0, True)
        attend(2 * i + 1, 1, True)
    attend(B - 2, 0, True)
    attend(B - 1, 1, False)
    finish(B - 1, 1)


def in_turn(eng, one):
    one(0, 0)
    one(1, 1)
    with eng.Fori(1, B // 2) as i:
        one(2 * i, 0)
        one(2 * i + 1, 1)


def flamingo_kernel(nc, a, out, last_phase=99):
    ctx = ExitStack()
    with ctx:
        def sb(name, shape, dt=F32):
            return ctx.enter_context(nc.sbuf_tensor(name, shape, dt))

        def ps(name, shape):
            return ctx.enter_context(nc.psum_tensor(name, shape, F32))

        X = sb("X", [P, B, D])
        ident = sb("ident", [P, P])
        gates = sb("gates", [P, 8])
        neg_half = sb("neg_half", [P, 32])
        work = sb("work", [P, WORK])
        bank = [ps(f"bank{i}", [P, 512]) for i in range(8)]

        class Area:

            def __init__(self):
                self.at = 0

            def take(self, *shape, dt=F32):
                n = 1
                for s in shape:
                    n *= s
                words = n if dt in (F32, U32) else (n + 3) // 4
                v = work[:, self.at:self.at + words]
                self.at += words
                assert self.at <= WORK, self.at
                if dt != F32:
                    v = v.bitcast(dt)[:, 0:n]
                names = " ".join("abcd"[:len(shape)])
                sizes = {"abcd"[i]: s for i, s in enumerate(shape)}
                return v.rearrange(f"p ({names}) -> p {names}", **sizes)

        loads = []

        def resident(phase, name, chunks, parts=P):
            src = a[name]
            n = src.shape[-1]
            w = sb(name, [P, chunks, n])
            full = src.shape[0] // P
            if full:
                loads.append((phase, w[:, 0:full, :], src[0:full * P, :].rearrange("(c p) n -> p c n", p=P)))
            if src.shape[0] % P:
                loads.append((phase, w[0:src.shape[0] % P, full, :], src[full * P:, :]))
            return w

        def column(phase, name, chunks=1):
            w = sb(name, [P, chunks])
            loads.append((phase, w[:, :], a[name]))
            return w

        def row(phase, name):
            n = a[name].shape[0]
            w = sb(name, [P, n])
            loads.append((phase, w[:, :], a[name].rearrange("(o n) -> o n", o=1).broadcast_to([P, n])))
            return w

        wq = [resident(2 * L, n, 2) for L, n in enumerate(("L0_WqT", "L1_Wq", "L2_WqT", "L3_Wq"))]
        wk = [None] + [resident(2 * L, n, 2) for L, n in ((1, "L1_Wk"), (2, "L2_WkT"), (3, "L3_Wk"))]
        wv = [None] + [resident(2 * L, n, 2) for L, n in ((1, "L1_Wv"), (2, "L2_WvT"), (3, "L3_Wv"))]
        wkv0 = resident(0, "L0_WkvT", 2)
        wlkv0 = resident(0, "L0_WlkvT", 2)
        wo = [resident(2 * L, n, 4 if L == 1 else 2) for L, n in enumerate(("L0_WoT", "L1_Wo", "L2_WoT", "L3_Wo"))]
        bo = [row(2 * L, f"L{L}_bo") for L in range(4)]
        ctx_gain = {0: column(0, "L0_ln_x_g", 2), 3: column(6, "L3_ln2_g", 2)}
        ctx_bias = {0: column(0, "L0_ln_x_b", 2), 3: column(6, "L3_ln2_b", 2)}
        x_gain = {0: column(0, "L0_ln_l_g", 2), 3: column(6, "L3_ln1_g", 2)}
        x_bias = {0: column(0, "L0_ln_l_b", 2), 3: column(6, "L3_ln1_b", 2)}
        q_gain = column(0, "L0_qn_g2")
        k_gain = column(0, "L0_kn_g2")
        bq3, bk3, bv3 = column(6, "L3_bq", 2), column(6, "L3_bk", 2), row(6, "L3_bv")
        bq3s = sb("bq3_scaled", [P, 2])
        qg0s = sb("q_gain_scaled", [P, 1])

        iota = row(1, "iota")
        ew0 = resident(1, "F0_router_w", 2)
        eb0 = row(1, "F0_router_b")
        eb2 = sb("F0_b2", [E0, D])
        loads.append((1, eb2[:, :], a["F0_b2"]))
        eb1 = sb("F0_b1", [P, E0, 2 * HID0 // P])
        loads.append((1, eb1[:, :, :], a["F0_b1c"]))
        ew1 = resident(3, "F1_Wr", 2)
        up1 = resident(3, "F1_up", 2)
        down1 = resident(3, "F1_down", 1 + E1)
        ew2 = resident(5, "F2_gateT", 2)
        lin2 = sb("F2_weight", [P, 2, E2, D])
        for c in range(2):
            loads.append((5, lin2[:, c, :, :], a["F2_weight"][:, c * P:(c + 1) * P, :].rearrange("e p n -> p e n")))

        start = signals(nc, ctx, "start", "x_loaded consts weights gates memsets gates_done neg_half scaled")
        loaded = [ctx.enter_context(nc.semaphore(f"weights_loaded_{p}")) for p in range(8)]
        n_loads = [0] * 8
        for p, _, _ in loads:
            n_loads[p] += 1
        ended = ctx.enter_context(nc.semaphore("phase_ended"))
        stored = ctx.enter_context(nc.semaphore("stored"))
        shared = signals(nc, ctx, "attn", " ".join(raised_by_attention(0)))
        at = []
        for L in range(4):
            before = {n: sum(raised_by_attention(k)[n] for k in range(L) if 2 * k in BUILT) for n in raised_by_attention(0)}
            at.append(Named(**{n: Signal(sem, before[n]) for n, sem in shared.by_name.items()}))
        mx0 = signals(nc, ctx, "dense", "ln_x rstd_x x_turned x_copied logits route oh_turned oh_copied b2_row b2_added "
                      "w_in0 w_in1 value gate sigmoid hidden out resid")
        mx1 = signals(nc, ctx, "squared", "ln_x rstd_x x_turned x_copied logits route exped ones hidden relu squared masked "
                      "h_turned h_copied out resid")
        mx2 = signals(nc, ctx, "linear", "ln_x rstd_x x_turned x_copied logits route exped out combined resid")
        mx3 = signals(nc, ctx, "slots", "w_in consts const_sums ln_x rstd_x x_turned x_copied hidden gelu logits picked "
                      "exped alpha sums alpha_turned alpha_copied pooled pooled_turned pooled_copied gru_in rz_in rz_tanh "
                      "rz_done n_tanh slots_new s_turned s_copied qkv qk_copied v_done attn masked attn_exped attn_turned "
                      "attn_copied comm y_stats rstd_y y_normed y_turned y_copied values values_done mixed mixed_copied "
                      "out resid")

        area = Area()
        C = [area.take(NCH, DC) for _ in range(2)]
        CNorm = [area.take(NCH, DC) for _ in range(2)]
        CT = [area.take(2, NKP) for _ in range(2)]
        XN = [area.take(D) for _ in range(2)]
        XN2 = [area.take(D) for _ in range(2)]
        XT = [area.take(2, P) for _ in range(2)]
        QK = [area.take(5, D) for _ in range(2)]
        QKsq = area.take(5, D)
        QT = [area.take(4, T) for _ in range(2)]
        KT = [area.take(2048) for _ in range(2)]
        V = [area.take(2048) for _ in range(2)]
        PR = [area.take(4, P) for _ in range(2)]
        PT = [area.take(4, T) for _ in range(2)]
        O = area.take(512)
        OT = area.take(4, T)
        RO = area.take(D)
        M8 = [area.take(NC, dt=U8) for _ in range(2)]
        MR = [area.take(4, P) for _ in range(2)]
        st6 = [area.take(4, 6) for _ in range(2)]
        mv = [area.take(4, 2) for _ in range(2)]
        rs = [area.take(4) for _ in range(2)]
        ss = [area.take(20) for _ in range(2)]
        rr = [area.take(20) for _ in range(2)]
        nmax = [area.take(1) for _ in range(2)]
        pmax = [area.take(1) for _ in range(2)]
        rsum = [area.take(8) for _ in range(2)]
        rinv = area.take(8)
        S_bank = (bank[0], bank[1])
        PT_bank = (bank[2], bank[3])
        O_bank = bank[4]
        R_bank = bank[5]
        J_bank = (bank[6], bank[7])

        area = Area()
        FX = [area.take(D) for _ in range(2)]
        FXT = [area.take(2, T) for _ in range(2)]
        Fst6, Fmv, Frs = [[area.take(n) for _ in range(2)] for n in (6, 2, 1)]
        LG = [area.take(8) for _ in range(2)]
        V8 = [area.take(8) for _ in range(2)]
        I8 = [area.take(8, dt=U32) for _ in range(2)]
        IF = [area.take(2) for _ in range(2)]
        ED = [area.take(6) for _ in range(2)]
        WF = [area.take(9) for _ in range(2)]
        WB = [area.take(8) for _ in range(2)]
        mixture = area.at
        XA = area.take(2, B * T)
        OHG = area.take(B, E0)
        OHT = [area.take(T) for _ in range(2)]
        W1 = [area.take(2, 2 * HID0) for _ in range(2)]
        W2 = [area.take(HID0 // P, D) for _ in range(2)]
        QT_TOK = 4 * T
        SG = [area.take(QT_TOK) for _ in range(2)]
        AC = area.take(HID0 // P, QT_TOK)
        area.at = mixture
        RL = [area.take(3 * HID1) for _ in range(3)]
        SQ = [area.take(3 * HID1) for _ in range(3)]
        HT = [area.take(3, T) for _ in range(3)]
        area.at = mixture
        ACC = area.take(D)
        area.at = mixture
        XS = area.take(B, D + 1)
        ML = area.take(B, NS)
        SI, SIT, MEAN = area.take(D), area.take(2, P), area.take(2, 1)
        SW1, SW2 = area.take(4, P), area.take(NS)
        SWih, SWhh, Sbih, Sbhh = area.take(2, 3 * D), area.take(2, 3 * D), area.take(3 * D), area.take(3 * D)
        SWq, SWk, SWv, SWvp, SWo = area.take(2, DQ), area.take(2, DQ), area.take(2, D), area.take(2, D), area.take(2, D)
        Sb1, Sb2, Sbq, Sbk = area.take(1), area.take(NS), area.take(1), area.take(1)
        Sbv, Sbvp, Sbo, Sg, Sb = area.take(D), area.take(D), area.take(D), area.take(2), area.take(2)
        BD = area.take(P)
        TAU = area.take(2)
        GH = area.take(3 * D)
        HG = [area.take(T) for _ in range(2)]
        LS, LR, LV = [[area.take(n) for _ in range(2)] for n in (NS, NS, 8)]
        pair = [Named(AL=area.take(2, NS), ALP=area.take(2, P), AS=area.take(2), AR=area.take(2),
                                ALT=area.take(T), DEN=area.take(1), SU=area.take(D), SUT=area.take(2, P),
                                RZ=area.take(2 * D), NN=area.take(D), S=area.take(D), ST=area.take(2, P),
                                QS=area.take(2, P), VS=area.take(D), AT=area.take(P), AX=area.take(1), AU=area.take(1),
                                AI=area.take(1), ATT=area.take(P), Y=area.take(D), y6=area.take(6), ymv=area.take(2),
                                yrs=area.take(1), YT=area.take(2, P), SV=area.take(D), MT=area.take(4, T))
                for _ in range(2)]
        slot_loads = []
        for dst, n in ((SI, "slot_init2"), (Sb1, "b1"), (Sbq, "bq"), (Sbk, "bk"), (Sg, "ln_g"), (Sb, "ln_b"), (BD, "apart"),
                       (SW2, "w2")):
            slot_loads.append((dst, a["F3_" + n]))
        for dst, n in ((SIT, "slot_initT2"), (SW1, "w1"), (SWih, "WihT"), (SWhh, "WhhT"), (SWq, "wq"), (SWk, "wk"),
                       (SWv, "wv"), (SWvp, "wvp"), (SWo, "wo")):
            slot_loads.append((dst, a["F3_" + n].rearrange("(c p) n -> p c n", p=P)))
        for dst, n in ((Sbih, "bih"), (Sbhh, "bhh"), (Sb2, "b2"), (Sbv, "bv"), (Sbvp, "bvp"), (Sbo, "bo"), (TAU[:, 0:1], "tau")):
            src = a["F3_" + n]
            slot_loads.append((dst, src.rearrange("(o n) -> o n", o=1).broadcast_to([P, src.shape[0]])))

        def kt(L, j):
            m = 4 if L == 1 else 2
            return KT[j][:, 0:m * 512].rearrange("p (m n) -> p m n", m=m)

        def vv(L, j):
            n = 512 if L == 1 else 256
            return V[j][:, 0:CHUNKS[L] * n].rearrange("p (c n) -> p c n", n=n)

        phases = [p for p in BUILT if p <= last_phase]

        def eb1_at(eng, e, f):
            return eb1[:, e, f:f + 1]

        def q_is_first(q):
            return isinstance(q, int) and q == 0

        def begin(eng, p):
            if p != phases[0]:
                eng.wait_ge(ended, 4 * (phases.index(p) if p in phases else len(phases)))

        def end(eng):
            eng.drain().then_inc(ended, 1)

        block = ctx.enter_context(nc.Block())

        @block.sync
        def _(sp):
            sp.dma_start(X[0:T, :, :], a["x"].rearrange("b t d -> t b d")).then_inc(start.x_loaded, 16)
            sp.dma_start(ident[:, :], a["ident"]).then_inc(start.consts, 16)
            sp.dma_start(gates[:, :], a["gates"].rearrange("(o n) -> o n", o=1).broadcast_to([P, 8])).then_inc(start.gates, 16)
            for q, dst, src in loads:
                if q == 0:
                    sp.dma_start(dst, src).then_inc(loaded[q], 16)

            def later_loads():
                for q, dst, src in loads:
                    if q > 0:
                        sp.dma_start(dst, src).then_inc(loaded[q], 16)

            def attention(L):
                s = at[L]
                begin(sp, 2 * L)
                if L in (0, 3):
                    wait_for(sp, s.cleared, 1)

                def load(t, j):
                    bt = bass.ds(t, 1)
                    if L in (0, 3):
                        wait_for(sp, s.ln_ctx, 10 * (t - 1))
                        apart(sp)
                        src = a["ctx"][bt, :, :]
                        sp.dma_start(C[j][:, 0:NCH - 1, :],
                                     src[:, 0:(NCH - 1) * P, :].rearrange("o (c p) d -> p (o c) d", p=P)
                                     ).then_inc((s.ctx_in0, s.ctx_in1)[j].sem, 16)
                        sp.dma_start(C[j][0:LAST, NCH - 1, :],
                                     src[:, (NCH - 1) * P:NC, :].rearrange("o p d -> p (o d)")
                                     ).then_inc((s.ctx_in0, s.ctx_in1)[j].sem, 16)
                        if L == 0:
                            wait_for(sp, s.mask_row, t - 1)
                            apart(sp)
                            sp.dma_start(M8[j][0:T, :], a["mask"][bt, :].broadcast_to([T, NC])
                                         ).then_inc((s.mask_in0, s.mask_in1)[j].sem, 16)
                    else:
                        wait_for(sp, s.proj, STEPS[L] * (t - 1))
                        apart(sp)
                        src = a["ctxT"][bt, :, :]
                        for c in range(2):
                            sp.dma_start(CT[j][0:CW[c], c, 0:NC],
                                         src[:, c * P:c * P + CW[c], :].rearrange("o p n -> p (o n)")
                                         ).then_inc((s.ctx_in0, s.ctx_in1)[j].sem, 16)

                load(0, 0)
                load(1, 1)
                if 2 * L == phases[0]:
                    later_loads()
                with sp.Fori(1, B // 2) as i:
                    load(2 * i, 0)
                    load(2 * i + 1, 1)


            def dense_experts():
                begin(sp, 1)
                if 1 == phases[0]:
                    later_loads()
                s = mx0

                def load(e, j):
                    wait_count(sp, s.out, 16 * (e - 1))
                    apart(sp)
                    w = (s.w_in0, s.w_in1)[j]
                    src = a["F0_w1"][bass.ds(e, 1), :, :]
                    for c in range(2):
                        sp.dma_start(W1[j][:, c, :], src[:, c * P:(c + 1) * P, :].rearrange("o p n -> p (o n)")
                                     ).then_inc(w, 16)
                    sp.dma_start(W2[j][:, :, :], a["F0_w2"][bass.ds(e, 1), :, :].rearrange("o (c p) n -> p (o c) n", p=P)
                                 ).then_inc(w, 16)

                load(0, 0)
                load(1, 1)
                with sp.Fori(1, E0 // 2) as i:
                    load(2 * i, 0)
                    load(2 * i + 1, 1)

            def squared_experts():
                begin(sp, 3)
                if 3 == phases[0]:
                    later_loads()

            def linear_experts():
                begin(sp, 5)
                if 5 == phases[0]:
                    later_loads()

            def slot_mixer():
                begin(sp, 7)
                if 7 == phases[0]:
                    later_loads()
                for dst, src in slot_loads:
                    sp.dma_start(dst, src).then_inc(mx3.w_in, 16)

            for p in phases:
                if p % 2 == 0:
                    attention(p // 2)
                else:
                    (dense_experts, squared_experts, linear_experts, slot_mixer)[p // 2]()
            begin(sp, None)
            for p in range(8):
                if n_loads[p]:
                    sp.wait_ge(loaded[p], 16 * n_loads[p])
            sp.dma_start(out.rearrange("b t d -> t b d"), X[0:T, :, :]).then_inc(stored, 16)
            sp.wait_ge(stored, 16)

        @block.gpsimd
        def _(pool):
            nc.gpsimd.memset(neg_half[:, :], -0.5).then_inc(start.neg_half, 1)
            pool.wait_ge(start.neg_half, 1)

            def attention(L):
                s = at[L]
                begin(pool, 2 * L)
                def prepare(t, j):
                    def ln_ctx():
                        wait_for(pool, s.ln_ctx, 10 * t + 7)
                        nc.gpsimd.tensor_tensor(rs[j][:, 0:3], rs[j][:, 0:3], neg_half[:, 0:3], ALU.pow
                                                ).then_inc(s.rstd_ctx.sem, 1)

                    def ln_x(k):
                        wait_for(pool, s.ln_x, 4 * (NORMS[L] * t + k) + 3)
                        nc.gpsimd.tensor_tensor(rs[j][0:T, 3:4], rs[j][0:T, 3:4], neg_half[0:T, 0:1], ALU.pow
                                                ).then_inc(s.rstd_x.sem, 1)

                    if L in (0, 3):
                        ln_ctx()
                    for k in range(NORMS[L]):
                        ln_x(k)
                    if L == 0:
                        wait_for(pool, s.qk_rms, 4 * t + 3)
                        nc.gpsimd.tensor_tensor(rr[j][:, :], rr[j][:, :], neg_half[:, 0:20], ALU.pow
                                                ).then_inc(s.rqk.sem, 1)

                in_turn(pool, prepare)
                end(pool)


            def rstd_x(s, p, last=True):
                begin(pool, p)

                def one(t, j):
                    pool.wait_ge(s.ln_x, 4 * t + 3)
                    nc.gpsimd.tensor_tensor(Frs[j][0:T, :], Frs[j][0:T, :], neg_half[0:T, 0:1], ALU.pow
                                            ).then_inc(s.rstd_x, 1)

                in_turn(pool, one)
                if last:
                    end(pool)

            def dense_experts():
                rstd_x(mx0, 1)

            def squared_experts():
                rstd_x(mx1, 3)

            def linear_experts():
                rstd_x(mx2, 5)

            def slot_mixer():
                s = mx3
                rstd_x(s, 7, last=False)

                def one(u, k):
                    pool.wait_ge(s.y_stats, 4 * (u + 1))
                    nc.gpsimd.tensor_tensor(pair[k].yrs[:, :], pair[k].yrs[:, :], neg_half[:, 0:1], ALU.pow
                                            ).then_inc(s.rstd_y, 1)

                with pool.Fori(0, B // 4) as i:
                    one(2 * i, 0)
                    one(2 * i + 1, 1)
                end(pool)

            for p in phases:
                if p % 2 == 0:
                    attention(p // 2)
                else:
                    (dense_experts, squared_experts, linear_experts, slot_mixer)[p // 2]()

        @block.scalar
        def _(act):
            act.wait_ge(start.gates, 16)
            nc.scalar.activation(gates[:, :], gates[:, :], ACT.Tanh).then_inc(start.gates_done, 1)
            act.wait_ge(loaded[0], 16 * n_loads[0])
            nc.scalar.mul(qg0s[:, :], q_gain[:, :], HWID[0] ** -0.5).then_inc(start.scaled, 1)
            act.wait_ge(start.scaled, 1)

            def attention(L):
                s = at[L]
                H, W, NK = HEADS[L], HWID[L], KEYS[L]
                scale = float(W) ** -0.5
                begin(act, 2 * L)
                wait_for(act, s.cleared, 1)
                if L == 3:
                    act.wait_ge(loaded[6], 16 * n_loads[6])
                    nc.scalar.mul(bq3s[:, :], bq3[:, :], scale).then_inc(start.scaled, 1)
                    act.wait_ge(start.scaled, 2)

                def step(t, j, n):
                    src = J_bank[(j * STEPS[L] + n) % 2]
                    wait_for(act, s.proj, STEPS[L] * t + n + 1)
                    kind = n
                    if L == 0:
                        if n in (0, 1):
                            m = CW[n]
                            ins = nc.scalar.activation(CT[j][0:m, n, :], src[0:m, 0:NKP], ACT.Identity,
                                                       bias=ctx_bias[0][0:m, n:n + 1], scale=ctx_gain[0][0:m, n:n + 1])
                        elif n == 2:
                            for c in range(2):
                                ins = nc.scalar.activation(XT[j][:, c, 0:T], src[:, c * T:(c + 1) * T], ACT.Identity,
                                                           bias=x_bias[0][:, c:c + 1], scale=x_gain[0][:, c:c + 1])
                        elif n in (3, 4, 5, 6):
                            nc.scalar.copy(QK[j][:, n - 3, :], src[:, 0:D])
                            ins = nc.scalar.copy(vv(0, j)[:, n - 3, :], src[:, D:2 * D])
                        elif n == 7:
                            ins = nc.scalar.copy(QK[j][0:T, 4, :], src[0:T, 0:D])
                        elif n in (8, 9):
                            ins = nc.scalar.mul(kt(0, j)[:, n - 8, :], src[:, :], k_gain[:, 0:1])
                        else:
                            ins = nc.scalar.mul(QT[j][:, 0:2, :], src[:, 0:2 * T].rearrange("p (m t) -> p m t", m=2),
                                                qg0s[:, 0:1])
                    else:
                        if L == 3:
                            if n in (0, 1):
                                m = CW[n]
                                ins = nc.scalar.activation(CT[j][0:m, n, :], src[0:m, 0:NKP], ACT.Identity,
                                                           bias=ctx_bias[3][0:m, n:n + 1], scale=ctx_gain[3][0:m, n:n + 1])
                            kind = n - 2
                        MQ = 4 if L == 1 else 2
                        if kind == 0:
                            if L == 3:
                                for c in range(2):
                                    ins = nc.scalar.activation(XT[j][:, c, 0:T], src[:, c * T:(c + 1) * T], ACT.Identity,
                                                               bias=x_bias[3][:, c:c + 1], scale=x_gain[3][:, c:c + 1])
                            else:
                                ins = nc.scalar.copy(XT[j][:, :, 0:T], src[:, 0:2 * T].rearrange("p (c t) -> p c t", c=2))
                        elif kind == 1:
                            if L == 3:
                                for m in range(2):
                                    ins = nc.scalar.activation(QT[j][:, m, :], src[:, m * T:(m + 1) * T], ACT.Identity,
                                                               bias=bq3s[:, m:m + 1], scale=scale)
                            else:
                                ins = nc.scalar.mul(QT[j][:, 0:MQ, :], src[:, 0:MQ * T].rearrange("p (m t) -> p m t", m=MQ),
                                                    scale)
                        elif 2 <= kind < 2 + MQ:
                            m = kind - 2
                            if L == 3:
                                ins = nc.scalar.activation(kt(3, j)[:, m, 0:NC], src[:, 0:NC], ACT.Identity,
                                                           bias=bk3[:, m:m + 1])
                            else:
                                ins = nc.scalar.copy(kt(L, j)[:, m, 0:NC], src[:, 0:NC])
                        elif kind >= 2 + MQ:
                            c = kind - 2 - MQ
                            ins = nc.scalar.copy(vv(L, j)[:, c, :], src[:, 0:(512 if L == 1 else 256)])
                    ins.then_inc(s.copied.sem, 1)

                def exp(t, j, h):
                    n = H * t + h
                    k = (H * j + h) % 2
                    wait_for(act, s.maxed, MAXES[L] * (n + 1))
                    wait_for(act, s.probs_turned, n - 1)
                    pr = PR[k][0:T, :, :].rearrange("p c n -> p (c n)")
                    nc.scalar.activation(pr[:, 0:NK], S_bank[k][0:T, 0:NK], ACT.Exp, bias=nmax[k][0:T, :],
                                         accum_out=rsum[j][0:T, h:h + 1]).then_inc(s.exped.sem, 1)

                def o_copy(t, j):
                    wait_for(act, s.o_turned, t + 1)
                    wait_for(act, s.out, t)
                    m = 4 if L == 1 else 2
                    nc.scalar.copy(OT[:, 0:m, :], R_bank[:, 0:m * T].rearrange("p (m t) -> p m t", m=m)
                                   ).then_inc(s.o_copied.sem, 1)

                def prepare(t, j):
                    for n in range(STEPS[L]):
                        step(t, j, n)

                def attend(t, j, more):
                    exp(t, j, 0)
                    if H > 1:
                        exp(t, j, 1)
                    if not (isinstance(t, int) and t == 0):
                        o_copy(t - 1, 1 - j)
                    for h in range(H):
                        if more:
                            for n in GROUPS[L][h]:
                                step(t + 1, 1 - j, n)
                        if h + 2 < H:
                            exp(t, j, h + 2)

                pipelined(act, prepare, attend, o_copy)
                end(act)


            def x_copy(s, t, j):
                act.wait_ge(s.x_turned, t + 1)
                nc.scalar.copy(FXT[j][:, :, :], bank[0][:, 0:2 * T].rearrange("p (c t) -> p c t", c=2)
                               ).then_inc(s.x_copied, 1)

            def exp_difference(s, n_route, t, j):
                act.wait_ge(s.route, n_route * t + 4)
                nc.scalar.activation(ED[j][0:T, 1:2], ED[j][0:T, 0:1], ACT.Exp).then_inc(s.exped, 1)

            def dense_experts():
                s = mx0
                begin(act, 1)
                act.wait_ge(loaded[1], 16 * n_loads[1])

                def batch(t, j):
                    act.wait_ge(s.x_turned, t + 1)
                    src = bank[0][:, 0:2 * T].rearrange("p (c t) -> p c t", c=2)
                    nc.scalar.copy(FXT[j][:, :, :], src).then_inc(s.x_copied, 1)
                    nc.scalar.copy(XA[:, :, bass.ds(T * t, T)], src).then_inc(s.x_copied, 1)
                    act.wait_ge(s.oh_turned, t + 1)
                    nc.scalar.copy(OHT[j][0:E0, :], bank[1][0:E0, 128:128 + T]).then_inc(s.oh_copied, 1)

                in_turn(act, batch)

                def tokens(e, q):
                    for f in range(HID0 // P):
                        n = 8 * (4 * e + q) + f
                        act.wait_ge(s.gate, n + 1)
                        wait_count(act, s.hidden, n - 1)
                        nc.scalar.activation(SG[f % 2][:, :], bank[2 + f % 2][:, 0:QT_TOK], ACT.Sigmoid,
                                             bias=eb1_at(act, e, 8 + f)).then_inc(s.sigmoid, 1)

                for e in range(E0):
                    tokens(e, 0)
                    tokens(e, 1)
                    with act.Fori(2, 4) as q:
                        tokens(e, q)
                end(act)

            def squared_experts():
                s = mx1
                begin(act, 3)

                def hidden(t, j, g):
                    act.wait_ge(s.hidden, 3 * t + g + 1)
                    nc.scalar.activation(RL[g][0:T, :], bank[2 + g][0:T, 0:3 * HID1], ACT.Relu).then_inc(s.relu, 1)
                    act.wait_ge(s.relu, 3 * t + g + 1)
                    nc.scalar.square(SQ[g][0:T, :], RL[g][0:T, :]).then_inc(s.squared, 1)

                def prepare(t, j):
                    x_copy(s, t, j)
                    exp_difference(s, 9, t, j)
                    for g in range(3):
                        hidden(t, j, g)

                def attend(t, j, more):
                    if more:
                        prepare(t + 1, 1 - j)

                pipelined(act, prepare, attend, lambda t, j: None)
                end(act)

            def linear_experts():
                s = mx2
                begin(act, 5)

                def prepare(t, j):
                    x_copy(s, t, j)
                    exp_difference(s, 11, t, j)

                in_turn(act, prepare)
                end(act)

            def slot_mixer():
                s = mx3
                begin(act, 7)
                act.wait_ge(s.w_in, 16 * len(slot_loads))

                def prepare(t, j):
                    x_copy(s, t, j)

                def attend(t, j, more):
                    act.wait_ge(s.hidden, t + 1)
                    if isinstance(t, int) and t == 0:
                        act.wait_ge(s.consts, 9)
                    nc.scalar.activation(HG[j][:, :], bank[1 + j][:, 0:T], ACT.Gelu, bias=Sb1[:, 0:1]).then_inc(s.gelu, 1)
                    if more:
                        prepare(t + 1, 1 - j)

                pipelined(act, prepare, attend, lambda t, j: None)

                def weights(u, k):
                    w = pair[k]
                    for m in range(2):
                        ins = nc.scalar.activation(w.AL[0:T, m, :], ML[0:T, bass.ds(2 * u + m, 1), :], ACT.Exp,
                                                   accum_out=w.AS[0:T, m:m + 1])
                    ins.then_inc(s.exped, 1)

                def pooled(u, k):
                    act.wait_ge(s.pooled_turned, u + 1)
                    nc.scalar.copy(pair[k].SUT[:, :, :], bank[4 * k][:, 0:2 * P].rearrange("p (c n) -> p c n", c=2)
                                   ).then_inc(s.pooled_copied, 1)

                def rz_tanh(u, k):
                    act.wait_ge(s.rz_in, 2 * u + 1)
                    nc.scalar.activation(pair[k].RZ[:, :], pair[k].RZ[:, :], ACT.Tanh, scale=0.5).then_inc(s.rz_tanh, 1)

                def n_tanh(u, k):
                    act.wait_ge(s.rz_done, 3 * (u + 1))
                    nc.scalar.activation(pair[k].NN[:, :], pair[k].NN[:, :], ACT.Tanh).then_inc(s.n_tanh, 1)

                def slots_copy(u, k):
                    act.wait_ge(s.s_turned, u + 1)
                    nc.scalar.copy(pair[k].ST[:, :, :], bank[4 * k][:, 0:2 * P].rearrange("p (c n) -> p c n", c=2)
                                   ).then_inc(s.s_copied, 1)

                def qk_copy(u, k):
                    act.wait_ge(s.qkv, u + 1)
                    for m, b in ((0, Sbq), (1, Sbk)):
                        ins = nc.scalar.activation(pair[k].QS[0:DQ, m, :], bank[4 * k + 1][0:DQ, m * P:(m + 1) * P],
                                                   ACT.Identity, bias=b[0:DQ, 0:1])
                    ins.then_inc(s.qk_copied, 1)

                def attn_exp(u, k):
                    act.wait_ge(s.masked, 2 * (u + 1))
                    nc.scalar.activation(pair[k].AT[:, :], pair[k].AT[:, :], ACT.Exp, bias=pair[k].AX[:, 0:1],
                                         accum_out=pair[k].AU[:, 0:1]).then_inc(s.attn_exped, 1)

                def y_copy(u, k):
                    act.wait_ge(s.y_turned, u + 1)
                    for c in range(2):
                        ins = nc.scalar.activation(pair[k].YT[:, c, :], bank[4 * k][:, c * P:(c + 1) * P], ACT.Identity,
                                                   bias=Sb[:, c:c + 1], scale=Sg[:, c:c + 1])
                    ins.then_inc(s.y_copied, 1)

                def mixed_copy(u, k):
                    act.wait_ge(s.mixed, u + 1)
                    for m in range(2):
                        ins = nc.scalar.copy(pair[k].MT[:, 2 * m:2 * m + 2, :],
                                             bank[4 * k + 3 * (1 - m)][:, 0:2 * T].rearrange("p (c t) -> p c t", c=2))
                    ins.then_inc(s.mixed_copied, 1)

                act.wait_ge(s.picked, 8 * B)
                with act.Fori(0, B // 4) as i:
                    for stage in (weights, pooled, rz_tanh, n_tanh, slots_copy, qk_copy, attn_exp, y_copy, mixed_copy):
                        stage(2 * i, 0)
                        stage(2 * i + 1, 1)
                end(act)

            for p in phases:
                if p % 2 == 0:
                    attention(p // 2)
                else:
                    (dense_experts, squared_experts, linear_experts, slot_mixer)[p // 2]()

        @block.vector
        def _(dve):
            dve.wait_ge(start.gates_done, 1)
            dve.wait_ge(start.x_loaded, 16)

            def attention(L):
                s = at[L]
                H, W, NK, CH = HEADS[L], HWID[L], KEYS[L], CHUNKS[L]
                begin(dve, 2 * L)
                for j in range(2):
                    if L in (0, 3):
                        nc.vector.memset(C[j][96:P, NCH - 1, :], 0.0)
                    if L == 0:
                        nc.vector.memset(XT[j][:, :, T:P], 0.0)
                        nc.vector.memset(QK[j][96:P, 4, :], 1.0)
                        nc.vector.memset(MR[j][0:T, NCH - 1, LAST:P], FAR)
                        nc.vector.memset(MR[j][0:T, NCH, 0:T], 0.0)
                        nc.vector.memset(MR[j][0:T, NCH, T:P], FAR)
                    if L in (1, 2):
                        nc.vector.memset(CT[j][:, :, NC:NKP], 0.0)
                    if L > 0:
                        nc.vector.memset(PR[j][0:T, NCH - 1, LAST:P], 0.0)
                dve.drain().then_inc(s.cleared.sem, 1)
                wait_for(dve, s.cleared, 1)
                dve.wait_ge(loaded[2 * L], 16 * n_loads[2 * L])

                def ln_ctx_stats(t, j):
                    wait_for(dve, (s.ctx_in0, s.ctx_in1)[j], 32 * (t // 2 + 1))
                    b = 10 * t
                    for c in range(NCH):
                        nc.vector.bn_stats(st6[j][:, c, :], C[j][:, c, :]).then_inc(s.ln_ctx.sem, 1)
                    wait_for(dve, s.ln_ctx, b + 3)
                    apart(dve)
                    for c in range(NCH):
                        nc.vector.bn_aggr(mv[j][:, c, :], st6[j][:, c, :]).then_inc(s.ln_ctx.sem, 1)
                    wait_for(dve, s.ln_ctx, b + 6)
                    nc.vector.tensor_scalar(rs[j][:, 0:3], mv[j][:, 0:3, 1], LN_EPS, None, ALU.add).then_inc(s.ln_ctx.sem, 1)

                def ln_ctx_norm(t, j):
                    wait_for(dve, s.rstd_ctx, t + 1)
                    for c in range(NCH):
                        nc.vector.tensor_scalar(CNorm[j][:, c, :], C[j][:, c, :], mv[j][:, c, 0:1], rs[j][:, c:c + 1],
                                                ALU.subtract, ALU.mult).then_inc(s.ln_ctx.sem, 1)

                def ln_x(t, j, k):
                    b = 4 * (NORMS[L] * t + k)
                    src = X[0:T, bass.ds(t, 1), :] if k == 0 else XN[j][0:T, :]
                    dst = XN[j] if k == 0 else XN2[j]
                    if k:
                        wait_for(dve, s.ln_x, b)
                    nc.vector.bn_stats(st6[j][0:T, 3, :], src).then_inc(s.ln_x.sem, 1)
                    wait_for(dve, s.ln_x, b + 1)
                    apart(dve)
                    nc.vector.bn_aggr(mv[j][0:T, 3, :], st6[j][0:T, 3, :]).then_inc(s.ln_x.sem, 1)
                    wait_for(dve, s.ln_x, b + 2)
                    nc.vector.tensor_scalar(rs[j][0:T, 3:4], mv[j][0:T, 3, 1:2], LN_EPS, None, ALU.add).then_inc(s.ln_x.sem, 1)

                def ln_x_norm(t, j, k):
                    src = X[0:T, bass.ds(t, 1), :] if k == 0 else XN[j][0:T, :]
                    dst = XN[j] if k == 0 else XN2[j]
                    wait_for(dve, s.rstd_x, NORMS[L] * t + k + 1)
                    nc.vector.tensor_scalar(dst[0:T, :], src, mv[j][0:T, 3, 0:1], rs[j][0:T, 3:4],
                                            ALU.subtract, ALU.mult).then_inc(s.ln_x.sem, 1)

                def mask_row(t, j):
                    wait_for(dve, (s.mask_in0, s.mask_in1)[j], 16 * (t // 2 + 1))
                    mr = MR[j][0:T, :, :].rearrange("p c n -> p (c n)")
                    nc.vector.tensor_scalar(mr[:, 0:NC], M8[j][0:T, :], -FAR, FAR, ALU.mult, ALU.add
                                            ).then_inc(s.mask_row.sem, 1)

                def rms(t, j):
                    wait_for(dve, s.copied, STEPS[L] * t + 8)
                    b = 4 * t
                    nc.vector.tensor_tensor(QKsq[:, :, :], QK[j][:, :, :], QK[j][:, :, :], ALU.mult).then_inc(s.qk_rms.sem, 1)
                    wait_for(dve, s.qk_rms, b + 1)
                    nc.vector.reduce_sum(ss[j][:, :], QKsq[:, :, :].rearrange("p c (h w) -> p (c h) w", w=W), axis=AXX
                                         ).then_inc(s.qk_rms.sem, 1)
                    wait_for(dve, s.qk_rms, b + 2)
                    nc.vector.tensor_scalar(rr[j][:, :], ss[j][:, :], 1.0 / W, 1e-16, ALU.mult, ALU.max
                                            ).then_inc(s.qk_rms.sem, 1)

                def rms_scale(t, j):
                    wait_for(dve, s.rqk, t + 1)
                    v = QK[j][:, :, :].rearrange("p c (h w) -> p (c h) w", w=W)
                    nc.vector.tensor_tensor(v, v, rr[j][:, :].rearrange("p (n o) -> p n o", o=1).broadcast_to([P, 20, W]),
                                            ALU.mult).then_inc(s.qk_rms.sem, 1)

                def maximum(t, j, h):
                    n = H * t + h
                    k = (H * j + h) % 2
                    wait_for(dve, s.scores, n + 1)
                    if L == 0:
                        if h == 0:
                            wait_for(dve, s.mask_row, t + 1)
                        sc = S_bank[k][0:T, 0:NK]
                        apart(dve)
                        nc.vector.tensor_tensor_reduce(out=sc, in0=sc, in1=MR[j][0:T, :, :].rearrange("p c n -> p (c n)"),
                                                       scale=1.0, scalar=-3.0e38, op0=ALU.add, op1=ALU.max,
                                                       accum_out=pmax[k][0:T, :]).then_inc(s.maxed.sem, 1)
                        wait_for(dve, s.maxed, 2 * n + 1)
                        nc.vector.tensor_scalar(nmax[k][0:T, :], pmax[k][0:T, :], -1.0, None, ALU.mult).then_inc(s.maxed.sem, 1)
                    else:
                        nc.vector.tensor_reduce(nmax[k][0:T, :], S_bank[k][0:T, 0:NK], axis=AXX, op=ALU.max,
                                                negate=True).then_inc(s.maxed.sem, 1)

                def probs_copy(t, j, h):
                    n = H * t + h
                    k = (H * j + h) % 2
                    wait_for(dve, s.probs_turned, n + 1)
                    wait_for(dve, s.pv, n - 1)
                    nc.vector.tensor_copy(PT[k][:, 0:CH, :], PT_bank[k][:, 0:CH * T].rearrange("p (c t) -> p c t", c=CH)
                                          ).then_inc(s.probs_copied.sem, 1)

                def o_scale(t, j):
                    wait_for(dve, s.pv, H * (t + 1))
                    wait_for(dve, s.o_turned, t)
                    nc.vector.reciprocal(rinv[0:T, 0:H], rsum[j][0:T, 0:H]).then_inc(s.o_scaled.sem, 1)
                    wait_for(dve, s.o_scaled, 2 * t + 1)
                    if H == 1:
                        nc.vector.scalar_tensor_tensor(O[0:T, 0:W], O_bank[0:T, 0:W], rinv[0:T, 0:1], bv3[0:T, :],
                                                       ALU.mult, ALU.add).then_inc(s.o_scaled.sem, 1)
                    else:
                        nc.vector.tensor_tensor(O[0:T, 0:H * W].rearrange("p (h w) -> p h w", h=H),
                                                O_bank[0:T, 0:H * W].rearrange("p (h w) -> p h w", h=H),
                                                rinv[0:T, 0:H].rearrange("p (h o) -> p h o", o=1).broadcast_to([T, H, W]),
                                                ALU.mult).then_inc(s.o_scaled.sem, 1)

                def residual(t, j):
                    wait_for(dve, s.out, t + 1)
                    nc.vector.tensor_tensor(RO[0:T, :], R_bank[0:T, 0:D], bo[L][0:T, :], ALU.add).then_inc(s.resid.sem, 1)
                    wait_for(dve, s.resid, 2 * t + 1)
                    xt = X[0:T, bass.ds(t, 1), :].rearrange("p o d -> p (o d)")
                    nc.vector.scalar_tensor_tensor(xt, RO[0:T, :], gates[0:T, L:L + 1], xt, ALU.mult, ALU.add
                                                   ).then_inc(s.resid.sem, 1)

                def norms(t, j):
                    if L in (0, 3):
                        ln_ctx_stats(t, j)
                    ln_x(t, j, 0)
                    if L in (0, 3):
                        ln_ctx_norm(t, j)
                    if L == 0:
                        mask_row(t, j)
                    ln_x_norm(t, j, 0)
                    if NORMS[L] == 2:
                        ln_x(t, j, 1)
                        ln_x_norm(t, j, 1)

                def prepare(t, j):
                    norms(t, j)
                    if L == 0:
                        rms(t, j)
                        rms_scale(t, j)

                def attend(t, j, more):
                    maximum(t, j, 0)
                    if H > 1:
                        maximum(t, j, 1)
                    if more:
                        norms(t + 1, 1 - j)
                    for h in range(H):
                        probs_copy(t, j, h)
                        if h == 0 and not (isinstance(t, int) and t == 0):
                            residual(t - 1, 1 - j)
                        if h + 2 < H:
                            maximum(t, j, h + 2)
                        if L == 0 and more and h == 2:
                            rms(t + 1, 1 - j)
                    if L == 0 and more:
                        rms_scale(t + 1, 1 - j)
                    o_scale(t, j)

                pipelined(dve, prepare, attend, residual)
                end(dve)


            def x_norm(s, t, j):
                src = X[0:T, bass.ds(t, 1), :]
                nc.vector.bn_stats(Fst6[j][0:T, :], src).then_inc(s.ln_x, 1)
                dve.wait_ge(s.ln_x, 4 * t + 1)
                apart(dve)
                nc.vector.bn_aggr(Fmv[j][0:T, :], Fst6[j][0:T, :]).then_inc(s.ln_x, 1)
                dve.wait_ge(s.ln_x, 4 * t + 2)
                nc.vector.tensor_scalar(Frs[j][0:T, :], Fmv[j][0:T, 1:2], LN_EPS, None, ALU.add).then_inc(s.ln_x, 1)
                dve.wait_ge(s.rstd_x, t + 1)
                wait_count(dve, s.x_turned, t - 1)
                nc.vector.tensor_scalar(FX[j][0:T, :], src, Fmv[j][0:T, 0:1], Frs[j][0:T, :],
                                        ALU.subtract, ALU.mult).then_inc(s.ln_x, 1)

            def choose(s, n, t, j, bias=None):
                b = n * t
                dve.wait_ge(s.logits, t + 1)
                if bias is None:
                    nc.vector.tensor_copy(LG[j][0:T, :], bank[1][0:T, 0:8]).then_inc(s.route, 1)
                else:
                    nc.vector.tensor_tensor(LG[j][0:T, :], bank[1][0:T, 0:8], bias[0:T, :], ALU.add).then_inc(s.route, 1)
                dve.wait_ge(s.route, b + 1)
                apart(dve)
                nc.vector.max(V8[j][0:T, :], LG[j][0:T, :]).then_inc(s.route, 1)
                dve.wait_ge(s.route, b + 2)
                apart(dve)
                nc.vector.max_index(I8[j][0:T, :], V8[j][0:T, :], LG[j][0:T, :]).then_inc(s.route, 1)
                nc.vector.tensor_tensor(ED[j][0:T, 0:1], V8[j][0:T, 1:2], V8[j][0:T, 0:1], ALU.subtract).then_inc(s.route, 1)
                dve.wait_ge(s.route, b + 3)
                nc.vector.tensor_copy(IF[j][0:T, :], I8[j][0:T, 0:2]).then_inc(s.route, 1)

            def first_weight(s, n, t, j):
                dve.wait_ge(s.exped, t + 1)
                nc.vector.tensor_scalar(ED[j][0:T, 2:3], ED[j][0:T, 1:2], 1.0, None, ALU.add).then_inc(s.route, 1)
                dve.wait_ge(s.route, n * t + 6)
                nc.vector.reciprocal(ED[j][0:T, 3:4], ED[j][0:T, 2:3]).then_inc(s.route, 1)
                dve.wait_ge(s.route, n * t + 7)

            def dense_experts():
                s = mx0
                begin(dve, 1)
                dve.wait_ge(loaded[1], 16 * n_loads[1])

                def batch(t, j):
                    x_norm(s, t, j)
                    choose(s, 7, t, j, eb0)
                    dve.wait_ge(s.route, 7 * t + 5)
                    nc.vector.tensor_scalar(WF[j][0:T, 0:8], iota[0:T, :], IF[j][0:T, 0:1], None, ALU.is_equal
                                            ).then_inc(s.route, 1)
                    dve.wait_ge(s.route, 7 * t + 6)
                    nc.vector.tensor_scalar(OHG[0:T, bass.ds(t, 1), :], WF[j][0:T, 0:8], gates[0:T, 4:5], None, ALU.mult
                                            ).then_inc(s.route, 1)
                    dve.wait_ge(s.b2_row, t + 1)
                    xt = X[0:T, bass.ds(t, 1), :].rearrange("p o d -> p (o d)")
                    nc.vector.scalar_tensor_tensor(xt, bank[1][0:T, 256:512], gates[0:T, 4:5], xt, ALU.mult, ALU.add
                                                   ).then_inc(s.b2_added, 1)

                in_turn(dve, batch)

                def tokens(e, q):
                    for f in range(HID0 // P):
                        n = 8 * (4 * e + q) + f
                        dve.wait_ge(s.value, n + 1)
                        dve.wait_ge(s.sigmoid, n + 1)
                        if f == 0:
                            wait_count(dve, s.out, 4 * (4 * e + q))
                        nc.vector.scalar_tensor_tensor(AC[:, f, :], bank[4 + f % 2][:, 0:QT_TOK], eb1_at(dve, e, f),
                                                       SG[f % 2][:, :], ALU.add, ALU.mult).then_inc(s.hidden, 1)
                    for k in range(4):
                        m = 4 * (4 * e + q) + k
                        dve.wait_ge(s.out, m + 1)
                        t = 4 * q + k
                        xt = X[0:T, bass.ds(t, 1), :].rearrange("p o d -> p (o d)")
                        nc.vector.scalar_tensor_tensor(xt, bank[6 + k % 2][0:T, 0:D], OHG[0:T, bass.ds(t, 1), e:e + 1],
                                                       xt, ALU.mult, ALU.add).then_inc(s.resid, 1)

                for e in range(E0):
                    with dve.Fori(0, 4) as q:
                        tokens(e, q)
                end(dve)

            def squared_experts():
                s = mx1
                begin(dve, 3)
                for j in range(2):
                    nc.vector.memset(WF[j][0:T, 0:1], 1.0).then_inc(s.ones, 1)
                dve.wait_ge(loaded[3], 16 * n_loads[3])
                dve.wait_ge(loaded[1], 16 * n_loads[1])
                dve.wait_ge(s.ones, 2)

                def route(t, j):
                    choose(s, 9, t, j)
                    first_weight(s, 9, t, j)
                    nc.vector.tensor_scalar(ED[j][0:T, 4:5], ED[j][0:T, 3:4], 1.0, None, ALU.is_ge).then_inc(s.route, 1)
                    dve.wait_ge(s.route, 9 * t + 8)
                    nc.vector.tensor_scalar(WF[j][0:T, 1:9], iota[0:T, :], IF[j][0:T, 0:1], ED[j][0:T, 4:5],
                                            ALU.is_equal, ALU.mult).then_inc(s.route, 1)
                    dve.wait_ge(s.route, 9 * t + 9)

                def mask(t, j, g):
                    dve.wait_ge(s.squared, 3 * t + g + 1)
                    v = SQ[g][0:T, :].rearrange("p (e n) -> p e n", e=3)
                    w = WF[j][0:T, 3 * g:3 * g + 3].rearrange("p (e o) -> p e o", o=1).broadcast_to([T, 3, HID1])
                    nc.vector.tensor_tensor(v, v, w, ALU.mult).then_inc(s.masked, 1)

                def h_copy(t, j, g):
                    dve.wait_ge(s.h_turned, 3 * t + g + 1)
                    nc.vector.tensor_copy(HT[g][:, :, :], bank[5 + (3 * j + g) % 2][:, 0:3 * T].rearrange("p (c t) -> p c t", c=3)
                                          ).then_inc(s.h_copied, 1)

                def residual(t, j):
                    dve.wait_ge(s.out, t + 1)
                    xt = X[0:T, bass.ds(t, 1), :].rearrange("p o d -> p (o d)")
                    nc.vector.scalar_tensor_tensor(xt, bank[7][0:T, 0:D], gates[0:T, 5:6], xt, ALU.mult, ALU.add
                                                   ).then_inc(s.resid, 1)

                def prepare(t, j):
                    x_norm(s, t, j)
                    route(t, j)
                    for g in range(3):
                        mask(t, j, g)

                def attend(t, j, more):
                    if more:
                        x_norm(s, t + 1, 1 - j)
                    for g in range(3):
                        h_copy(t, j, g)
                    if more:
                        route(t + 1, 1 - j)
                        mask(t + 1, 1 - j, 0)
                    residual(t, j)
                    if more:
                        mask(t + 1, 1 - j, 1)
                        mask(t + 1, 1 - j, 2)

                pipelined(dve, prepare, attend, lambda t, j: None)
                end(dve)

            def linear_experts():
                s = mx2
                begin(dve, 5)
                dve.wait_ge(loaded[5], 16 * n_loads[5])
                dve.wait_ge(loaded[1], 16 * n_loads[1])

                def route(t, j):
                    choose(s, 11, t, j)
                    first_weight(s, 11, t, j)
                    nc.vector.tensor_tensor(ED[j][0:T, 4:5], ED[j][0:T, 1:2], ED[j][0:T, 3:4], ALU.mult).then_inc(s.route, 1)
                    nc.vector.tensor_scalar(WF[j][0:T, 0:8], iota[0:T, :], IF[j][0:T, 0:1], ED[j][0:T, 3:4],
                                            ALU.is_equal, ALU.mult).then_inc(s.route, 1)
                    dve.wait_ge(s.route, 11 * t + 8)
                    nc.vector.tensor_scalar(WB[j][0:T, :], iota[0:T, :], IF[j][0:T, 1:2], ED[j][0:T, 4:5],
                                            ALU.is_equal, ALU.mult).then_inc(s.route, 1)
                    dve.wait_ge(s.route, 11 * t + 10)
                    nc.vector.tensor_tensor(WF[j][0:T, 0:8], WF[j][0:T, 0:8], WB[j][0:T, :], ALU.add).then_inc(s.route, 1)
                    dve.wait_ge(s.route, 11 * t + 11)

                def combine(t, j, g):
                    dve.wait_ge(s.out, 4 * t + g + 1)
                    for k in range(2):
                        e = 2 * g + k
                        y, w = bank[2 + g][0:T, k * D:(k + 1) * D], WF[j][0:T, e:e + 1]
                        if e == 0:
                            nc.vector.tensor_scalar(ACC[0:T, :], y, w, None, ALU.mult).then_inc(s.combined, 1)
                        else:
                            dve.wait_ge(s.combined, 8 * t + e)
                            nc.vector.scalar_tensor_tensor(ACC[0:T, :], y, w, ACC[0:T, :], ALU.mult, ALU.add
                                                           ).then_inc(s.combined, 1)

                def prepare(t, j):
                    x_norm(s, t, j)
                    route(t, j)

                def attend(t, j, more):
                    if more:
                        x_norm(s, t + 1, 1 - j)
                    for g in range(4):
                        combine(t, j, g)
                    dve.wait_ge(s.combined, 8 * (t + 1))
                    xt = X[0:T, bass.ds(t, 1), :].rearrange("p o d -> p (o d)")
                    nc.vector.scalar_tensor_tensor(xt, ACC[0:T, :], gates[0:T, 6:7], xt, ALU.mult, ALU.add
                                                   ).then_inc(s.resid, 1)
                    if more:
                        route(t + 1, 1 - j)

                pipelined(dve, prepare, attend, lambda t, j: None)
                end(dve)

            def slot_mixer():
                s = mx3
                begin(dve, 7)
                for k in range(2):
                    nc.vector.memset(pair[k].ALP[0:T, 0, NS:P], 0.0)
                    nc.vector.memset(pair[k].ALP[0:T, 1, 0:NS], 0.0)
                nc.vector.memset(XS[0:T, :, D:D + 1], 1.0).then_inc(s.consts, 1)
                dve.wait_ge(s.w_in, 16 * len(slot_loads))
                nc.vector.reduce_sum(MEAN[:, :, :].rearrange("p c o -> p (c o)"), SIT[:, :, 0:NS], axis=AXX
                                     ).then_inc(s.consts, 1)
                nc.vector.tensor_scalar(TAU[:, 1:2], TAU[:, 0:1], -1.0, None, ALU.mult).then_inc(s.consts, 1)
                dve.wait_ge(s.consts, 3)
                nc.vector.tensor_scalar(MEAN[:, :, :], MEAN[:, :, :], 1.0 / NS, None, ALU.mult).then_inc(s.consts, 1)
                nc.vector.tensor_tensor(TAU[:, 0:1], TAU[:, 0:1], TAU[:, 1:2], ALU.max).then_inc(s.consts, 1)
                dve.wait_ge(s.consts, 5)
                nc.vector.tensor_scalar(TAU[:, 1:2], TAU[:, 0:1], 0.1, None, ALU.add).then_inc(s.consts, 1)
                dve.wait_ge(s.consts, 6)
                nc.vector.reciprocal(TAU[:, 0:1], TAU[:, 1:2]).then_inc(s.consts, 1)
                dve.wait_ge(s.const_sums, 1)
                nc.vector.tensor_tensor(GH[:, 0:512], bank[4][:, :], Sbhh[:, 0:512], ALU.add).then_inc(s.consts, 1)
                nc.vector.tensor_tensor(Sb1[:, :], bank[6][:, 0:1], Sb1[:, :], ALU.add).then_inc(s.consts, 1)
                dve.wait_ge(s.consts, 9)
                nc.vector.tensor_tensor(GH[:, 512:768], bank[5][:, 0:D], Sbhh[:, 512:768], ALU.add).then_inc(s.consts, 1)
                nc.vector.tensor_tensor(GH[:, 0:512], GH[:, 0:512], Sbih[:, 0:512], ALU.add).then_inc(s.consts, 1)
                dve.wait_ge(s.consts, 11)

                def pick(t, j):
                    b = 8 * t
                    nc.vector.tensor_copy(XS[0:T, bass.ds(t, 1), 0:D].rearrange("p o d -> p (o d)"), FX[j][0:T, :]
                                          ).then_inc(s.picked, 1)
                    dve.wait_ge(s.logits, t + 1)
                    nc.vector.tensor_tensor(LS[j][0:T, :], bank[3][0:T, 0:NS], Sb2[0:T, :], ALU.add).then_inc(s.picked, 1)
                    dve.wait_ge(s.picked, b + 2)
                    nc.vector.tensor_scalar(LS[j][0:T, :], LS[j][0:T, :], TAU[0:T, 0:1], None, ALU.mult
                                            ).then_inc(s.picked, 1)
                    dve.wait_ge(s.picked, b + 3)
                    apart(dve)
                    nc.vector.max(LV[j][0:T, :], LS[j][0:T, :]).then_inc(s.picked, 1)
                    dve.wait_ge(s.picked, b + 4)
                    apart(dve)
                    nc.vector.match_replace(out=LR[j][0:T, :], in_to_replace=LV[j][0:T, :], in_values=LS[j][0:T, :],
                                            imm_value=-3.0e38).then_inc(s.picked, 1)
                    dve.wait_ge(s.picked, b + 5)
                    nc.vector.tensor_tensor(LR[j][0:T, :], LR[j][0:T, :], LS[j][0:T, :], ALU.is_equal).then_inc(s.picked, 1)
                    dve.wait_ge(s.picked, b + 6)
                    nc.vector.tensor_scalar(LS[j][0:T, :], LS[j][0:T, :], LV[j][0:T, 0:1], None, ALU.subtract
                                            ).then_inc(s.picked, 1)
                    dve.wait_ge(s.picked, b + 7)
                    nc.vector.scalar_tensor_tensor(ML[0:T, bass.ds(t, 1), :].rearrange("p o n -> p (o n)"), LR[j][0:T, :],
                                                   FAR, LS[j][0:T, :], ALU.mult, ALU.add).then_inc(s.picked, 1)

                def prepare(t, j):
                    x_norm(s, t, j)

                def attend(t, j, more):
                    if more:
                        prepare(t + 1, 1 - j)
                    if isinstance(t, int) and t == 0:
                        dve.wait_ge(s.ln_x, 4)
                    pick(t, j)

                pipelined(dve, prepare, attend, lambda t, j: None)

                def alpha(u, k):
                    w = pair[k]
                    dve.wait_ge(s.exped, u + 1)
                    nc.vector.reciprocal(w.AR[0:T, :], w.AS[0:T, :]).then_inc(s.alpha, 1)
                    dve.wait_ge(s.alpha, 3 * u + 1)
                    for m in range(2):
                        nc.vector.tensor_scalar(w.ALP[0:T, m, m * NS:(m + 1) * NS], w.AL[0:T, m, :], w.AR[0:T, m:m + 1],
                                                None, ALU.mult).then_inc(s.alpha, 1)

                def pooled(u, k):
                    w = pair[k]
                    dve.wait_ge(s.sums, u + 1)
                    nc.vector.tensor_scalar(w.DEN[:, :], bank[4 * k][:, D:D + 1], 1e-8, None, ALU.add).then_inc(s.pooled, 1)
                    dve.wait_ge(s.pooled, 3 * u + 1)
                    nc.vector.reciprocal(w.DEN[:, :], w.DEN[:, :]).then_inc(s.pooled, 1)
                    dve.wait_ge(s.pooled, 3 * u + 2)
                    nc.vector.tensor_scalar(w.SU[:, :], bank[4 * k][:, 0:D], w.DEN[:, 0:1], None, ALU.mult
                                            ).then_inc(s.pooled, 1)

                def alpha_copy(u, k):
                    dve.wait_ge(s.alpha_turned, u + 1)
                    nc.vector.tensor_copy(pair[k].ALT[:, :], bank[4 * k + 1][:, 0:T]).then_inc(s.alpha_copied, 1)

                def rz_in(u, k):
                    dve.wait_ge(s.gru_in, u + 1)
                    nc.vector.tensor_tensor(pair[k].RZ[:, :], bank[4 * k + 2][:, :], GH[:, 0:512], ALU.add).then_inc(s.rz_in, 1)
                    nc.vector.tensor_tensor(pair[k].NN[:, :], bank[4 * k + 3][:, 0:D], Sbih[:, 512:768], ALU.add
                                            ).then_inc(s.rz_in, 1)

                def rz_done(u, k):
                    w = pair[k]
                    dve.wait_ge(s.rz_tanh, u + 1)
                    nc.vector.tensor_scalar(w.RZ[:, :], w.RZ[:, :], 0.5, 0.5, ALU.mult, ALU.add).then_inc(s.rz_done, 1)
                    dve.wait_ge(s.rz_done, 3 * u + 1)
                    nc.vector.tensor_tensor(w.RZ[:, 0:D], w.RZ[:, 0:D], GH[:, 512:768], ALU.mult).then_inc(s.rz_done, 1)
                    dve.wait_ge(s.rz_done, 3 * u + 2)
                    nc.vector.tensor_tensor(w.NN[:, :], w.NN[:, :], w.RZ[:, 0:D], ALU.add).then_inc(s.rz_done, 1)

                def slots_new(u, k):
                    w = pair[k]
                    dve.wait_ge(s.n_tanh, u + 1)
                    nc.vector.tensor_tensor(w.S[:, :], SI[:, :], w.NN[:, :], ALU.subtract).then_inc(s.slots_new, 1)
                    dve.wait_ge(s.slots_new, 3 * u + 1)
                    nc.vector.tensor_tensor(w.S[:, :], w.S[:, :], w.RZ[:, D:2 * D], ALU.mult).then_inc(s.slots_new, 1)
                    dve.wait_ge(s.slots_new, 3 * u + 2)
                    nc.vector.tensor_tensor(w.S[:, :], w.S[:, :], w.NN[:, :], ALU.add).then_inc(s.slots_new, 1)

                def v_done(u, k):
                    dve.wait_ge(s.qkv, u + 1)
                    nc.vector.tensor_tensor(pair[k].VS[:, :], bank[4 * k + 3][:, 0:D], Sbv[:, :], ALU.add
                                            ).then_inc(s.v_done, 1)

                def masked(u, k):
                    w = pair[k]
                    dve.wait_ge(s.attn, u + 1)
                    nc.vector.scalar_tensor_tensor(w.AT[:, :], bank[4 * k + 2][:, 0:P], float(DQ) ** -0.5, BD[:, :],
                                                   ALU.mult, ALU.add).then_inc(s.masked, 1)
                    dve.wait_ge(s.masked, 2 * u + 1)
                    nc.vector.tensor_reduce(w.AX[:, :], w.AT[:, :], axis=AXX, op=ALU.max, negate=True).then_inc(s.masked, 1)

                def attn_copy(u, k):
                    w = pair[k]
                    dve.wait_ge(s.attn_turned, u + 1)
                    nc.vector.tensor_copy(w.ATT[:, :], bank[4 * k + 3][:, 0:P]).then_inc(s.attn_copied, 1)
                    nc.vector.reciprocal(w.AI[:, :], w.AU[:, :]).then_inc(s.attn_copied, 1)

                def y_stats(u, k):
                    w = pair[k]
                    dve.wait_ge(s.comm, u + 1)
                    dve.wait_ge(s.attn_copied, 2 * (u + 1))
                    nc.vector.scalar_tensor_tensor(w.Y[:, :], bank[4 * k + 2][:, 0:D], w.AI[:, 0:1], w.S[:, :],
                                                   ALU.mult, ALU.add).then_inc(s.y_stats, 1)
                    dve.wait_ge(s.y_stats, 4 * u + 1)
                    nc.vector.bn_stats(w.y6[:, :], w.Y[:, :]).then_inc(s.y_stats, 1)
                    dve.wait_ge(s.y_stats, 4 * u + 2)
                    apart(dve)
                    nc.vector.bn_aggr(w.ymv[:, :], w.y6[:, :]).then_inc(s.y_stats, 1)
                    dve.wait_ge(s.y_stats, 4 * u + 3)
                    nc.vector.tensor_scalar(w.yrs[:, :], w.ymv[:, 1:2], LN_EPS, None, ALU.add).then_inc(s.y_stats, 1)

                def y_norm(u, k):
                    w = pair[k]
                    dve.wait_ge(s.rstd_y, u + 1)
                    nc.vector.tensor_scalar(w.Y[:, :], w.Y[:, :], w.ymv[:, 0:1], w.yrs[:, :], ALU.subtract, ALU.mult
                                            ).then_inc(s.y_normed, 1)

                def values_done(u, k):
                    dve.wait_ge(s.values, u + 1)
                    nc.vector.tensor_tensor(pair[k].SV[:, :], bank[4 * k + 1][:, 0:D], Sbvp[:, :], ALU.add
                                            ).then_inc(s.values_done, 1)

                def residual(u, k):
                    dve.wait_ge(s.out, u + 1)
                    r = pair[k].RZ[0:T, :].rearrange("p (m d) -> p m d", m=2)
                    nc.vector.tensor_tensor(r, bank[4 * k + 2][0:T, :].rearrange("p (m d) -> p m d", m=2),
                                            Sbo[0:T, :].rearrange("p (o d) -> p o d", o=1).broadcast_to([T, 2, D]), ALU.add
                                            ).then_inc(s.resid, 1)
                    dve.wait_ge(s.resid, 2 * u + 1)
                    xt = X[0:T, bass.ds(2 * u, 2), :]
                    nc.vector.scalar_tensor_tensor(xt, r, gates[0:T, 7:8], xt, ALU.mult, ALU.add).then_inc(s.resid, 1)

                with dve.Fori(0, B // 4) as i:
                    for stage in (alpha, pooled, alpha_copy, rz_in, rz_done, slots_new, v_done, masked, attn_copy, y_stats,
                                  y_norm, values_done, residual):
                        stage(2 * i, 0)
                        stage(2 * i + 1, 1)
                end(dve)

            for p in phases:
                if p % 2 == 0:
                    attention(p // 2)
                else:
                    (dense_experts, squared_experts, linear_experts, slot_mixer)[p // 2]()

        @block.tensor
        def _(pe):
            pe.wait_ge(start.consts, 16)

            def attention(L):
                s = at[L]
                H, W, NK, CH = HEADS[L], HWID[L], KEYS[L], CHUNKS[L]
                VN = 512 if L == 1 else 256
                MQ = 4 if L == 1 else 2
                begin(pe, 2 * L)
                wait_for(pe, s.cleared, 1)
                pe.wait_ge(loaded[2 * L], 16 * n_loads[2 * L])

                def step(t, j, n):
                    dst = J_bank[(j * STEPS[L] + n) % 2]
                    wait_for(pe, s.copied, STEPS[L] * t + n - 1)
                    done = STEPS[L] * t
                    mm, tr = nc.tensor.matmul, nc.tensor.transpose

                    def ctx_turn(c):
                        if c == 0:
                            wait_for(pe, s.ln_ctx, 10 * (t + 1))
                        else:
                            apart(pe)
                        for k in range(NCH):
                            ins = tr(dst[0:CW[c], k * P:(k + 1) * P], CNorm[j][:, k, c * P:c * P + CW[c]], ident[:, :])
                        return ins

                    def x_turn():
                        wait_for(pe, s.ln_x, 4 * NORMS[L] * (t + 1))
                        src = XN2[j] if NORMS[L] == 2 else XN[j]
                        for c in range(2):
                            ins = tr(dst[:, c * T:(c + 1) * T], src[0:T, c * P:(c + 1) * P], ident[0:T, 0:T])
                        return ins

                    def rows(lhs, parts, w, n_out, m_out):
                        for c in range(2):
                            ins = mm(dst[0:m_out, 0:n_out], lhs(c), w[0:parts[c], c, 0:n_out], start=(c == 0), stop=(c == 1))
                        return ins

                    if L == 0:
                        if n in (0, 1):
                            ins = ctx_turn(n)
                        elif n == 2:
                            ins = x_turn()
                        elif n in (3, 4, 5):
                            wait_for(pe, s.copied, done + 2)
                            k = n - 3
                            ins = rows(lambda c: CT[j][0:CW[c], c, k * P:(k + 1) * P], CW, wkv0, 512, P)
                        elif n == 6:
                            wait_for(pe, s.copied, done + 3)
                            ins = rows(lambda c: XT[j][:, c, :], (P, P), wlkv0, 512, P)
                        elif n == 7:
                            ins = rows(lambda c: XT[j][:, c, 0:T], (P, P), wq[0], D, T)
                        elif n in (8, 9):
                            m = n - 8
                            wait_for(pe, s.qk_rms, 4 * (t + 1))
                            for k in range(4):
                                ins = tr(dst[:, k * P:(k + 1) * P], QK[j][:, k, m * P:(m + 1) * P], ident[:, :])
                        else:
                            for m in range(2):
                                ins = tr(dst[:, m * T:(m + 1) * T], QK[j][0:T, 4, m * P:(m + 1) * P], ident[0:T, 0:T])
                    else:
                        kind = n
                        if L == 3:
                            kind = n - 2
                            if n in (0, 1):
                                ins = ctx_turn(n)
                        first = done + (3 if L == 3 else 1)
                        if kind == 0:
                            ins = x_turn()
                        elif kind == 1:
                            wait_for(pe, s.copied, first)
                            for m in range(MQ):
                                for c in range(2):
                                    ins = mm(dst[:, m * T:(m + 1) * T], wq[L][:, c, m * P:(m + 1) * P], XT[j][:, c, 0:T],
                                             start=(c == 0), stop=(c == 1))
                        elif 2 <= kind < 2 + MQ:
                            m = kind - 2
                            if m == 0 and L != 3:
                                wait_for(pe, (s.ctx_in0, s.ctx_in1)[j], 32 * (t // 2 + 1))
                            for c in range(2):
                                ins = mm(dst[:, 0:NC], wk[L][0:CW[c], c, m * P:(m + 1) * P], CT[j][0:CW[c], c, 0:NC],
                                         start=(c == 0), stop=(c == 1))
                        elif kind >= 2 + MQ:
                            k = kind - 2 - MQ
                            ins = rows(lambda c: CT[j][0:CW[c], c, k * P:(k + 1) * P], CW, wv[L], VN, P)
                    ins.then_inc(s.proj.sem, 1)

                def scores(t, j, h):
                    n = H * t + h
                    k = (H * j + h) % 2
                    wait_for(pe, s.exped, n - 1)
                    if h == 0:
                        wait_for(pe, s.copied, STEPS[L] * (t + 1))
                    if H == 1:
                        for m in range(2):
                            ins = nc.tensor.matmul(S_bank[k][0:T, 0:NK], QT[j][:, m, :], kt(L, j)[:, m, 0:NK],
                                                   start=(m == 0), stop=(m == 1))
                    else:
                        m, b = h // 2, W * (h % 2)
                        ins = nc.tensor.matmul(S_bank[k][0:T, 0:NK], QT[j][b:b + W, m, :], kt(L, j)[b:b + W, m, 0:NK],
                                               start=True, stop=True)
                    ins.then_inc(s.scores.sem, 1)

                def probs_turn(t, j, h):
                    n = H * t + h
                    k = (H * j + h) % 2
                    wait_for(pe, s.exped, n + 1)
                    wait_for(pe, s.probs_copied, n - 1)
                    for c in range(CH):
                        ins = nc.tensor.transpose(PT_bank[k][:, c * T:(c + 1) * T], PR[k][0:T, c, :], ident[0:T, 0:T])
                    ins.then_inc(s.probs_turned.sem, 1)

                def weigh(t, j, h):
                    n = H * t + h
                    k = (H * j + h) % 2
                    wait_for(pe, s.probs_copied, n + 1)
                    if h == 0:
                        wait_for(pe, s.o_scaled, 2 * t)
                    for c in range(CH):
                        ins = nc.tensor.matmul(O_bank[0:T, h * W:(h + 1) * W], PT[k][:, c, :],
                                               vv(L, j)[:, c, h * W:(h + 1) * W], start=(c == 0), stop=(c == CH - 1))
                    ins.then_inc(s.pv.sem, 1)

                def o_turn(t, j):
                    wait_for(pe, s.o_scaled, 2 * (t + 1))
                    wait_for(pe, s.resid, 2 * t)
                    for m in range(H * W // P):
                        ins = nc.tensor.transpose(R_bank[:, m * T:(m + 1) * T], O[0:T, m * P:(m + 1) * P], ident[0:T, 0:T])
                    ins.then_inc(s.o_turned.sem, 1)

                def project(t, j):
                    wait_for(pe, s.o_copied, t + 1)
                    M = H * W // P
                    for m in range(M):
                        ins = nc.tensor.matmul(R_bank[0:T, 0:D], OT[:, m, :], wo[L][:, m, :], start=(m == 0), stop=(m == M - 1))
                    ins.then_inc(s.out.sem, 1)

                def prepare(t, j):
                    for n in range(STEPS[L]):
                        step(t, j, n)

                def attend(t, j, more):
                    started = not (isinstance(t, int) and t == 0)
                    scores(t, j, 0)
                    if H > 1:
                        scores(t, j, 1)
                    if started:
                        o_turn(t - 1, 1 - j)
                    for h in range(H):
                        probs_turn(t, j, h)
                        if h + 2 < H:
                            scores(t, j, h + 2)
                        if h == 0 and started:
                            project(t - 1, 1 - j)
                        if more:
                            for n in GROUPS[L][h]:
                                step(t + 1, 1 - j, n)
                        weigh(t, j, h)

                def finish(t, j):
                    o_turn(t, j)
                    project(t, j)

                pipelined(pe, prepare, attend, finish)
                end(pe)


            def x_turn(s, t, j):
                pe.wait_ge(s.ln_x, 4 * (t + 1))
                wait_count(pe, s.x_copied, t if s is not mx0 else 2 * t)
                for c in range(2):
                    ins = nc.tensor.transpose(bank[0][:, c * T:(c + 1) * T], FX[j][0:T, c * P:(c + 1) * P], ident[0:T, 0:T])
                ins.then_inc(s.x_turned, 1)

            def logits(s, w, n_route, t, j):
                pe.wait_ge(s.x_copied, t + 1 if s is not mx0 else 2 * t + 1)
                wait_count(pe, s.route, n_route * (t - 1) + 1)
                for c in range(2):
                    ins = nc.tensor.matmul(bank[1][0:T, 0:8], FXT[j][:, c, :], w[:, c, :], start=(c == 0), stop=(c == 1))
                ins.then_inc(s.logits, 1)

            def dense_experts():
                s = mx0
                begin(pe, 1)
                pe.wait_ge(loaded[1], 16 * n_loads[1])

                def batch(t, j):
                    x_turn(s, t, j)
                    wait_count(pe, s.b2_added, t)
                    logits(s, ew0, 7, t, j)
                    pe.wait_ge(s.route, 7 * t + 6)
                    nc.tensor.transpose(bank[1][0:E0, 128:128 + T], WF[j][0:T, 0:8], ident[0:T, 0:T]).then_inc(s.oh_turned, 1)
                    pe.wait_ge(s.oh_copied, t + 1)
                    nc.tensor.matmul(bank[1][0:T, 256:512], OHT[j][0:E0, :], eb2[:, :], start=True, stop=True
                                     ).then_inc(s.b2_row, 1)

                in_turn(pe, batch)
                pe.wait_ge(s.x_copied, 2 * B)
                pe.wait_ge(s.b2_added, B)

                def tokens(e, j, q):
                    if q_is_first(q):
                        pe.wait_ge((s.w_in0, s.w_in1)[j], 48 * (e // 2 + 1))
                    for f in range(HID0 // P):
                        n = 8 * (4 * e + q) + f
                        for half, to, sig, used in ((1, 2, s.gate, s.sigmoid), (0, 4, s.value, s.hidden)):
                            wait_count(pe, used, n - 1)
                            for c in range(2):
                                col = half * HID0 + f * P
                                ins = nc.tensor.matmul(bank[to + f % 2][:, 0:QT_TOK], W1[j][:, c, col:col + P],
                                                       XA[:, c, bass.ds(QT_TOK * q, QT_TOK)], start=(c == 0), stop=(c == 1))
                            ins.then_inc(sig, 1)
                    pe.wait_ge(s.hidden, 8 * (4 * e + q + 1))
                    for k in range(4):
                        m = 4 * (4 * e + q) + k
                        wait_count(pe, s.resid, m - 1)
                        for f in range(HID0 // P):
                            ins = nc.tensor.matmul(bank[6 + k % 2][0:T, 0:D], AC[:, f, k * T:(k + 1) * T], W2[j][:, f, :],
                                                   start=(f == 0), stop=(f == HID0 // P - 1))
                        ins.then_inc(s.out, 1)

                for e in range(E0):
                    tokens(e, e % 2, 0)
                    with pe.Fori(1, 4) as q:
                        tokens(e, e % 2, q)
                end(pe)

            def squared_experts():
                s = mx1
                begin(pe, 3)
                pe.wait_ge(loaded[3], 16 * n_loads[3])

                def hidden(t, j, g):
                    wait_count(pe, s.relu, 3 * (t - 1) + g + 1)
                    for c in range(2):
                        ins = nc.tensor.matmul(bank[2 + g][0:T, 0:3 * HID1], FXT[j][:, c, :],
                                               up1[:, c, 3 * HID1 * g:3 * HID1 * (g + 1)], start=(c == 0), stop=(c == 1))
                    ins.then_inc(s.hidden, 1)

                def turn(t, j, g):
                    pe.wait_ge(s.masked, 3 * t + g + 1)
                    wait_count(pe, s.h_copied, 3 * t + g - 1)
                    for k in range(3):
                        ins = nc.tensor.transpose(bank[5 + (3 * j + g) % 2][:, k * T:(k + 1) * T],
                                                  SQ[g][0:T, k * HID1:(k + 1) * HID1], ident[0:T, 0:T])
                    ins.then_inc(s.h_turned, 1)

                def down(t, j, g):
                    pe.wait_ge(s.h_copied, 3 * t + g + 1)
                    if g == 0:
                        wait_count(pe, s.resid, t)
                    for k in range(3):
                        ins = nc.tensor.matmul(bank[7][0:T, 0:D], HT[g][:, k, :], down1[:, 3 * g + k, :],
                                               start=(g == 0 and k == 0), stop=(g == 2 and k == 2))
                    if g == 2:
                        ins.then_inc(s.out, 1)

                def prepare(t, j):
                    x_turn(s, t, j)
                    logits(s, ew1, 9, t, j)
                    for g in range(3):
                        hidden(t, j, g)

                def attend(t, j, more):
                    turn(t, j, 0)
                    turn(t, j, 1)
                    down(t, j, 0)
                    if more:
                        x_turn(s, t + 1, 1 - j)
                    down(t, j, 1)
                    turn(t, j, 2)
                    if more:
                        logits(s, ew1, 9, t + 1, 1 - j)
                        hidden(t + 1, 1 - j, 0)
                    down(t, j, 2)
                    if more:
                        hidden(t + 1, 1 - j, 1)
                        hidden(t + 1, 1 - j, 2)

                pipelined(pe, prepare, attend, lambda t, j: None)
                end(pe)

            def linear_experts():
                s = mx2
                begin(pe, 5)
                pe.wait_ge(loaded[5], 16 * n_loads[5])

                def experts(t, j, g):
                    wait_count(pe, s.combined, 8 * (t - 1) + 2 * g + 2)
                    for c in range(2):
                        ins = nc.tensor.matmul(bank[2 + g][0:T, :], FXT[j][:, c, :],
                                               lin2[:, c, 2 * g:2 * g + 2, :].rearrange("p e n -> p (e n)"),
                                               start=(c == 0), stop=(c == 1))
                    ins.then_inc(s.out, 1)

                def prepare(t, j):
                    x_turn(s, t, j)
                    logits(s, ew2, 11, t, j)

                def attend(t, j, more):
                    for g in range(4):
                        experts(t, j, g)
                        if g == 1 and more:
                            x_turn(s, t + 1, 1 - j)
                    if more:
                        logits(s, ew2, 11, t + 1, 1 - j)

                pipelined(pe, prepare, attend, lambda t, j: None)
                end(pe)

            def slot_mixer():
                s = mx3
                begin(pe, 7)
                pe.wait_ge(s.w_in, 16 * len(slot_loads))
                mm, tr = nc.tensor.matmul, nc.tensor.transpose
                for c in range(2):
                    mm(bank[4][:, :], SIT[:, c, :], SWhh[:, c, 0:512], start=(c == 0), stop=(c == 1))
                for c in range(2):
                    mm(bank[5][:, 0:D], SIT[:, c, :], SWhh[:, c, 512:768], start=(c == 0), stop=(c == 1))
                pe.wait_ge(s.consts, 4)
                for c in range(2):
                    ins = mm(bank[6][:, 0:1], SW1[:, 2 + c, :], MEAN[:, c, :], start=(c == 0), stop=(c == 1))
                ins.then_inc(s.const_sums, 1)

                def prepare(t, j):
                    x_turn(s, t, j)

                def attend(t, j, more):
                    pe.wait_ge(s.x_copied, t + 1)
                    wait_count(pe, s.gelu, t - 1)
                    for c in range(2):
                        ins = mm(bank[1 + j][:, 0:T], SW1[:, c, :], FXT[j][:, c, :], start=(c == 0), stop=(c == 1))
                    ins.then_inc(s.hidden, 1)
                    if more:
                        prepare(t + 1, 1 - j)
                    pe.wait_ge(s.gelu, t + 1)
                    wait_count(pe, s.picked, 8 * (t - 1) + 2)
                    mm(bank[3][0:T, 0:NS], HG[j][:, :], SW2[:, :], start=True, stop=True).then_inc(s.logits, 1)

                pipelined(pe, prepare, attend, lambda t, j: None)

                def turn(src, k):
                    for c in range(2):
                        ins = tr(bank[4 * k][:, c * P:(c + 1) * P], src[:, c * P:(c + 1) * P], ident[:, :])
                    return ins

                def product(dst, lhs, w, lo, hi):
                    for c in range(2):
                        ins = mm(dst, lhs[:, c, :], w[:, c, lo:hi], start=(c == 0), stop=(c == 1))
                    return ins

                def sums(u, k):
                    pe.wait_ge(s.alpha, 3 * (u + 1))
                    for m in range(2):
                        ins = mm(bank[4 * k][:, 0:D + 1], pair[k].ALP[0:T, m, :],
                                 XS[0:T, bass.ds(2 * u + m, 1), :].rearrange("p o d -> p (o d)"), start=(m == 0), stop=(m == 1))
                    ins.then_inc(s.sums, 1)

                def alpha_turn(u, k):
                    for m in range(2):
                        ins = mm(bank[4 * k + 1][:, 0:T], pair[k].ALP[0:T, m, :], ident[0:T, 0:T], start=(m == 0), stop=(m == 1))
                    ins.then_inc(s.alpha_turned, 1)

                def pooled_turn(u, k):
                    pe.wait_ge(s.pooled, 3 * (u + 1))
                    turn(pair[k].SU, k).then_inc(s.pooled_turned, 1)

                def gru_in(u, k):
                    pe.wait_ge(s.pooled_copied, u + 1)
                    product(bank[4 * k + 2][:, :], pair[k].SUT, SWih, 0, 512)
                    product(bank[4 * k + 3][:, 0:D], pair[k].SUT, SWih, 512, 768).then_inc(s.gru_in, 1)

                def s_turn(u, k):
                    pe.wait_ge(s.slots_new, 3 * (u + 1))
                    turn(pair[k].S, k).then_inc(s.s_turned, 1)

                def qkv(u, k):
                    pe.wait_ge(s.s_copied, u + 1)
                    pe.wait_ge(s.alpha_copied, u + 1)
                    for m, w in ((0, SWq), (1, SWk)):
                        for c in range(2):
                            mm(bank[4 * k + 1][0:DQ, m * P:(m + 1) * P], w[:, c, :], pair[k].ST[:, c, :],
                               start=(c == 0), stop=(c == 1))
                    product(bank[4 * k + 3][:, 0:D], pair[k].ST, SWv, 0, D).then_inc(s.qkv, 1)

                def attn(u, k):
                    pe.wait_ge(s.qk_copied, u + 1)
                    mm(bank[4 * k + 2][:, 0:P], pair[k].QS[0:DQ, 0, :], pair[k].QS[0:DQ, 1, :], start=True, stop=True
                       ).then_inc(s.attn, 1)

                def attn_turn(u, k):
                    pe.wait_ge(s.attn_exped, u + 1)
                    pe.wait_ge(s.v_done, u + 1)
                    tr(bank[4 * k + 3][:, 0:P], pair[k].AT[:, :], ident[:, :]).then_inc(s.attn_turned, 1)

                def comm(u, k):
                    pe.wait_ge(s.attn_copied, 2 * (u + 1))
                    mm(bank[4 * k + 2][:, 0:D], pair[k].ATT[:, :], pair[k].VS[:, :], start=True, stop=True).then_inc(s.comm, 1)

                def y_turn(u, k):
                    pe.wait_ge(s.y_normed, u + 1)
                    turn(pair[k].Y, k).then_inc(s.y_turned, 1)

                def values(u, k):
                    pe.wait_ge(s.y_copied, u + 1)
                    product(bank[4 * k + 1][:, 0:D], pair[k].YT, SWvp, 0, D).then_inc(s.values, 1)

                def mixed(u, k):
                    pe.wait_ge(s.values_done, u + 1)
                    for m in range(2):
                        for c in range(2):
                            ins = mm(bank[4 * k + 3 * (1 - m)][:, c * T:(c + 1) * T],
                                     pair[k].SV[NS * m:NS * (m + 1), c * P:(c + 1) * P], pair[k].ALT[NS * m:NS * (m + 1), :],
                                     start=True, stop=True)
                    ins.then_inc(s.mixed, 1)

                def out_rows(u, k):
                    pe.wait_ge(s.mixed_copied, u + 1)
                    for m in range(2):
                        for c in range(2):
                            ins = mm(bank[4 * k + 2][0:T, m * D:(m + 1) * D], pair[k].MT[:, 2 * m + c, :], SWo[:, c, :],
                                     start=(c == 0), stop=(c == 1))
                    ins.then_inc(s.out, 1)

                with pe.Fori(0, B // 4) as i:
                    for stage in (sums, alpha_turn, pooled_turn, gru_in, s_turn, qkv, attn, attn_turn, comm, y_turn, values,
                                  mixed, out_rows):
                        stage(2 * i, 0)
                        stage(2 * i + 1, 1)
                end(pe)

            for p in phases:
                if p % 2 == 0:
                    attention(p // 2)
                else:
                    (dense_experts, squared_experts, linear_experts, slot_mixer)[p // 2]()


_OUTS = [((B, T, D), 'float32')]


def layout(inputs):
    import numpy as _np

    v = {k: _np.asarray(x) for k, x in inputs.items()}

    def column(x):
        return _np.pad(x, (0, -len(x) % P)).reshape(-1, P).T

    r = {"x": v["x"], "ctx": v["ctx_768"], "ctxT": v["ctx_768"].transpose(0, 2, 1), "mask": v["mask_BxS2_bk0"],
         "gates": _np.concatenate([v["g_xattn"], v["g_ffn"]]), "ident": _np.eye(P, dtype=_np.float32),
         "L0_WqT": v["L0_xattn_Wq"].T, "L0_WkvT": v["L0_xattn_Wkv"].T, "L0_WlkvT": v["L0_xattn_Wlkv"].T,
         "L0_WoT": v["L0_xattn_Wo"].T, "L2_WoT": v["L2_xattn_Wo"].T,
         "L0_qn_g2": column(_np.tile(v["L0_xattn_qn_g"], 2)), "L0_kn_g2": column(_np.tile(v["L0_xattn_kn_g"], 2))}
    for n in ("Wq", "Wk", "Wv"):
        r[f"L1_{n}"] = v[f"L1_xattn_{n}"]
        r[f"L2_{n}T"] = v[f"L2_xattn_{n}"].T
        r[f"L3_{n}"] = v[f"L3_xattn_{n}"]
    r["iota"] = _np.arange(8, dtype=_np.float32)
    for n in ("router_w", "router_b", "b2", "w1", "w2"):
        r[f"F0_{n}"] = v[f"L0_ffn_{n}"]
    r["F0_b1c"] = v["L0_ffn_b1"].reshape(E0, -1, P).transpose(2, 0, 1)
    r["F1_Wr"] = v["L1_ffn_Wr"]
    r["F1_up"] = _np.concatenate([v["L1_ffn_Ws1"][None], v["L1_ffn_W1"]]).transpose(1, 0, 2).reshape(D, -1)
    r["F1_down"] = _np.concatenate([v["L1_ffn_Ws2"][None], v["L1_ffn_W2"]]).reshape(-1, D)
    s = {k[7:]: x for k, x in v.items() if k.startswith("L3_ffn_")}
    for n in ("w1", "w2", "wq", "wk", "wv", "wvp", "wo", "b2", "bih", "bhh", "bv", "bvp", "bo", "tau"):
        r[f"F3_{n}"] = s[n]
    for n in ("b1", "bq", "bk", "ln_g", "ln_b"):
        r[f"F3_{n}"] = column(s[n])
    r["F3_WihT"], r["F3_WhhT"] = s["Wih"].T, s["Whh"].T
    r["F3_slot_init2"] = _np.tile(s["slot_init"], (2, 1))
    r["F3_slot_initT2"] = _np.tile(s["slot_init"].T, (1, 2))
    r["F3_apart"] = _np.kron(1 - _np.eye(2), _np.ones((NS, NS))).astype(_np.float32) * _np.float32(FAR)
    r["F2_gateT"], r["F2_weight"] = v["L2_ffn_gate_w"].T, v["L2_ffn_weight"]
    r["L1_Wo"], r["L3_Wo"] = v["L1_xattn_Wo"], v["L3_xattn_Wo"]
    for L in range(4):
        r[f"L{L}_bo"] = v[f"L{L}_xattn_bo"]
    for n in ("ln_x_g", "ln_x_b", "ln_l_g", "ln_l_b"):
        r[f"L0_{n}"] = column(v[f"L0_xattn_{n}"])
    for n in ("ln1_g", "ln1_b", "ln2_g", "ln2_b", "bq", "bk"):
        r[f"L3_{n}"] = column(v[f"L3_xattn_{n}"])
    r["L3_bv"] = v["L3_xattn_bv"]
    return r


def kernel(**inputs):
    import numpy as _np
    import concourse.bacc as _bacc
    from concourse import mybir as _mybir
    from concourse.bass_utils import run_bass_kernel_spmd as _run

    nc = _bacc.Bacc("TRN2", target_bir_lowering=False, num_devices=1)
    arrays, args = {}, {}
    for name, x in layout(inputs).items():
        x = _np.ascontiguousarray(x)
        arrays[f"in_{name}"] = x
        args[name] = nc.dram_tensor(f"in_{name}", x.shape, _mybir.dt.from_np(x.dtype), kind="ExternalInput").ap()
    out = nc.dram_tensor("out_0_dram", _OUTS[0][0], _mybir.dt.float32, kind="ExternalOutput").ap()
    flamingo_kernel(nc, args, out)
    r = _run(nc, [arrays], core_ids=[0])
    return r.results[0]["out_0_dram"]
```

```python
from contextlib import ExitStack

import concourse.bass as bass
from concourse import mybir

ALU = mybir.AluOpType
ACT = mybir.ActivationFunctionType
F32 = mybir.dt.float32
U8 = mybir.dt.uint8
U32 = mybir.dt.uint32
I32 = mybir.dt.int32
AXX = mybir.AxisListType.X

B, T, D = 16, 100, 256
NC, DC = 361, 192
P = 128
NCH = 3
LAST = NC - (NCH - 1) * P
NKP = NCH * P
CW = (P, DC - P)
LN_EPS = 1e-5
FAR = -1.0e30

HEADS = (4, 8, 4, 1)
HWID = (64, 64, 64, 256)
KEYS = (NKP + P, NC, NC, NC)
CHUNKS = (NCH + 1, NCH, NCH, NCH)
GROUPS = (
    ((0, 1, 2), (3, 4, 5), (6, 7), (8, 9, 10)),
    ((0,), (1, 2), (3,), (4,), (5,), (6,), (7,), (8,)),
    ((0, 1), (2, 3), (4, 5), (6,)),
    ((0, 1, 2, 3, 4, 5, 6, 7, 8),),
)
STEPS = tuple(sum(len(g) for g in gs) for gs in GROUPS)
NORMS = (2, 1, 1, 2)
MAXES = (2, 1, 1, 1)
E0, HID0 = 8, 1024
TILES0 = (B * T - E0) // P + E0
STEPS0 = -(-B * T // P)
E1, HID1 = 8, 128
E2 = 8
NS, TOPS, DQ = 64, 8, 64
BUILT = (0, 1, 2, 3, 4, 5, 6, 7)
PLACED = 29
WORK = 24600


class Named:

    def __init__(self, **by_name):
        self.by_name = by_name

    def __getattr__(self, name):
        return self.by_name[name]


def signals(nc, ctx, phase, names):
    return Named(**{n: ctx.enter_context(nc.semaphore(f"{phase}_{n}")) for n in names.split()})


class Signal:

    def __init__(self, sem, before):
        self.sem, self.before = sem, before


def raised_by_attention(L):
    H, own_ctx = HEADS[L], L in (0, 3)
    per_batch = {"ln_ctx": 10 * own_ctx, "rstd_ctx": own_ctx, "ln_x": 4 * NORMS[L], "rstd_x": NORMS[L],
                 "proj": STEPS[L], "copied": STEPS[L], "mask_row": L == 0, "qk_rms": 4 * (L == 0), "rqk": L == 0,
                 "scores": H, "maxed": MAXES[L] * H, "exped": H, "probs_turned": H, "probs_copied": H, "pv": H,
                 "o_scaled": 2, "o_turned": 1, "o_copied": 1, "out": 1, "resid": 2}
    counts = {n: B * int(c) for n, c in per_batch.items()}
    counts.update(ctx_in0=16 * B, ctx_in1=16 * B, mask_in0=8 * B * (L == 0), mask_in1=8 * B * (L == 0), cleared=1)
    return counts


def wait_for(eng, signal, count):
    if isinstance(count, int) and count <= 0:
        return
    eng.wait_ge(signal.sem, signal.before + count)


def apart(eng):
    eng.nop(nofuse=True)


def wait_count(eng, sem, count):
    if isinstance(count, int) and count <= 0:
        return
    eng.wait_ge(sem, count)


def pipelined(eng, prepare, attend, finish, n=B):
    prepare(0, 0)
    attend(0, 0, True)
    attend(1, 1, True)
    with eng.Fori(1, n // 2 - 1) as i:
        attend(2 * i, 0, True)
        attend(2 * i + 1, 1, True)
    attend(n - 2, 0, True)
    attend(n - 1, 1, False)
    finish(n - 1, 1)


def in_turn(eng, one, n=B):
    one(0, 0)
    one(1, 1)
    with eng.Fori(1, n // 2) as i:
        one(2 * i, 0)
        one(2 * i + 1, 1)


def flamingo_kernel(nc, a, out, last_phase=99):
    ctx = ExitStack()
    with ctx:
        def sb(name, shape, dt=F32):
            return ctx.enter_context(nc.sbuf_tensor(name, shape, dt))

        def ps(name, shape):
            return ctx.enter_context(nc.psum_tensor(name, shape, F32))

        X = sb("X", [P, B, D])
        ident = sb("ident", [P, P])
        gates = sb("gates", [P, 8])
        neg_half = sb("neg_half", [P, 32])
        work = sb("work", [P, WORK])
        bank = [ps(f"bank{i}", [P, 512]) for i in range(8)]

        class Area:

            def __init__(self):
                self.at = 0

            def take(self, *shape, dt=F32):
                n = 1
                for s in shape:
                    n *= s
                words = n if dt in (F32, U32, I32) else (n + 3) // 4
                v = work[:, self.at:self.at + words]
                self.at += words
                assert self.at <= WORK, self.at
                if dt != F32:
                    v = v.bitcast(dt)[:, 0:n]
                names = " ".join("abcd"[:len(shape)])
                sizes = {"abcd"[i]: s for i, s in enumerate(shape)}
                return v.rearrange(f"p ({names}) -> p {names}", **sizes)

        loads = []

        def resident(phase, name, chunks, parts=P):
            src = a[name]
            n = src.shape[-1]
            w = sb(name, [P, chunks, n])
            full = src.shape[0] // P
            if full:
                loads.append((phase, w[:, 0:full, :], src[0:full * P, :].rearrange("(c p) n -> p c n", p=P)))
            if src.shape[0] % P:
                loads.append((phase, w[0:src.shape[0] % P, full, :], src[full * P:, :]))
            return w

        def column(phase, name, chunks=1):
            w = sb(name, [P, chunks])
            loads.append((phase, w[:, :], a[name]))
            return w

        def row(phase, name):
            n = a[name].shape[0]
            w = sb(name, [P, n])
            loads.append((phase, w[:, :], a[name].rearrange("(o n) -> o n", o=1).broadcast_to([P, n])))
            return w

        wq = [resident(2 * L, n, 2) for L, n in enumerate(("L0_WqT", "L1_Wq", "L2_WqT", "L3_Wq"))]
        wk = [None] + [resident(2 * L, n, 2) for L, n in ((1, "L1_Wk"), (2, "L2_WkT"), (3, "L3_Wk"))]
        wv = [None] + [resident(2 * L, n, 2) for L, n in ((1, "L1_Wv"), (2, "L2_WvT"), (3, "L3_Wv"))]
        wkv0 = resident(0, "L0_WkvT", 2)
        wlkv0 = resident(0, "L0_WlkvT", 2)
        wo = [resident(2 * L, n, 4 if L == 1 else 2) for L, n in enumerate(("L0_WoT", "L1_Wo", "L2_WoT", "L3_Wo"))]
        bo = [row(2 * L, f"L{L}_bo") for L in range(4)]
        ctx_gain = {0: column(0, "L0_ln_x_g", 2), 3: column(6, "L3_ln2_g", 2)}
        ctx_bias = {0: column(0, "L0_ln_x_b", 2), 3: column(6, "L3_ln2_b", 2)}
        x_gain = {0: column(0, "L0_ln_l_g", 2), 3: column(6, "L3_ln1_g", 2)}
        x_bias = {0: column(0, "L0_ln_l_b", 2), 3: column(6, "L3_ln1_b", 2)}
        q_gain = column(0, "L0_qn_g2")
        k_gain = column(0, "L0_kn_g2")
        bq3, bk3, bv3 = column(6, "L3_bq", 2), column(6, "L3_bk", 2), row(6, "L3_bv")
        bq3s = sb("bq3_scaled", [P, 2])
        qg0s = sb("q_gain_scaled", [P, 1])

        earlier = resident(1, "earlier", 1)
        tile_starts = row(1, "tile_starts")
        tile_iota = row(1, "tile_iota")
        ones = sb("ones", [P, P])
        zeros = sb("zeros", [P, D])
        iota = row(1, "iota")
        ew0 = resident(1, "F0_router_w", 2)
        eb0 = row(1, "F0_router_b")
        ew1 = resident(3, "F1_Wr", 2)
        up1 = resident(3, "F1_up", 2)
        down1 = resident(3, "F1_down", 1 + E1)
        ew2 = resident(5, "F2_gateT", 2)
        lin2 = sb("F2_weight", [P, 2, E2, D])
        for c in range(2):
            loads.append((5, lin2[:, c, :, :], a["F2_weight"][:, c * P:(c + 1) * P, :].rearrange("e p n -> p e n")))

        start = signals(nc, ctx, "start", "x_loaded consts gates gates_done neg_half scaled zeros")
        loaded = [ctx.enter_context(nc.semaphore(f"weights_loaded_{p}")) for p in range(8)]
        n_loads = [0] * 8
        for p, _, _ in loads:
            n_loads[p] += 1
        ended = ctx.enter_context(nc.semaphore("phase_ended"))
        stored = ctx.enter_context(nc.semaphore("stored"))
        shared = signals(nc, ctx, "attn", " ".join(raised_by_attention(0)))
        at = []
        for L in range(4):
            before = {n: sum(raised_by_attention(k)[n] for k in range(L) if 2 * k in BUILT) for n in raised_by_attention(0)}
            at.append(Named(**{n: Signal(sem, before[n]) for n, sem in shared.by_name.items()}))
        mx0 = signals(nc, ctx, "routed", "ln_x rstd_x x_turned x_copied logits route "
                      "xr_copied ranks places zeroed scattered rows_in0 rows_in1 w1_in0 w1_in1 w2_in0 w2_in1 rows_turned rows_copied value gate sigmoid hidden out "
                      "y_copied y_stored0 y_stored1 gathered resid")
        mx1 = signals(nc, ctx, "squared", "ln_x rstd_x x_turned x_copied logits route exped ones hidden relu squared masked "
                      "h_turned h_copied out resid")
        mx2 = signals(nc, ctx, "linear", "ln_x rstd_x x_turned x_copied logits route exped out combined resid")
        mx3 = signals(nc, ctx, "slots", "w_in consts const_sums ln_x rstd_x x_turned x_copied hidden gelu logits picked "
                      "exped alpha sums alpha_turned alpha_copied pooled pooled_turned pooled_copied gru_in rz_in rz_tanh "
                      "rz_done n_tanh slots_new s_turned s_copied qkv qk_copied v_done attn masked attn_exped attn_turned "
                      "attn_copied comm y_stats rstd_y y_normed y_turned y_copied values values_done mixed mixed_copied "
                      "out resid")

        area = Area()
        C = [area.take(NCH, DC) for _ in range(2)]
        CNorm = [area.take(NCH, DC) for _ in range(2)]
        CT = [area.take(2, NKP) for _ in range(2)]
        XN = [area.take(D) for _ in range(2)]
        XN2 = [area.take(D) for _ in range(2)]
        XT = [area.take(2, P) for _ in range(2)]
        QK = [area.take(5, D) for _ in range(2)]
        QKsq = area.take(5, D)
        QT = [area.take(4, T) for _ in range(2)]
        KT = [area.take(2048) for _ in range(2)]
        V = [area.take(2048) for _ in range(2)]
        PR = [area.take(4, P) for _ in range(2)]
        PT = [area.take(4, T) for _ in range(2)]
        O = area.take(512)
        OT = area.take(4, T)
        RO = area.take(D)
        M8 = [area.take(NC, dt=U8) for _ in range(2)]
        MR = [area.take(4, P) for _ in range(2)]
        st6 = [area.take(4, 6) for _ in range(2)]
        mv = [area.take(4, 2) for _ in range(2)]
        rs = [area.take(4) for _ in range(2)]
        ss = [area.take(20) for _ in range(2)]
        rr = [area.take(20) for _ in range(2)]
        nmax = [area.take(1) for _ in range(2)]
        pmax = [area.take(1) for _ in range(2)]
        rsum = [area.take(8) for _ in range(2)]
        rinv = area.take(8)
        S_bank = (bank[0], bank[1])
        PT_bank = (bank[2], bank[3])
        O_bank = bank[4]
        R_bank = bank[5]
        J_bank = (bank[6], bank[7])

        area = Area()
        FX = [area.take(D) for _ in range(2)]
        FXT = [area.take(2, T) for _ in range(2)]
        Fst6, Fmv, Frs = area.take(B, 6), area.take(B, 2), area.take(B)
        LG = [area.take(8) for _ in range(2)]
        V8 = [area.take(8) for _ in range(2)]
        I8 = [area.take(8, dt=U32) for _ in range(2)]
        IF = [area.take(2) for _ in range(2)]
        ED = [area.take(6) for _ in range(2)]
        WF = [area.take(9) for _ in range(2)]
        WB = [area.take(8) for _ in range(2)]
        mixture = area.at
        XR0 = area.take(B, D)
        OH = area.take(B, E0)
        LGA, V8A, I8A = area.take(B, E0), area.take(B, 8), area.take(B, 8, dt=U32)
        I1 = area.take(B)
        CUM = [area.take(B, E0) for _ in range(2)]
        PLACE = area.take(B, E0)
        GT = area.take(E0, STEPS0)
        NT = [area.take(E0) for _ in range(4)]
        TE = area.take(TILES0, E0)
        TX = [area.take(TILES0) for _ in range(2)]
        TXI = area.take(TILES0, dt=I32)
        PF = area.take(B)
        PI = area.take(B, dt=I32)
        W1 = [area.take(2, 2 * HID0) for _ in range(2)]
        W2 = [area.take(HID0 // P, D) for _ in range(2)]
        B1 = [area.take(2 * HID0 // P) for _ in range(2)]
        B2 = [area.take(D) for _ in range(2)]
        TR = [area.take(D) for _ in range(2)]
        TT = [area.take(2, P) for _ in range(2)]
        SG = [area.take(P) for _ in range(2)]
        AC = area.take(HID0 // P, P)
        YR = [area.take(D) for _ in range(2)]
        area.at = mixture
        RL = [area.take(3 * HID1) for _ in range(3)]
        SQ = [area.take(3 * HID1) for _ in range(3)]
        HT = [area.take(3, T) for _ in range(3)]
        area.at = mixture
        ACC = area.take(D)
        area.at = mixture
        XS = area.take(B, D + 1)
        ML = area.take(B, NS)
        SI, SIT, MEAN = area.take(D), area.take(2, P), area.take(2, 1)
        SW1, SW2 = area.take(4, P), area.take(NS)
        SWih, SWhh, Sbih, Sbhh = area.take(2, 3 * D), area.take(2, 3 * D), area.take(3 * D), area.take(3 * D)
        SWq, SWk, SWv, SWvp, SWo = area.take(2, DQ), area.take(2, DQ), area.take(2, D), area.take(2, D), area.take(2, D)
        Sb1, Sb2, Sbq, Sbk = area.take(1), area.take(NS), area.take(1), area.take(1)
        Sbv, Sbvp, Sbo, Sg, Sb = area.take(D), area.take(D), area.take(D), area.take(2), area.take(2)
        BD = area.take(P)
        TAU = area.take(2)
        GH = area.take(3 * D)
        HG = [area.take(T) for _ in range(2)]
        LS, LR, LV = [[area.take(n) for _ in range(2)] for n in (NS, NS, 8)]
        pair = [Named(AL=area.take(2, NS), ALP=area.take(2, P), AS=area.take(2), AR=area.take(2),
                                ALT=area.take(T), DEN=area.take(1), SU=area.take(D), SUT=area.take(2, P),
                                RZ=area.take(2 * D), NN=area.take(D), S=area.take(D), ST=area.take(2, P),
                                QS=area.take(2, P), VS=area.take(D), AT=area.take(P), AX=area.take(1), AU=area.take(1),
                                AI=area.take(1), ATT=area.take(P), Y=area.take(D), y6=area.take(6), ymv=area.take(2),
                                yrs=area.take(1), YT=area.take(2, P), SV=area.take(D), MT=area.take(4, T))
                for _ in range(2)]
        slot_loads = []
        for dst, n in ((SI, "slot_init2"), (Sb1, "b1"), (Sbq, "bq"), (Sbk, "bk"), (Sg, "ln_g"), (Sb, "ln_b"), (BD, "apart"),
                       (SW2, "w2")):
            slot_loads.append((dst, a["F3_" + n]))
        for dst, n in ((SIT, "slot_initT2"), (SW1, "w1"), (SWih, "WihT"), (SWhh, "WhhT"), (SWq, "wq"), (SWk, "wk"),
                       (SWv, "wv"), (SWvp, "wvp"), (SWo, "wo")):
            slot_loads.append((dst, a["F3_" + n].rearrange("(c p) n -> p c n", p=P)))
        for dst, n in ((Sbih, "bih"), (Sbhh, "bhh"), (Sb2, "b2"), (Sbv, "bv"), (Sbvp, "bvp"), (Sbo, "bo"), (TAU[:, 0:1], "tau")):
            src = a["F3_" + n]
            slot_loads.append((dst, src.rearrange("(o n) -> o n", o=1).broadcast_to([P, src.shape[0]])))

        def kt(L, j):
            m = 4 if L == 1 else 2
            return KT[j][:, 0:m * 512].rearrange("p (m n) -> p m n", m=m)

        def vv(L, j):
            n = 512 if L == 1 else 256
            return V[j][:, 0:CHUNKS[L] * n].rearrange("p (c n) -> p c n", n=n)

        phases = [p for p in BUILT if p <= last_phase]

        def begin(eng, p):
            if p != phases[0]:
                eng.wait_ge(ended, 4 * (phases.index(p) if p in phases else len(phases)))

        def end(eng):
            eng.drain().then_inc(ended, 1)

        sorted_x = nc.dram_tensor("sorted_x", (TILES0 * P, D), F32, kind="Internal").ap()
        sorted_y = nc.dram_tensor("sorted_y", (TILES0 * P, D), F32, kind="Internal").ap()

        block = ctx.enter_context(nc.Block())

        @block.sync
        def _(sp):
            sp.dma_start(X[0:T, :, :], a["x"].rearrange("b t d -> t b d")).then_inc(start.x_loaded, 16)
            sp.dma_start(ident[:, :], a["ident"]).then_inc(start.consts, 16)
            sp.dma_start(gates[:, :], a["gates"].rearrange("(o n) -> o n", o=1).broadcast_to([P, 8])).then_inc(start.gates, 16)
            for q, dst, src in loads:
                if q == 0:
                    sp.dma_start(dst, src).then_inc(loaded[q], 16)
            sp.wait_ge(start.zeros, 2)
            sp.dma_start(sorted_x.rearrange("(i p) d -> p i d", p=P),
                         zeros[:, :].rearrange("p (o d) -> p o d", o=1).broadcast_to([P, TILES0, D])).then_inc(mx0.zeroed, 16)

            def later_loads():
                for q, dst, src in loads:
                    if q > 0:
                        sp.dma_start(dst, src).then_inc(loaded[q], 16)

            def attention(L):
                s = at[L]
                begin(sp, 2 * L)
                if L in (0, 3):
                    wait_for(sp, s.cleared, 1)

                def load(t, j):
                    bt = bass.ds(t, 1)
                    if L in (0, 3):
                        wait_for(sp, s.ln_ctx, 10 * (t - 1))
                        apart(sp)
                        src = a["ctx"][bt, :, :]
                        sp.dma_start(C[j][:, 0:NCH - 1, :],
                                     src[:, 0:(NCH - 1) * P, :].rearrange("o (c p) d -> p (o c) d", p=P)
                                     ).then_inc((s.ctx_in0, s.ctx_in1)[j].sem, 16)
                        sp.dma_start(C[j][0:LAST, NCH - 1, :],
                                     src[:, (NCH - 1) * P:NC, :].rearrange("o p d -> p (o d)")
                                     ).then_inc((s.ctx_in0, s.ctx_in1)[j].sem, 16)
                        if L == 0:
                            wait_for(sp, s.mask_row, t - 1)
                            apart(sp)
                            sp.dma_start(M8[j][0:T, :], a["mask"][bt, :].broadcast_to([T, NC])
                                         ).then_inc((s.mask_in0, s.mask_in1)[j].sem, 16)
                    else:
                        wait_for(sp, s.proj, STEPS[L] * (t - 1))
                        apart(sp)
                        src = a["ctxT"][bt, :, :]
                        for c in range(2):
                            sp.dma_start(CT[j][0:CW[c], c, 0:NC],
                                         src[:, c * P:c * P + CW[c], :].rearrange("o p n -> p (o n)")
                                         ).then_inc((s.ctx_in0, s.ctx_in1)[j].sem, 16)

                load(0, 0)
                load(1, 1)
                if 2 * L == phases[0]:
                    later_loads()
                with sp.Fori(1, B // 2) as i:
                    load(2 * i, 0)
                    load(2 * i + 1, 1)


            def routed_experts():
                begin(sp, 1)
                if 1 == phases[0]:
                    later_loads()
                s = mx0

                sp.wait_ge(s.places, PLACED)

                def load(i, j):
                    e = sp.value_load(TXI[0:1, bass.ds(i, 1)], min_val=0, max_val=E0 - 1)
                    one = bass.ds(e, 1)
                    wait_count(sp, s.hidden, 8 * (i - 1))
                    apart(sp)
                    for c in range(2):
                        sp.dma_start(W1[j][:, c, :], a["F0_w1"][one, c * P:(c + 1) * P, :].rearrange("o p n -> p (o n)")
                                     ).then_inc((s.w1_in0, s.w1_in1)[j], 16)
                    sp.dma_start(B1[j][:, :], a["F0_b1c"][one, :, :].rearrange("o p n -> p (o n)")
                                 ).then_inc((s.w1_in0, s.w1_in1)[j], 16)
                    if isinstance(i, int) and i == 0:
                        sp.wait_ge(s.scattered, 16 * B)
                    sp.dma_start(TR[j][:, :], sorted_x[bass.ds(i * P, P), :]).then_inc((s.rows_in0, s.rows_in1)[j], 16)
                    wait_count(sp, s.y_copied, i - 1)
                    apart(sp)
                    sp.dma_start(W2[j][:, :, :], a["F0_w2"][one, :, :].rearrange("o (c p) n -> p (o c) n", p=P)
                                 ).then_inc((s.w2_in0, s.w2_in1)[j], 16)
                    sp.dma_start(B2[j][:, :], a["F0_b2"][one, :].broadcast_to([P, D])).then_inc((s.w2_in0, s.w2_in1)[j], 16)

                def store(i, j):
                    sp.wait_ge(s.y_copied, i + 1)
                    apart(sp)
                    sp.dma_start(sorted_y[bass.ds(i * P, P), :], YR[j][:, :]
                                 ).then_inc((s.y_stored0, s.y_stored1)[j], 16)

                load(0, 0)
                load(1, 1)
                with sp.Fori(1, TILES0 // 2) as i:
                    for j in range(2):
                        load(2 * i + j, j)
                        store(2 * i + j - 2, j)
                store(TILES0 - 2, 0)
                store(TILES0 - 1, 1)

            def squared_experts():
                begin(sp, 3)
                if 3 == phases[0]:
                    later_loads()

            def linear_experts():
                begin(sp, 5)
                if 5 == phases[0]:
                    later_loads()

            def slot_mixer():
                begin(sp, 7)
                if 7 == phases[0]:
                    later_loads()
                for dst, src in slot_loads:
                    sp.dma_start(dst, src).then_inc(mx3.w_in, 16)

            for p in phases:
                if p % 2 == 0:
                    attention(p // 2)
                else:
                    (routed_experts, squared_experts, linear_experts, slot_mixer)[p // 2]()
            begin(sp, None)
            for p in range(8):
                if n_loads[p]:
                    sp.wait_ge(loaded[p], 16 * n_loads[p])
            sp.dma_start(out.rearrange("b t d -> t b d"), X[0:T, :, :]).then_inc(stored, 16)
            sp.wait_ge(stored, 16)

        @block.gpsimd
        def _(pool):
            nc.gpsimd.memset(zeros[:, :], 0.0).then_inc(start.zeros, 1)
            nc.gpsimd.memset(ones[:, :], 1.0).then_inc(start.zeros, 1)
            nc.gpsimd.memset(neg_half[:, :], -0.5).then_inc(start.neg_half, 1)
            pool.wait_ge(start.neg_half, 1)

            def attention(L):
                s = at[L]
                begin(pool, 2 * L)
                def prepare(t, j):
                    def ln_ctx():
                        wait_for(pool, s.ln_ctx, 10 * t + 7)
                        nc.gpsimd.tensor_tensor(rs[j][:, 0:3], rs[j][:, 0:3], neg_half[:, 0:3], ALU.pow
                                                ).then_inc(s.rstd_ctx.sem, 1)

                    def ln_x(k):
                        wait_for(pool, s.ln_x, 4 * (NORMS[L] * t + k) + 3)
                        nc.gpsimd.tensor_tensor(rs[j][0:T, 3:4], rs[j][0:T, 3:4], neg_half[0:T, 0:1], ALU.pow
                                                ).then_inc(s.rstd_x.sem, 1)

                    if L in (0, 3):
                        ln_ctx()
                    for k in range(NORMS[L]):
                        ln_x(k)
                    if L == 0:
                        wait_for(pool, s.qk_rms, 4 * t + 3)
                        nc.gpsimd.tensor_tensor(rr[j][:, :], rr[j][:, :], neg_half[:, 0:20], ALU.pow
                                                ).then_inc(s.rqk.sem, 1)

                in_turn(pool, prepare)
                end(pool)


            def rstd_x(s, p, last=True):
                begin(pool, p)
                pool.wait_ge(s.ln_x, 2 * B + 1)
                nc.gpsimd.tensor_tensor(Frs[0:T, :], Frs[0:T, :], neg_half[0:T, 0:B], ALU.pow).then_inc(s.rstd_x, 1)
                if last:
                    end(pool)

            def routed_experts():
                s = mx0
                rstd_x(s, 1, last=False)
                pool.wait_ge(s.places, PLACED)
                pool.wait_ge(s.zeroed, 16)
                for t in range(B):
                    nc.gpsimd.indirect_dma_start(sorted_x, bass.IndirectOffsetOnAxis(PI[0:T, t:t + 1], 0), XR0[0:T, t, :],
                                                 None).then_inc(s.scattered, 16)
                pool.wait_ge(s.scattered, 16 * B)
                pool.wait_ge(s.y_stored0, 8 * TILES0)
                pool.wait_ge(s.y_stored1, 8 * TILES0)
                for t in range(B):
                    nc.gpsimd.indirect_dma_start(XR0[0:T, t, :], None, sorted_y,
                                                 bass.IndirectOffsetOnAxis(PI[0:T, t:t + 1], 0)).then_inc(s.gathered, 16)
                end(pool)

            def squared_experts():
                rstd_x(mx1, 3)

            def linear_experts():
                rstd_x(mx2, 5)

            def slot_mixer():
                s = mx3
                rstd_x(s, 7, last=False)

                def one(u, k):
                    pool.wait_ge(s.y_stats, 4 * (u + 1))
                    nc.gpsimd.tensor_tensor(pair[k].yrs[:, :], pair[k].yrs[:, :], neg_half[:, 0:1], ALU.pow
                                            ).then_inc(s.rstd_y, 1)

                with pool.Fori(0, B // 4) as i:
                    one(2 * i, 0)
                    one(2 * i + 1, 1)
                end(pool)

            for p in phases:
                if p % 2 == 0:
                    attention(p // 2)
                else:
                    (routed_experts, squared_experts, linear_experts, slot_mixer)[p // 2]()

        @block.scalar
        def _(act):
            act.wait_ge(start.gates, 16)
            nc.scalar.activation(gates[:, :], gates[:, :], ACT.Tanh).then_inc(start.gates_done, 1)
            act.wait_ge(loaded[0], 16 * n_loads[0])
            nc.scalar.mul(qg0s[:, :], q_gain[:, :], HWID[0] ** -0.5).then_inc(start.scaled, 1)
            act.wait_ge(start.scaled, 1)

            def attention(L):
                s = at[L]
                H, W, NK = HEADS[L], HWID[L], KEYS[L]
                scale = float(W) ** -0.5
                begin(act, 2 * L)
                wait_for(act, s.cleared, 1)
                if L == 3:
                    act.wait_ge(loaded[6], 16 * n_loads[6])
                    nc.scalar.mul(bq3s[:, :], bq3[:, :], scale).then_inc(start.scaled, 1)
                    act.wait_ge(start.scaled, 2)

                def step(t, j, n):
                    src = J_bank[(j * STEPS[L] + n) % 2]
                    wait_for(act, s.proj, STEPS[L] * t + n + 1)
                    kind = n
                    if L == 0:
                        if n in (0, 1):
                            m = CW[n]
                            ins = nc.scalar.activation(CT[j][0:m, n, :], src[0:m, 0:NKP], ACT.Identity,
                                                       bias=ctx_bias[0][0:m, n:n + 1], scale=ctx_gain[0][0:m, n:n + 1])
                        elif n == 2:
                            for c in range(2):
                                ins = nc.scalar.activation(XT[j][:, c, 0:T], src[:, c * T:(c + 1) * T], ACT.Identity,
                                                           bias=x_bias[0][:, c:c + 1], scale=x_gain[0][:, c:c + 1])
                        elif n in (3, 4, 5, 6):
                            nc.scalar.copy(QK[j][:, n - 3, :], src[:, 0:D])
                            ins = nc.scalar.copy(vv(0, j)[:, n - 3, :], src[:, D:2 * D])
                        elif n == 7:
                            ins = nc.scalar.copy(QK[j][0:T, 4, :], src[0:T, 0:D])
                        elif n in (8, 9):
                            ins = nc.scalar.mul(kt(0, j)[:, n - 8, :], src[:, :], k_gain[:, 0:1])
                        else:
                            ins = nc.scalar.mul(QT[j][:, 0:2, :], src[:, 0:2 * T].rearrange("p (m t) -> p m t", m=2),
                                                qg0s[:, 0:1])
                    else:
                        if L == 3:
                            if n in (0, 1):
                                m = CW[n]
                                ins = nc.scalar.activation(CT[j][0:m, n, :], src[0:m, 0:NKP], ACT.Identity,
                                                           bias=ctx_bias[3][0:m, n:n + 1], scale=ctx_gain[3][0:m, n:n + 1])
                            kind = n - 2
                        MQ = 4 if L == 1 else 2
                        if kind == 0:
                            if L == 3:
                                for c in range(2):
                                    ins = nc.scalar.activation(XT[j][:, c, 0:T], src[:, c * T:(c + 1) * T], ACT.Identity,
                                                               bias=x_bias[3][:, c:c + 1], scale=x_gain[3][:, c:c + 1])
                            else:
                                ins = nc.scalar.copy(XT[j][:, :, 0:T], src[:, 0:2 * T].rearrange("p (c t) -> p c t", c=2))
                        elif kind == 1:
                            if L == 3:
                                for m in range(2):
                                    ins = nc.scalar.activation(QT[j][:, m, :], src[:, m * T:(m + 1) * T], ACT.Identity,
                                                               bias=bq3s[:, m:m + 1], scale=scale)
                            else:
                                ins = nc.scalar.mul(QT[j][:, 0:MQ, :], src[:, 0:MQ * T].rearrange("p (m t) -> p m t", m=MQ),
                                                    scale)
                        elif 2 <= kind < 2 + MQ:
                            m = kind - 2
                            if L == 3:
                                ins = nc.scalar.activation(kt(3, j)[:, m, 0:NC], src[:, 0:NC], ACT.Identity,
                                                           bias=bk3[:, m:m + 1])
                            else:
                                ins = nc.scalar.copy(kt(L, j)[:, m, 0:NC], src[:, 0:NC])
                        elif kind >= 2 + MQ:
                            c = kind - 2 - MQ
                            ins = nc.scalar.copy(vv(L, j)[:, c, :], src[:, 0:(512 if L == 1 else 256)])
                    ins.then_inc(s.copied.sem, 1)

                def exp(t, j, h):
                    n = H * t + h
                    k = (H * j + h) % 2
                    wait_for(act, s.maxed, MAXES[L] * (n + 1))
                    wait_for(act, s.probs_turned, n - 1)
                    pr = PR[k][0:T, :, :].rearrange("p c n -> p (c n)")
                    nc.scalar.activation(pr[:, 0:NK], S_bank[k][0:T, 0:NK], ACT.Exp, bias=nmax[k][0:T, :],
                                         accum_out=rsum[j][0:T, h:h + 1]).then_inc(s.exped.sem, 1)

                def o_copy(t, j):
                    wait_for(act, s.o_turned, t + 1)
                    wait_for(act, s.out, t)
                    m = 4 if L == 1 else 2
                    nc.scalar.copy(OT[:, 0:m, :], R_bank[:, 0:m * T].rearrange("p (m t) -> p m t", m=m)
                                   ).then_inc(s.o_copied.sem, 1)

                def prepare(t, j):
                    for n in range(STEPS[L]):
                        step(t, j, n)

                def attend(t, j, more):
                    exp(t, j, 0)
                    if H > 1:
                        exp(t, j, 1)
                    if not (isinstance(t, int) and t == 0):
                        o_copy(t - 1, 1 - j)
                    for h in range(H):
                        if more:
                            for n in GROUPS[L][h]:
                                step(t + 1, 1 - j, n)
                        if h + 2 < H:
                            exp(t, j, h + 2)

                pipelined(act, prepare, attend, o_copy)
                end(act)


            def x_copy(s, t, j):
                act.wait_ge(s.x_turned, t + 1)
                nc.scalar.copy(FXT[j][:, :, :], bank[0][:, 0:2 * T].rearrange("p (c t) -> p c t", c=2)
                               ).then_inc(s.x_copied, 1)

            def exp_difference(s, n_route, t, j):
                act.wait_ge(s.route, n_route * t + 4)
                nc.scalar.activation(ED[j][0:T, 1:2], ED[j][0:T, 0:1], ACT.Exp).then_inc(s.exped, 1)

            def routed_experts():
                s = mx0
                begin(act, 1)
                act.wait_ge(loaded[1], 16 * n_loads[1])

                in_turn(act, lambda t, j: x_copy(s, t, j))

                def rows_copy(i, j):
                    act.wait_ge(s.rows_turned, i + 1)
                    nc.scalar.copy(TT[j][:, :, :], bank[0][:, 0:2 * P].rearrange("p (c t) -> p c t", c=2)
                                   ).then_inc(s.rows_copied, 1)

                def tile(i, j, more):
                    for f in range(HID0 // P):
                        n = 8 * i + f
                        act.wait_ge(s.gate, n + 1)
                        wait_count(act, s.hidden, n - 1)
                        nc.scalar.activation(SG[f % 2][:, :], bank[2 + f % 2][:, 0:P], ACT.Sigmoid,
                                             bias=B1[j][:, 8 + f:9 + f]).then_inc(s.sigmoid, 1)
                    if more:
                        rows_copy(i + 1, 1 - j)

                pipelined(act, rows_copy, tile, lambda i, j: None, TILES0)
                end(act)

            def squared_experts():
                s = mx1
                begin(act, 3)

                def hidden(t, j, g):
                    act.wait_ge(s.hidden, 3 * t + g + 1)
                    nc.scalar.activation(RL[g][0:T, :], bank[2 + g][0:T, 0:3 * HID1], ACT.Relu).then_inc(s.relu, 1)
                    act.wait_ge(s.relu, 3 * t + g + 1)
                    nc.scalar.square(SQ[g][0:T, :], RL[g][0:T, :]).then_inc(s.squared, 1)

                def prepare(t, j):
                    x_copy(s, t, j)
                    exp_difference(s, 9, t, j)
                    for g in range(3):
                        hidden(t, j, g)

                def attend(t, j, more):
                    if more:
                        prepare(t + 1, 1 - j)

                pipelined(act, prepare, attend, lambda t, j: None)
                end(act)

            def linear_experts():
                s = mx2
                begin(act, 5)

                def prepare(t, j):
                    x_copy(s, t, j)
                    exp_difference(s, 11, t, j)

                in_turn(act, prepare)
                end(act)

            def slot_mixer():
                s = mx3
                begin(act, 7)
                act.wait_ge(s.w_in, 16 * len(slot_loads))

                def prepare(t, j):
                    x_copy(s, t, j)

                def attend(t, j, more):
                    act.wait_ge(s.hidden, t + 1)
                    if isinstance(t, int) and t == 0:
                        act.wait_ge(s.consts, 9)
                    nc.scalar.activation(HG[j][:, :], bank[1 + j][:, 0:T], ACT.Gelu, bias=Sb1[:, 0:1]).then_inc(s.gelu, 1)
                    if more:
                        prepare(t + 1, 1 - j)

                pipelined(act, prepare, attend, lambda t, j: None)

                def weights(u, k):
                    w = pair[k]
                    for m in range(2):
                        ins = nc.scalar.activation(w.AL[0:T, m, :], ML[0:T, bass.ds(2 * u + m, 1), :], ACT.Exp,
                                                   accum_out=w.AS[0:T, m:m + 1])
                    ins.then_inc(s.exped, 1)

                def pooled(u, k):
                    act.wait_ge(s.pooled_turned, u + 1)
                    nc.scalar.copy(pair[k].SUT[:, :, :], bank[4 * k][:, 0:2 * P].rearrange("p (c n) -> p c n", c=2)
                                   ).then_inc(s.pooled_copied, 1)

                def rz_tanh(u, k):
                    act.wait_ge(s.rz_in, 2 * u + 1)
                    nc.scalar.activation(pair[k].RZ[:, :], pair[k].RZ[:, :], ACT.Tanh, scale=0.5).then_inc(s.rz_tanh, 1)

                def n_tanh(u, k):
                    act.wait_ge(s.rz_done, 3 * (u + 1))
                    nc.scalar.activation(pair[k].NN[:, :], pair[k].NN[:, :], ACT.Tanh).then_inc(s.n_tanh, 1)

                def slots_copy(u, k):
                    act.wait_ge(s.s_turned, u + 1)
                    nc.scalar.copy(pair[k].ST[:, :, :], bank[4 * k][:, 0:2 * P].rearrange("p (c n) -> p c n", c=2)
                                   ).then_inc(s.s_copied, 1)

                def qk_copy(u, k):
                    act.wait_ge(s.qkv, u + 1)
                    for m, b in ((0, Sbq), (1, Sbk)):
                        ins = nc.scalar.activation(pair[k].QS[0:DQ, m, :], bank[4 * k + 1][0:DQ, m * P:(m + 1) * P],
                                                   ACT.Identity, bias=b[0:DQ, 0:1])
                    ins.then_inc(s.qk_copied, 1)

                def attn_exp(u, k):
                    act.wait_ge(s.masked, 2 * (u + 1))
                    nc.scalar.activation(pair[k].AT[:, :], pair[k].AT[:, :], ACT.Exp, bias=pair[k].AX[:, 0:1],
                                         accum_out=pair[k].AU[:, 0:1]).then_inc(s.attn_exped, 1)

                def y_copy(u, k):
                    act.wait_ge(s.y_turned, u + 1)
                    for c in range(2):
                        ins = nc.scalar.activation(pair[k].YT[:, c, :], bank[4 * k][:, c * P:(c + 1) * P], ACT.Identity,
                                                   bias=Sb[:, c:c + 1], scale=Sg[:, c:c + 1])
                    ins.then_inc(s.y_copied, 1)

                def mixed_copy(u, k):
                    act.wait_ge(s.mixed, u + 1)
                    for m in range(2):
                        ins = nc.scalar.copy(pair[k].MT[:, 2 * m:2 * m + 2, :],
                                             bank[4 * k + 3 * (1 - m)][:, 0:2 * T].rearrange("p (c t) -> p c t", c=2))
                    ins.then_inc(s.mixed_copied, 1)

                act.wait_ge(s.picked, 8 * B)
                with act.Fori(0, B // 4) as i:
                    for stage in (weights, pooled, rz_tanh, n_tanh, slots_copy, qk_copy, attn_exp, y_copy, mixed_copy):
                        stage(2 * i, 0)
                        stage(2 * i + 1, 1)
                end(act)

            for p in phases:
                if p % 2 == 0:
                    attention(p // 2)
                else:
                    (routed_experts, squared_experts, linear_experts, slot_mixer)[p // 2]()

        @block.vector
        def _(dve):
            dve.wait_ge(start.gates_done, 1)
            dve.wait_ge(start.x_loaded, 16)

            def attention(L):
                s = at[L]
                H, W, NK, CH = HEADS[L], HWID[L], KEYS[L], CHUNKS[L]
                begin(dve, 2 * L)
                for j in range(2):
                    if L in (0, 3):
                        nc.vector.memset(C[j][96:P, NCH - 1, :], 0.0)
                    if L == 0:
                        nc.vector.memset(XT[j][:, :, T:P], 0.0)
                        nc.vector.memset(QK[j][96:P, 4, :], 1.0)
                        nc.vector.memset(MR[j][0:T, NCH - 1, LAST:P], FAR)
                        nc.vector.memset(MR[j][0:T, NCH, 0:T], 0.0)
                        nc.vector.memset(MR[j][0:T, NCH, T:P], FAR)
                    if L in (1, 2):
                        nc.vector.memset(CT[j][:, :, NC:NKP], 0.0)
                    if L > 0:
                        nc.vector.memset(PR[j][0:T, NCH - 1, LAST:P], 0.0)
                dve.drain().then_inc(s.cleared.sem, 1)
                wait_for(dve, s.cleared, 1)
                dve.wait_ge(loaded[2 * L], 16 * n_loads[2 * L])

                def ln_ctx_stats(t, j):
                    wait_for(dve, (s.ctx_in0, s.ctx_in1)[j], 32 * (t // 2 + 1))
                    b = 10 * t
                    for c in range(NCH):
                        nc.vector.bn_stats(st6[j][:, c, :], C[j][:, c, :]).then_inc(s.ln_ctx.sem, 1)
                    wait_for(dve, s.ln_ctx, b + 3)
                    apart(dve)
                    for c in range(NCH):
                        nc.vector.bn_aggr(mv[j][:, c, :], st6[j][:, c, :]).then_inc(s.ln_ctx.sem, 1)
                    wait_for(dve, s.ln_ctx, b + 6)
                    nc.vector.tensor_scalar(rs[j][:, 0:3], mv[j][:, 0:3, 1], LN_EPS, None, ALU.add).then_inc(s.ln_ctx.sem, 1)

                def ln_ctx_norm(t, j):
                    wait_for(dve, s.rstd_ctx, t + 1)
                    for c in range(NCH):
                        nc.vector.tensor_scalar(CNorm[j][:, c, :], C[j][:, c, :], mv[j][:, c, 0:1], rs[j][:, c:c + 1],
                                                ALU.subtract, ALU.mult).then_inc(s.ln_ctx.sem, 1)

                def ln_x(t, j, k):
                    b = 4 * (NORMS[L] * t + k)
                    src = X[0:T, bass.ds(t, 1), :] if k == 0 else XN[j][0:T, :]
                    dst = XN[j] if k == 0 else XN2[j]
                    if k:
                        wait_for(dve, s.ln_x, b)
                    nc.vector.bn_stats(st6[j][0:T, 3, :], src).then_inc(s.ln_x.sem, 1)
                    wait_for(dve, s.ln_x, b + 1)
                    apart(dve)
                    nc.vector.bn_aggr(mv[j][0:T, 3, :], st6[j][0:T, 3, :]).then_inc(s.ln_x.sem, 1)
                    wait_for(dve, s.ln_x, b + 2)
                    nc.vector.tensor_scalar(rs[j][0:T, 3:4], mv[j][0:T, 3, 1:2], LN_EPS, None, ALU.add).then_inc(s.ln_x.sem, 1)

                def ln_x_norm(t, j, k):
                    src = X[0:T, bass.ds(t, 1), :] if k == 0 else XN[j][0:T, :]
                    dst = XN[j] if k == 0 else XN2[j]
                    wait_for(dve, s.rstd_x, NORMS[L] * t + k + 1)
                    nc.vector.tensor_scalar(dst[0:T, :], src, mv[j][0:T, 3, 0:1], rs[j][0:T, 3:4],
                                            ALU.subtract, ALU.mult).then_inc(s.ln_x.sem, 1)

                def mask_row(t, j):
                    wait_for(dve, (s.mask_in0, s.mask_in1)[j], 16 * (t // 2 + 1))
                    mr = MR[j][0:T, :, :].rearrange("p c n -> p (c n)")
                    nc.vector.tensor_scalar(mr[:, 0:NC], M8[j][0:T, :], -FAR, FAR, ALU.mult, ALU.add
                                            ).then_inc(s.mask_row.sem, 1)

                def rms(t, j):
                    wait_for(dve, s.copied, STEPS[L] * t + 8)
                    b = 4 * t
                    nc.vector.tensor_tensor(QKsq[:, :, :], QK[j][:, :, :], QK[j][:, :, :], ALU.mult).then_inc(s.qk_rms.sem, 1)
                    wait_for(dve, s.qk_rms, b + 1)
                    nc.vector.reduce_sum(ss[j][:, :], QKsq[:, :, :].rearrange("p c (h w) -> p (c h) w", w=W), axis=AXX
                                         ).then_inc(s.qk_rms.sem, 1)
                    wait_for(dve, s.qk_rms, b + 2)
                    nc.vector.tensor_scalar(rr[j][:, :], ss[j][:, :], 1.0 / W, 1e-16, ALU.mult, ALU.max
                                            ).then_inc(s.qk_rms.sem, 1)

                def rms_scale(t, j):
                    wait_for(dve, s.rqk, t + 1)
                    v = QK[j][:, :, :].rearrange("p c (h w) -> p (c h) w", w=W)
                    nc.vector.tensor_tensor(v, v, rr[j][:, :].rearrange("p (n o) -> p n o", o=1).broadcast_to([P, 20, W]),
                                            ALU.mult).then_inc(s.qk_rms.sem, 1)

                def maximum(t, j, h):
                    n = H * t + h
                    k = (H * j + h) % 2
                    wait_for(dve, s.scores, n + 1)
                    if L == 0:
                        if h == 0:
                            wait_for(dve, s.mask_row, t + 1)
                        sc = S_bank[k][0:T, 0:NK]
                        apart(dve)
                        nc.vector.tensor_tensor_reduce(out=sc, in0=sc, in1=MR[j][0:T, :, :].rearrange("p c n -> p (c n)"),
                                                       scale=1.0, scalar=-3.0e38, op0=ALU.add, op1=ALU.max,
                                                       accum_out=pmax[k][0:T, :]).then_inc(s.maxed.sem, 1)
                        wait_for(dve, s.maxed, 2 * n + 1)
                        nc.vector.tensor_scalar(nmax[k][0:T, :], pmax[k][0:T, :], -1.0, None, ALU.mult).then_inc(s.maxed.sem, 1)
                    else:
                        nc.vector.tensor_reduce(nmax[k][0:T, :], S_bank[k][0:T, 0:NK], axis=AXX, op=ALU.max,
                                                negate=True).then_inc(s.maxed.sem, 1)

                def probs_copy(t, j, h):
                    n = H * t + h
                    k = (H * j + h) % 2
                    wait_for(dve, s.probs_turned, n + 1)
                    wait_for(dve, s.pv, n - 1)
                    nc.vector.tensor_copy(PT[k][:, 0:CH, :], PT_bank[k][:, 0:CH * T].rearrange("p (c t) -> p c t", c=CH)
                                          ).then_inc(s.probs_copied.sem, 1)

                def o_scale(t, j):
                    wait_for(dve, s.pv, H * (t + 1))
                    wait_for(dve, s.o_turned, t)
                    nc.vector.reciprocal(rinv[0:T, 0:H], rsum[j][0:T, 0:H]).then_inc(s.o_scaled.sem, 1)
                    wait_for(dve, s.o_scaled, 2 * t + 1)
                    if H == 1:
                        nc.vector.scalar_tensor_tensor(O[0:T, 0:W], O_bank[0:T, 0:W], rinv[0:T, 0:1], bv3[0:T, :],
                                                       ALU.mult, ALU.add).then_inc(s.o_scaled.sem, 1)
                    else:
                        nc.vector.tensor_tensor(O[0:T, 0:H * W].rearrange("p (h w) -> p h w", h=H),
                                                O_bank[0:T, 0:H * W].rearrange("p (h w) -> p h w", h=H),
                                                rinv[0:T, 0:H].rearrange("p (h o) -> p h o", o=1).broadcast_to([T, H, W]),
                                                ALU.mult).then_inc(s.o_scaled.sem, 1)

                def residual(t, j):
                    wait_for(dve, s.out, t + 1)
                    nc.vector.tensor_tensor(RO[0:T, :], R_bank[0:T, 0:D], bo[L][0:T, :], ALU.add).then_inc(s.resid.sem, 1)
                    wait_for(dve, s.resid, 2 * t + 1)
                    xt = X[0:T, bass.ds(t, 1), :].rearrange("p o d -> p (o d)")
                    nc.vector.scalar_tensor_tensor(xt, RO[0:T, :], gates[0:T, L:L + 1], xt, ALU.mult, ALU.add
                                                   ).then_inc(s.resid.sem, 1)

                def norms(t, j):
                    if L in (0, 3):
                        ln_ctx_stats(t, j)
                    ln_x(t, j, 0)
                    if L in (0, 3):
                        ln_ctx_norm(t, j)
                    if L == 0:
                        mask_row(t, j)
                    ln_x_norm(t, j, 0)
                    if NORMS[L] == 2:
                        ln_x(t, j, 1)
                        ln_x_norm(t, j, 1)

                def prepare(t, j):
                    norms(t, j)
                    if L == 0:
                        rms(t, j)
                        rms_scale(t, j)

                def attend(t, j, more):
                    maximum(t, j, 0)
                    if H > 1:
                        maximum(t, j, 1)
                    if more:
                        norms(t + 1, 1 - j)
                    for h in range(H):
                        probs_copy(t, j, h)
                        if h == 0 and not (isinstance(t, int) and t == 0):
                            residual(t - 1, 1 - j)
                        if h + 2 < H:
                            maximum(t, j, h + 2)
                        if L == 0 and more and h == 2:
                            rms(t + 1, 1 - j)
                    if L == 0 and more:
                        rms_scale(t + 1, 1 - j)
                    o_scale(t, j)

                pipelined(dve, prepare, attend, residual)
                end(dve)


            def x_stats(s):
                for t in range(B):
                    nc.vector.bn_stats(Fst6[0:T, t, :], X[0:T, t, :]).then_inc(s.ln_x, 1)
                dve.wait_ge(s.ln_x, B)
                for t in range(B):
                    nc.vector.bn_aggr(Fmv[0:T, t, :], Fst6[0:T, t, :]).then_inc(s.ln_x, 1)
                dve.wait_ge(s.ln_x, 2 * B)
                nc.vector.tensor_scalar(Frs[0:T, :], Fmv[0:T, :, 1], LN_EPS, None, ALU.add).then_inc(s.ln_x, 1)
                dve.wait_ge(s.rstd_x, 1)

            def x_norm(s, t, j):
                wait_count(dve, s.x_turned, t - 1)
                nc.vector.tensor_scalar(FX[j][0:T, :], X[0:T, bass.ds(t, 1), :].rearrange("p o d -> p (o d)"),
                                        Fmv[0:T, bass.ds(t, 1), 0:1].rearrange("p o n -> p (o n)"),
                                        Frs[0:T, bass.ds(t, 1)], ALU.subtract, ALU.mult).then_inc(s.ln_x, 1)

            def choose(s, n, t, j, bias=None):
                b = n * t
                dve.wait_ge(s.logits, t + 1)
                if bias is None:
                    nc.vector.tensor_copy(LG[j][0:T, :], bank[1][0:T, 0:8]).then_inc(s.route, 1)
                else:
                    nc.vector.tensor_tensor(LG[j][0:T, :], bank[1][0:T, 0:8], bias[0:T, :], ALU.add).then_inc(s.route, 1)
                dve.wait_ge(s.route, b + 1)
                apart(dve)
                nc.vector.max(V8[j][0:T, :], LG[j][0:T, :]).then_inc(s.route, 1)
                dve.wait_ge(s.route, b + 2)
                apart(dve)
                nc.vector.max_index(I8[j][0:T, :], V8[j][0:T, :], LG[j][0:T, :]).then_inc(s.route, 1)
                nc.vector.tensor_tensor(ED[j][0:T, 0:1], V8[j][0:T, 1:2], V8[j][0:T, 0:1], ALU.subtract).then_inc(s.route, 1)
                dve.wait_ge(s.route, b + 3)
                nc.vector.tensor_copy(IF[j][0:T, :], I8[j][0:T, 0:2]).then_inc(s.route, 1)

            def first_weight(s, n, t, j):
                dve.wait_ge(s.exped, t + 1)
                nc.vector.tensor_scalar(ED[j][0:T, 2:3], ED[j][0:T, 1:2], 1.0, None, ALU.add).then_inc(s.route, 1)
                dve.wait_ge(s.route, n * t + 6)
                nc.vector.reciprocal(ED[j][0:T, 3:4], ED[j][0:T, 2:3]).then_inc(s.route, 1)
                dve.wait_ge(s.route, n * t + 7)

            def routed_experts():
                s = mx0
                begin(dve, 1)
                dve.wait_ge(loaded[1], 16 * n_loads[1])

                x_stats(s)

                def prepare(t, j):
                    x_norm(s, t, j)
                    dve.wait_ge(s.ln_x, 2 * B + 1 + t + 1)
                    nc.vector.tensor_copy(XR0[0:T, bass.ds(t, 1), :].rearrange("p o d -> p (o d)"), FX[j][0:T, :]
                                          ).then_inc(s.xr_copied, 1)

                def attend(t, j, more):
                    if more:
                        prepare(t + 1, 1 - j)
                    dve.wait_ge(s.logits, t + 1)
                    nc.vector.tensor_tensor(LGA[0:T, bass.ds(t, 1), :].rearrange("p o e -> p (o e)"), bank[1][0:T, 0:E0],
                                            eb0[0:T, :], ALU.add).then_inc(s.route, 1)

                pipelined(dve, prepare, attend, lambda t, j: None)
                dve.wait_ge(s.route, B)
                for t in range(B):
                    nc.vector.max(V8A[0:T, t, :], LGA[0:T, t, :]).then_inc(s.route, 1)
                dve.wait_ge(s.route, 2 * B)
                for t in range(B):
                    nc.vector.max_index(I8A[0:T, t, :], V8A[0:T, t, :], LGA[0:T, t, :]).then_inc(s.route, 1)
                dve.wait_ge(s.route, 3 * B)
                nc.vector.tensor_copy(I1[0:T, :], I8A[0:T, :, 0]).then_inc(s.route, 1)
                dve.wait_ge(s.route, 3 * B + 1)
                nc.vector.tensor_tensor(OH[0:T, :, :], iota[0:T, :].rearrange("p (o e) -> p o e", o=1).broadcast_to([T, B, E0]),
                                        I1[0:T, :].rearrange("p (b o) -> p b o", o=1).broadcast_to([T, B, E0]),
                                        ALU.is_equal).then_inc(s.route, 1)

                def wide(v, dims):
                    return v.broadcast_to([P, *dims])

                dve.wait_ge(s.ranks, 1)
                dve.wait_ge(s.route, 3 * B + 2)
                nc.vector.tensor_copy(CUM[0][:, :, :], bank[3][:, 0:B * E0].rearrange("p (b e) -> p b e", b=B)
                                      ).then_inc(s.places, 1)
                n = 1
                for k, d in enumerate((1, 2, 4, 8)):
                    src, dst = CUM[k % 2], CUM[1 - k % 2]
                    dve.wait_ge(s.places, n)
                    nc.vector.tensor_copy(dst[:, 0:d, :], src[:, 0:d, :]).then_inc(s.places, 1)
                    nc.vector.tensor_tensor(dst[:, d:B, :], src[:, d:B, :], src[:, 0:B - d, :], ALU.add).then_inc(s.places, 1)
                    n += 2
                dve.wait_ge(s.places, 9)
                nc.vector.tensor_tensor(GT[:, :, :], wide(CUM[0][:, B - 1:B, :].rearrange("p o e -> p e o"), (E0, STEPS0)),
                                        wide(tile_starts[:, :].rearrange("p (o k) -> p o k", o=1), (E0, STEPS0)),
                                        ALU.is_gt).then_inc(s.places, 1)
                dve.wait_ge(s.places, 10)
                nc.vector.reduce_sum(NT[0][:, :], GT[:, :, :], axis=AXX).then_inc(s.places, 1)
                n = 11
                for k, d in enumerate((1, 2, 4)):
                    src, dst = NT[k], NT[k + 1]
                    dve.wait_ge(s.places, n)
                    nc.vector.tensor_copy(dst[:, 0:d], src[:, 0:d]).then_inc(s.places, 1)
                    nc.vector.tensor_tensor(dst[:, d:E0], src[:, d:E0], src[:, 0:E0 - d], ALU.add).then_inc(s.places, 1)
                    n += 2
                dve.wait_ge(s.places, 17)
                nc.vector.tensor_tensor(TE[:, :, :], wide(NT[3][:, :].rearrange("p (o e) -> p o e", o=1), (TILES0, E0)),
                                        wide(tile_iota[:, :].rearrange("p (i o) -> p i o", o=1), (TILES0, E0)),
                                        ALU.is_le).then_inc(s.places, 1)
                nc.vector.tensor_tensor(NT[1][:, :], NT[3][:, :], NT[0][:, :], ALU.subtract).then_inc(s.places, 1)
                nc.vector.tensor_tensor(CUM[1][:, :, :], CUM[0][:, :, :], bank[3][:, 0:B * E0].rearrange("p (b e) -> p b e", b=B),
                                        ALU.subtract).then_inc(s.places, 1)
                dve.wait_ge(s.places, 20)
                nc.vector.reduce_sum(TX[0][:, :], TE[:, :, :], axis=AXX).then_inc(s.places, 1)
                nc.vector.tensor_scalar(NT[2][:, :], NT[1][:, :], float(P), None, ALU.mult).then_inc(s.places, 1)
                nc.vector.tensor_tensor(PLACE[0:T, :, :], CUM[1][0:T, :, :],
                                        bank[2][0:T, 0:B * E0].rearrange("p (b e) -> p b e", b=B), ALU.add).then_inc(s.places, 1)
                dve.wait_ge(s.places, 23)
                nc.vector.tensor_scalar(TX[1][:, :], TX[0][:, :], float(E0 - 1), None, ALU.min).then_inc(s.places, 1)
                nc.vector.tensor_tensor(PLACE[0:T, :, :], PLACE[0:T, :, :],
                                        NT[2][0:T, :].rearrange("p (o e) -> p o e", o=1).broadcast_to([T, B, E0]),
                                        ALU.add).then_inc(s.places, 1)
                dve.wait_ge(s.places, 25)
                nc.vector.tensor_copy(TXI[:, :], TX[1][:, :]).then_inc(s.places, 1)
                nc.vector.tensor_tensor(PLACE[0:T, :, :], PLACE[0:T, :, :], OH[0:T, :, :], ALU.mult).then_inc(s.places, 1)
                dve.wait_ge(s.places, 27)
                nc.vector.reduce_sum(PF[0:T, :], PLACE[0:T, :, :], axis=AXX).then_inc(s.places, 1)
                dve.wait_ge(s.places, 28)
                dve.wait_ge(s.xr_copied, B)
                nc.vector.tensor_copy(PI[0:T, :], PF[0:T, :]).then_inc(s.places, 1)

                def tile(i, j):
                    for f in range(HID0 // P):
                        n = 8 * i + f
                        dve.wait_ge(s.value, n + 1)
                        dve.wait_ge(s.sigmoid, n + 1)
                        if f == 0:
                            wait_count(dve, s.out, i)
                        nc.vector.scalar_tensor_tensor(AC[:, f, :], bank[4 + f % 2][:, 0:P], B1[j][:, f:f + 1],
                                                       SG[f % 2][:, :], ALU.add, ALU.mult).then_inc(s.hidden, 1)
                    dve.wait_ge(s.out, i + 1)
                    wait_count(dve, (s.y_stored0, s.y_stored1)[j], 16 * (i // 2))
                    nc.vector.tensor_tensor(YR[j][:, :], bank[6 + j][:, 0:D], B2[j][:, :], ALU.add).then_inc(s.y_copied, 1)

                in_turn(dve, tile, TILES0)
                dve.wait_ge(s.gathered, 16 * B)
                nc.vector.scalar_tensor_tensor(X[0:T, :, :], XR0[0:T, :, :], gates[0:T, 4:5], X[0:T, :, :], ALU.mult, ALU.add
                                               ).then_inc(s.resid, 1)
                end(dve)

            def squared_experts():
                s = mx1
                begin(dve, 3)
                for j in range(2):
                    nc.vector.memset(WF[j][0:T, 0:1], 1.0).then_inc(s.ones, 1)
                dve.wait_ge(loaded[3], 16 * n_loads[3])
                dve.wait_ge(loaded[1], 16 * n_loads[1])
                dve.wait_ge(s.ones, 2)
                x_stats(s)

                def route(t, j):
                    choose(s, 9, t, j)
                    first_weight(s, 9, t, j)
                    nc.vector.tensor_scalar(ED[j][0:T, 4:5], ED[j][0:T, 3:4], 1.0, None, ALU.is_ge).then_inc(s.route, 1)
                    dve.wait_ge(s.route, 9 * t + 8)
                    nc.vector.tensor_scalar(WF[j][0:T, 1:9], iota[0:T, :], IF[j][0:T, 0:1], ED[j][0:T, 4:5],
                                            ALU.is_equal, ALU.mult).then_inc(s.route, 1)
                    dve.wait_ge(s.route, 9 * t + 9)

                def mask(t, j, g):
                    dve.wait_ge(s.squared, 3 * t + g + 1)
                    v = SQ[g][0:T, :].rearrange("p (e n) -> p e n", e=3)
                    w = WF[j][0:T, 3 * g:3 * g + 3].rearrange("p (e o) -> p e o", o=1).broadcast_to([T, 3, HID1])
                    nc.vector.tensor_tensor(v, v, w, ALU.mult).then_inc(s.masked, 1)

                def h_copy(t, j, g):
                    dve.wait_ge(s.h_turned, 3 * t + g + 1)
                    nc.vector.tensor_copy(HT[g][:, :, :], bank[5 + (3 * j + g) % 2][:, 0:3 * T].rearrange("p (c t) -> p c t", c=3)
                                          ).then_inc(s.h_copied, 1)

                def residual(t, j):
                    dve.wait_ge(s.out, t + 1)
                    xt = X[0:T, bass.ds(t, 1), :].rearrange("p o d -> p (o d)")
                    nc.vector.scalar_tensor_tensor(xt, bank[7][0:T, 0:D], gates[0:T, 5:6], xt, ALU.mult, ALU.add
                                                   ).then_inc(s.resid, 1)

                def prepare(t, j):
                    x_norm(s, t, j)
                    route(t, j)
                    for g in range(3):
                        mask(t, j, g)

                def attend(t, j, more):
                    if more:
                        x_norm(s, t + 1, 1 - j)
                    for g in range(3):
                        h_copy(t, j, g)
                    if more:
                        route(t + 1, 1 - j)
                        mask(t + 1, 1 - j, 0)
                    residual(t, j)
                    if more:
                        mask(t + 1, 1 - j, 1)
                        mask(t + 1, 1 - j, 2)

                pipelined(dve, prepare, attend, lambda t, j: None)
                end(dve)

            def linear_experts():
                s = mx2
                begin(dve, 5)
                dve.wait_ge(loaded[5], 16 * n_loads[5])
                dve.wait_ge(loaded[1], 16 * n_loads[1])
                x_stats(s)

                def route(t, j):
                    choose(s, 11, t, j)
                    first_weight(s, 11, t, j)
                    nc.vector.tensor_tensor(ED[j][0:T, 4:5], ED[j][0:T, 1:2], ED[j][0:T, 3:4], ALU.mult).then_inc(s.route, 1)
                    nc.vector.tensor_scalar(WF[j][0:T, 0:8], iota[0:T, :], IF[j][0:T, 0:1], ED[j][0:T, 3:4],
                                            ALU.is_equal, ALU.mult).then_inc(s.route, 1)
                    dve.wait_ge(s.route, 11 * t + 8)
                    nc.vector.tensor_scalar(WB[j][0:T, :], iota[0:T, :], IF[j][0:T, 1:2], ED[j][0:T, 4:5],
                                            ALU.is_equal, ALU.mult).then_inc(s.route, 1)
                    dve.wait_ge(s.route, 11 * t + 10)
                    nc.vector.tensor_tensor(WF[j][0:T, 0:8], WF[j][0:T, 0:8], WB[j][0:T, :], ALU.add).then_inc(s.route, 1)
                    dve.wait_ge(s.route, 11 * t + 11)

                def combine(t, j, g):
                    dve.wait_ge(s.out, 4 * t + g + 1)
                    for k in range(2):
                        e = 2 * g + k
                        y, w = bank[2 + g][0:T, k * D:(k + 1) * D], WF[j][0:T, e:e + 1]
                        if e == 0:
                            nc.vector.tensor_scalar(ACC[0:T, :], y, w, None, ALU.mult).then_inc(s.combined, 1)
                        else:
                            dve.wait_ge(s.combined, 8 * t + e)
                            nc.vector.scalar_tensor_tensor(ACC[0:T, :], y, w, ACC[0:T, :], ALU.mult, ALU.add
                                                           ).then_inc(s.combined, 1)

                def prepare(t, j):
                    x_norm(s, t, j)
                    route(t, j)

                def attend(t, j, more):
                    if more:
                        x_norm(s, t + 1, 1 - j)
                    for g in range(4):
                        combine(t, j, g)
                    dve.wait_ge(s.combined, 8 * (t + 1))
                    xt = X[0:T, bass.ds(t, 1), :].rearrange("p o d -> p (o d)")
                    nc.vector.scalar_tensor_tensor(xt, ACC[0:T, :], gates[0:T, 6:7], xt, ALU.mult, ALU.add
                                                   ).then_inc(s.resid, 1)
                    if more:
                        route(t + 1, 1 - j)

                pipelined(dve, prepare, attend, lambda t, j: None)
                end(dve)

            def slot_mixer():
                s = mx3
                begin(dve, 7)
                x_stats(s)
                for k in range(2):
                    nc.vector.memset(pair[k].ALP[0:T, 0, NS:P], 0.0)
                    nc.vector.memset(pair[k].ALP[0:T, 1, 0:NS], 0.0)
                nc.vector.memset(XS[0:T, :, D:D + 1], 1.0).then_inc(s.consts, 1)
                dve.wait_ge(s.w_in, 16 * len(slot_loads))
                nc.vector.reduce_sum(MEAN[:, :, :].rearrange("p c o -> p (c o)"), SIT[:, :, 0:NS], axis=AXX
                                     ).then_inc(s.consts, 1)
                nc.vector.tensor_scalar(TAU[:, 1:2], TAU[:, 0:1], -1.0, None, ALU.mult).then_inc(s.consts, 1)
                dve.wait_ge(s.consts, 3)
                nc.vector.tensor_scalar(MEAN[:, :, :], MEAN[:, :, :], 1.0 / NS, None, ALU.mult).then_inc(s.consts, 1)
                nc.vector.tensor_tensor(TAU[:, 0:1], TAU[:, 0:1], TAU[:, 1:2], ALU.max).then_inc(s.consts, 1)
                dve.wait_ge(s.consts, 5)
                nc.vector.tensor_scalar(TAU[:, 1:2], TAU[:, 0:1], 0.1, None, ALU.add).then_inc(s.consts, 1)
                dve.wait_ge(s.consts, 6)
                nc.vector.reciprocal(TAU[:, 0:1], TAU[:, 1:2]).then_inc(s.consts, 1)
                dve.wait_ge(s.const_sums, 1)
                nc.vector.tensor_tensor(GH[:, 0:512], bank[4][:, :], Sbhh[:, 0:512], ALU.add).then_inc(s.consts, 1)
                nc.vector.tensor_tensor(Sb1[:, :], bank[6][:, 0:1], Sb1[:, :], ALU.add).then_inc(s.consts, 1)
                dve.wait_ge(s.consts, 9)
                nc.vector.tensor_tensor(GH[:, 512:768], bank[5][:, 0:D], Sbhh[:, 512:768], ALU.add).then_inc(s.consts, 1)
                nc.vector.tensor_tensor(GH[:, 0:512], GH[:, 0:512], Sbih[:, 0:512], ALU.add).then_inc(s.consts, 1)
                dve.wait_ge(s.consts, 11)

                def pick(t, j):
                    b = 8 * t
                    dve.wait_ge(s.ln_x, 2 * B + 1 + t + 1)
                    nc.vector.tensor_copy(XS[0:T, bass.ds(t, 1), 0:D].rearrange("p o d -> p (o d)"), FX[j][0:T, :]
                                          ).then_inc(s.picked, 1)
                    dve.wait_ge(s.logits, t + 1)
                    nc.vector.tensor_tensor(LS[j][0:T, :], bank[3][0:T, 0:NS], Sb2[0:T, :], ALU.add).then_inc(s.picked, 1)
                    dve.wait_ge(s.picked, b + 2)
                    nc.vector.tensor_scalar(LS[j][0:T, :], LS[j][0:T, :], TAU[0:T, 0:1], None, ALU.mult
                                            ).then_inc(s.picked, 1)
                    dve.wait_ge(s.picked, b + 3)
                    apart(dve)
                    nc.vector.max(LV[j][0:T, :], LS[j][0:T, :]).then_inc(s.picked, 1)
                    dve.wait_ge(s.picked, b + 4)
                    apart(dve)
                    nc.vector.match_replace(out=LR[j][0:T, :], in_to_replace=LV[j][0:T, :], in_values=LS[j][0:T, :],
                                            imm_value=-3.0e38).then_inc(s.picked, 1)
                    dve.wait_ge(s.picked, b + 5)
                    nc.vector.tensor_tensor(LR[j][0:T, :], LR[j][0:T, :], LS[j][0:T, :], ALU.is_equal).then_inc(s.picked, 1)
                    dve.wait_ge(s.picked, b + 6)
                    nc.vector.tensor_scalar(LS[j][0:T, :], LS[j][0:T, :], LV[j][0:T, 0:1], None, ALU.subtract
                                            ).then_inc(s.picked, 1)
                    dve.wait_ge(s.picked, b + 7)
                    nc.vector.scalar_tensor_tensor(ML[0:T, bass.ds(t, 1), :].rearrange("p o n -> p (o n)"), LR[j][0:T, :],
                                                   FAR, LS[j][0:T, :], ALU.mult, ALU.add).then_inc(s.picked, 1)

                def prepare(t, j):
                    x_norm(s, t, j)

                def attend(t, j, more):
                    if more:
                        prepare(t + 1, 1 - j)
                    pick(t, j)

                pipelined(dve, prepare, attend, lambda t, j: None)

                def alpha(u, k):
                    w = pair[k]
                    dve.wait_ge(s.exped, u + 1)
                    nc.vector.reciprocal(w.AR[0:T, :], w.AS[0:T, :]).then_inc(s.alpha, 1)
                    dve.wait_ge(s.alpha, 3 * u + 1)
                    for m in range(2):
                        nc.vector.tensor_scalar(w.ALP[0:T, m, m * NS:(m + 1) * NS], w.AL[0:T, m, :], w.AR[0:T, m:m + 1],
                                                None, ALU.mult).then_inc(s.alpha, 1)

                def pooled(u, k):
                    w = pair[k]
                    dve.wait_ge(s.sums, u + 1)
                    nc.vector.tensor_scalar(w.DEN[:, :], bank[4 * k][:, D:D + 1], 1e-8, None, ALU.add).then_inc(s.pooled, 1)
                    dve.wait_ge(s.pooled, 3 * u + 1)
                    nc.vector.reciprocal(w.DEN[:, :], w.DEN[:, :]).then_inc(s.pooled, 1)
                    dve.wait_ge(s.pooled, 3 * u + 2)
                    nc.vector.tensor_scalar(w.SU[:, :], bank[4 * k][:, 0:D], w.DEN[:, 0:1], None, ALU.mult
                                            ).then_inc(s.pooled, 1)

                def alpha_copy(u, k):
                    dve.wait_ge(s.alpha_turned, u + 1)
                    nc.vector.tensor_copy(pair[k].ALT[:, :], bank[4 * k + 1][:, 0:T]).then_inc(s.alpha_copied, 1)

                def rz_in(u, k):
                    dve.wait_ge(s.gru_in, u + 1)
                    nc.vector.tensor_tensor(pair[k].RZ[:, :], bank[4 * k + 2][:, :], GH[:, 0:512], ALU.add).then_inc(s.rz_in, 1)
                    nc.vector.tensor_tensor(pair[k].NN[:, :], bank[4 * k + 3][:, 0:D], Sbih[:, 512:768], ALU.add
                                            ).then_inc(s.rz_in, 1)

                def rz_done(u, k):
                    w = pair[k]
                    dve.wait_ge(s.rz_tanh, u + 1)
                    nc.vector.tensor_scalar(w.RZ[:, :], w.RZ[:, :], 0.5, 0.5, ALU.mult, ALU.add).then_inc(s.rz_done, 1)
                    dve.wait_ge(s.rz_done, 3 * u + 1)
                    nc.vector.tensor_tensor(w.RZ[:, 0:D], w.RZ[:, 0:D], GH[:, 512:768], ALU.mult).then_inc(s.rz_done, 1)
                    dve.wait_ge(s.rz_done, 3 * u + 2)
                    nc.vector.tensor_tensor(w.NN[:, :], w.NN[:, :], w.RZ[:, 0:D], ALU.add).then_inc(s.rz_done, 1)

                def slots_new(u, k):
                    w = pair[k]
                    dve.wait_ge(s.n_tanh, u + 1)
                    nc.vector.tensor_tensor(w.S[:, :], SI[:, :], w.NN[:, :], ALU.subtract).then_inc(s.slots_new, 1)
                    dve.wait_ge(s.slots_new, 3 * u + 1)
                    nc.vector.tensor_tensor(w.S[:, :], w.S[:, :], w.RZ[:, D:2 * D], ALU.mult).then_inc(s.slots_new, 1)
                    dve.wait_ge(s.slots_new, 3 * u + 2)
                    nc.vector.tensor_tensor(w.S[:, :], w.S[:, :], w.NN[:, :], ALU.add).then_inc(s.slots_new, 1)

                def v_done(u, k):
                    dve.wait_ge(s.qkv, u + 1)
                    nc.vector.tensor_tensor(pair[k].VS[:, :], bank[4 * k + 3][:, 0:D], Sbv[:, :], ALU.add
                                            ).then_inc(s.v_done, 1)

                def masked(u, k):
                    w = pair[k]
                    dve.wait_ge(s.attn, u + 1)
                    nc.vector.scalar_tensor_tensor(w.AT[:, :], bank[4 * k + 2][:, 0:P], float(DQ) ** -0.5, BD[:, :],
                                                   ALU.mult, ALU.add).then_inc(s.masked, 1)
                    dve.wait_ge(s.masked, 2 * u + 1)
                    nc.vector.tensor_reduce(w.AX[:, :], w.AT[:, :], axis=AXX, op=ALU.max, negate=True).then_inc(s.masked, 1)

                def attn_copy(u, k):
                    w = pair[k]
                    dve.wait_ge(s.attn_turned, u + 1)
                    nc.vector.tensor_copy(w.ATT[:, :], bank[4 * k + 3][:, 0:P]).then_inc(s.attn_copied, 1)
                    nc.vector.reciprocal(w.AI[:, :], w.AU[:, :]).then_inc(s.attn_copied, 1)

                def y_stats(u, k):
                    w = pair[k]
                    dve.wait_ge(s.comm, u + 1)
                    dve.wait_ge(s.attn_copied, 2 * (u + 1))
                    nc.vector.scalar_tensor_tensor(w.Y[:, :], bank[4 * k + 2][:, 0:D], w.AI[:, 0:1], w.S[:, :],
                                                   ALU.mult, ALU.add).then_inc(s.y_stats, 1)
                    dve.wait_ge(s.y_stats, 4 * u + 1)
                    nc.vector.bn_stats(w.y6[:, :], w.Y[:, :]).then_inc(s.y_stats, 1)
                    dve.wait_ge(s.y_stats, 4 * u + 2)
                    apart(dve)
                    nc.vector.bn_aggr(w.ymv[:, :], w.y6[:, :]).then_inc(s.y_stats, 1)
                    dve.wait_ge(s.y_stats, 4 * u + 3)
                    nc.vector.tensor_scalar(w.yrs[:, :], w.ymv[:, 1:2], LN_EPS, None, ALU.add).then_inc(s.y_stats, 1)

                def y_norm(u, k):
                    w = pair[k]
                    dve.wait_ge(s.rstd_y, u + 1)
                    nc.vector.tensor_scalar(w.Y[:, :], w.Y[:, :], w.ymv[:, 0:1], w.yrs[:, :], ALU.subtract, ALU.mult
                                            ).then_inc(s.y_normed, 1)

                def values_done(u, k):
                    dve.wait_ge(s.values, u + 1)
                    nc.vector.tensor_tensor(pair[k].SV[:, :], bank[4 * k + 1][:, 0:D], Sbvp[:, :], ALU.add
                                            ).then_inc(s.values_done, 1)

                def residual(u, k):
                    dve.wait_ge(s.out, u + 1)
                    r = pair[k].RZ[0:T, :].rearrange("p (m d) -> p m d", m=2)
                    nc.vector.tensor_tensor(r, bank[4 * k + 2][0:T, :].rearrange("p (m d) -> p m d", m=2),
                                            Sbo[0:T, :].rearrange("p (o d) -> p o d", o=1).broadcast_to([T, 2, D]), ALU.add
                                            ).then_inc(s.resid, 1)
                    dve.wait_ge(s.resid, 2 * u + 1)
                    xt = X[0:T, bass.ds(2 * u, 2), :]
                    nc.vector.scalar_tensor_tensor(xt, r, gates[0:T, 7:8], xt, ALU.mult, ALU.add).then_inc(s.resid, 1)

                with dve.Fori(0, B // 4) as i:
                    for stage in (alpha, pooled, alpha_copy, rz_in, rz_done, slots_new, v_done, masked, attn_copy, y_stats,
                                  y_norm, values_done, residual):
                        stage(2 * i, 0)
                        stage(2 * i + 1, 1)
                end(dve)

            for p in phases:
                if p % 2 == 0:
                    attention(p // 2)
                else:
                    (routed_experts, squared_experts, linear_experts, slot_mixer)[p // 2]()

        @block.tensor
        def _(pe):
            pe.wait_ge(start.consts, 16)

            def attention(L):
                s = at[L]
                H, W, NK, CH = HEADS[L], HWID[L], KEYS[L], CHUNKS[L]
                VN = 512 if L == 1 else 256
                MQ = 4 if L == 1 else 2
                begin(pe, 2 * L)
                wait_for(pe, s.cleared, 1)
                pe.wait_ge(loaded[2 * L], 16 * n_loads[2 * L])

                def step(t, j, n):
                    dst = J_bank[(j * STEPS[L] + n) % 2]
                    wait_for(pe, s.copied, STEPS[L] * t + n - 1)
                    done = STEPS[L] * t
                    mm, tr = nc.tensor.matmul, nc.tensor.transpose

                    def ctx_turn(c):
                        if c == 0:
                            wait_for(pe, s.ln_ctx, 10 * (t + 1))
                        else:
                            apart(pe)
                        for k in range(NCH):
                            ins = tr(dst[0:CW[c], k * P:(k + 1) * P], CNorm[j][:, k, c * P:c * P + CW[c]], ident[:, :])
                        return ins

                    def x_turn():
                        wait_for(pe, s.ln_x, 4 * NORMS[L] * (t + 1))
                        src = XN2[j] if NORMS[L] == 2 else XN[j]
                        for c in range(2):
                            ins = tr(dst[:, c * T:(c + 1) * T], src[0:T, c * P:(c + 1) * P], ident[0:T, 0:T])
                        return ins

                    def rows(lhs, parts, w, n_out, m_out):
                        for c in range(2):
                            ins = mm(dst[0:m_out, 0:n_out], lhs(c), w[0:parts[c], c, 0:n_out], start=(c == 0), stop=(c == 1))
                        return ins

                    if L == 0:
                        if n in (0, 1):
                            ins = ctx_turn(n)
                        elif n == 2:
                            ins = x_turn()
                        elif n in (3, 4, 5):
                            wait_for(pe, s.copied, done + 2)
                            k = n - 3
                            ins = rows(lambda c: CT[j][0:CW[c], c, k * P:(k + 1) * P], CW, wkv0, 512, P)
                        elif n == 6:
                            wait_for(pe, s.copied, done + 3)
                            ins = rows(lambda c: XT[j][:, c, :], (P, P), wlkv0, 512, P)
                        elif n == 7:
                            ins = rows(lambda c: XT[j][:, c, 0:T], (P, P), wq[0], D, T)
                        elif n in (8, 9):
                            m = n - 8
                            wait_for(pe, s.qk_rms, 4 * (t + 1))
                            for k in range(4):
                                ins = tr(dst[:, k * P:(k + 1) * P], QK[j][:, k, m * P:(m + 1) * P], ident[:, :])
                        else:
                            for m in range(2):
                                ins = tr(dst[:, m * T:(m + 1) * T], QK[j][0:T, 4, m * P:(m + 1) * P], ident[0:T, 0:T])
                    else:
                        kind = n
                        if L == 3:
                            kind = n - 2
                            if n in (0, 1):
                                ins = ctx_turn(n)
                        first = done + (3 if L == 3 else 1)
                        if kind == 0:
                            ins = x_turn()
                        elif kind == 1:
                            wait_for(pe, s.copied, first)
                            for m in range(MQ):
                                for c in range(2):
                                    ins = mm(dst[:, m * T:(m + 1) * T], wq[L][:, c, m * P:(m + 1) * P], XT[j][:, c, 0:T],
                                             start=(c == 0), stop=(c == 1))
                        elif 2 <= kind < 2 + MQ:
                            m = kind - 2
                            if m == 0 and L != 3:
                                wait_for(pe, (s.ctx_in0, s.ctx_in1)[j], 32 * (t // 2 + 1))
                            for c in range(2):
                                ins = mm(dst[:, 0:NC], wk[L][0:CW[c], c, m * P:(m + 1) * P], CT[j][0:CW[c], c, 0:NC],
                                         start=(c == 0), stop=(c == 1))
                        elif kind >= 2 + MQ:
                            k = kind - 2 - MQ
                            ins = rows(lambda c: CT[j][0:CW[c], c, k * P:(k + 1) * P], CW, wv[L], VN, P)
                    ins.then_inc(s.proj.sem, 1)

                def scores(t, j, h):
                    n = H * t + h
                    k = (H * j + h) % 2
                    wait_for(pe, s.exped, n - 1)
                    if h == 0:
                        wait_for(pe, s.copied, STEPS[L] * (t + 1))
                    if H == 1:
                        for m in range(2):
                            ins = nc.tensor.matmul(S_bank[k][0:T, 0:NK], QT[j][:, m, :], kt(L, j)[:, m, 0:NK],
                                                   start=(m == 0), stop=(m == 1))
                    else:
                        m, b = h // 2, W * (h % 2)
                        ins = nc.tensor.matmul(S_bank[k][0:T, 0:NK], QT[j][b:b + W, m, :], kt(L, j)[b:b + W, m, 0:NK],
                                               start=True, stop=True)
                    ins.then_inc(s.scores.sem, 1)

                def probs_turn(t, j, h):
                    n = H * t + h
                    k = (H * j + h) % 2
                    wait_for(pe, s.exped, n + 1)
                    wait_for(pe, s.probs_copied, n - 1)
                    for c in range(CH):
                        ins = nc.tensor.transpose(PT_bank[k][:, c * T:(c + 1) * T], PR[k][0:T, c, :], ident[0:T, 0:T])
                    ins.then_inc(s.probs_turned.sem, 1)

                def weigh(t, j, h):
                    n = H * t + h
                    k = (H * j + h) % 2
                    wait_for(pe, s.probs_copied, n + 1)
                    if h == 0:
                        wait_for(pe, s.o_scaled, 2 * t)
                    for c in range(CH):
                        ins = nc.tensor.matmul(O_bank[0:T, h * W:(h + 1) * W], PT[k][:, c, :],
                                               vv(L, j)[:, c, h * W:(h + 1) * W], start=(c == 0), stop=(c == CH - 1))
                    ins.then_inc(s.pv.sem, 1)

                def o_turn(t, j):
                    wait_for(pe, s.o_scaled, 2 * (t + 1))
                    wait_for(pe, s.resid, 2 * t)
                    for m in range(H * W // P):
                        ins = nc.tensor.transpose(R_bank[:, m * T:(m + 1) * T], O[0:T, m * P:(m + 1) * P], ident[0:T, 0:T])
                    ins.then_inc(s.o_turned.sem, 1)

                def project(t, j):
                    wait_for(pe, s.o_copied, t + 1)
                    M = H * W // P
                    for m in range(M):
                        ins = nc.tensor.matmul(R_bank[0:T, 0:D], OT[:, m, :], wo[L][:, m, :], start=(m == 0), stop=(m == M - 1))
                    ins.then_inc(s.out.sem, 1)

                def prepare(t, j):
                    for n in range(STEPS[L]):
                        step(t, j, n)

                def attend(t, j, more):
                    started = not (isinstance(t, int) and t == 0)
                    scores(t, j, 0)
                    if H > 1:
                        scores(t, j, 1)
                    if started:
                        o_turn(t - 1, 1 - j)
                    for h in range(H):
                        probs_turn(t, j, h)
                        if h + 2 < H:
                            scores(t, j, h + 2)
                        if h == 0 and started:
                            project(t - 1, 1 - j)
                        if more:
                            for n in GROUPS[L][h]:
                                step(t + 1, 1 - j, n)
                        weigh(t, j, h)

                def finish(t, j):
                    o_turn(t, j)
                    project(t, j)

                pipelined(pe, prepare, attend, finish)
                end(pe)


            def x_turn(s, t, j):
                pe.wait_ge(s.ln_x, 2 * B + 1 + t + 1)
                wait_count(pe, s.x_copied, t)
                for c in range(2):
                    ins = nc.tensor.transpose(bank[0][:, c * T:(c + 1) * T], FX[j][0:T, c * P:(c + 1) * P], ident[0:T, 0:T])
                ins.then_inc(s.x_turned, 1)

            def logits(s, w, n_route, t, j):
                pe.wait_ge(s.x_copied, t + 1)
                wait_count(pe, s.route, n_route * (t - 1) + 1)
                for c in range(2):
                    ins = nc.tensor.matmul(bank[1][0:T, 0:8], FXT[j][:, c, :], w[:, c, :], start=(c == 0), stop=(c == 1))
                ins.then_inc(s.logits, 1)

            def routed_experts():
                s = mx0
                begin(pe, 1)
                pe.wait_ge(loaded[1], 16 * n_loads[1])

                def attend(t, j, more):
                    pe.wait_ge(s.x_copied, t + 1)
                    if more:
                        x_turn(s, t + 1, 1 - j)
                    logits(s, ew0, 1, t, j)

                pipelined(pe, lambda t, j: x_turn(s, t, j), attend, lambda t, j: None)
                pe.wait_ge(start.zeros, 2)
                pe.wait_ge(s.route, 3 * B + 2)
                choices = OH[0:T, :, :].rearrange("p b e -> p (b e)")
                nc.tensor.matmul(bank[2][0:T, 0:B * E0], earlier[0:T, 0, :], choices, start=True, stop=True)
                nc.tensor.matmul(bank[3][:, 0:B * E0], ones[0:T, :], choices, start=True, stop=True).then_inc(s.ranks, 1)
                pe.wait_ge(s.places, PLACED)

                def rows_turn(i, j):
                    pe.wait_ge((s.rows_in0, s.rows_in1)[j], 16 * (i // 2 + 1))
                    wait_count(pe, s.rows_copied, i)
                    for c in range(2):
                        ins = nc.tensor.transpose(bank[0][:, c * P:(c + 1) * P], TR[j][:, c * P:(c + 1) * P], ident[:, :])
                    ins.then_inc(s.rows_turned, 1)

                def tile(i, j, more):
                    pe.wait_ge(s.rows_copied, i + 1)
                    pe.wait_ge((s.w1_in0, s.w1_in1)[j], 48 * (i // 2 + 1))
                    for f in range(HID0 // P):
                        n = 8 * i + f
                        for half, to, sig, used in ((1, 2, s.gate, s.sigmoid), (0, 4, s.value, s.hidden)):
                            wait_count(pe, used, n - 1)
                            for c in range(2):
                                col = half * HID0 + f * P
                                ins = nc.tensor.matmul(bank[to + f % 2][:, 0:P], W1[j][:, c, col:col + P], TT[j][:, c, :],
                                                       start=(c == 0), stop=(c == 1))
                            ins.then_inc(sig, 1)
                    if more:
                        rows_turn(i + 1, 1 - j)
                    pe.wait_ge(s.hidden, 8 * (i + 1))
                    wait_count(pe, s.y_copied, i - 1)
                    pe.wait_ge((s.w2_in0, s.w2_in1)[j], 32 * (i // 2 + 1))
                    for f in range(HID0 // P):
                        ins = nc.tensor.matmul(bank[6 + j][:, 0:D], AC[:, f, :], W2[j][:, f, :],
                                               start=(f == 0), stop=(f == HID0 // P - 1))
                    ins.then_inc(s.out, 1)

                pipelined(pe, rows_turn, tile, lambda i, j: None, TILES0)
                end(pe)

            def squared_experts():
                s = mx1
                begin(pe, 3)
                pe.wait_ge(loaded[3], 16 * n_loads[3])

                def hidden(t, j, g):
                    wait_count(pe, s.relu, 3 * (t - 1) + g + 1)
                    for c in range(2):
                        ins = nc.tensor.matmul(bank[2 + g][0:T, 0:3 * HID1], FXT[j][:, c, :],
                                               up1[:, c, 3 * HID1 * g:3 * HID1 * (g + 1)], start=(c == 0), stop=(c == 1))
                    ins.then_inc(s.hidden, 1)

                def turn(t, j, g):
                    pe.wait_ge(s.masked, 3 * t + g + 1)
                    wait_count(pe, s.h_copied, 3 * t + g - 1)
                    for k in range(3):
                        ins = nc.tensor.transpose(bank[5 + (3 * j + g) % 2][:, k * T:(k + 1) * T],
                                                  SQ[g][0:T, k * HID1:(k + 1) * HID1], ident[0:T, 0:T])
                    ins.then_inc(s.h_turned, 1)

                def down(t, j, g):
                    pe.wait_ge(s.h_copied, 3 * t + g + 1)
                    if g == 0:
                        wait_count(pe, s.resid, t)
                    for k in range(3):
                        ins = nc.tensor.matmul(bank[7][0:T, 0:D], HT[g][:, k, :], down1[:, 3 * g + k, :],
                                               start=(g == 0 and k == 0), stop=(g == 2 and k == 2))
                    if g == 2:
                        ins.then_inc(s.out, 1)

                def prepare(t, j):
                    x_turn(s, t, j)
                    logits(s, ew1, 9, t, j)
                    for g in range(3):
                        hidden(t, j, g)

                def attend(t, j, more):
                    turn(t, j, 0)
                    turn(t, j, 1)
                    down(t, j, 0)
                    if more:
                        x_turn(s, t + 1, 1 - j)
                    down(t, j, 1)
                    turn(t, j, 2)
                    if more:
                        logits(s, ew1, 9, t + 1, 1 - j)
                        hidden(t + 1, 1 - j, 0)
                    down(t, j, 2)
                    if more:
                        hidden(t + 1, 1 - j, 1)
                        hidden(t + 1, 1 - j, 2)

                pipelined(pe, prepare, attend, lambda t, j: None)
                end(pe)

            def linear_experts():
                s = mx2
                begin(pe, 5)
                pe.wait_ge(loaded[5], 16 * n_loads[5])

                def experts(t, j, g):
                    wait_count(pe, s.combined, 8 * (t - 1) + 2 * g + 2)
                    for c in range(2):
                        ins = nc.tensor.matmul(bank[2 + g][0:T, :], FXT[j][:, c, :],
                                               lin2[:, c, 2 * g:2 * g + 2, :].rearrange("p e n -> p (e n)"),
                                               start=(c == 0), stop=(c == 1))
                    ins.then_inc(s.out, 1)

                def prepare(t, j):
                    x_turn(s, t, j)
                    logits(s, ew2, 11, t, j)

                def attend(t, j, more):
                    for g in range(4):
                        experts(t, j, g)
                        if g == 1 and more:
                            x_turn(s, t + 1, 1 - j)
                    if more:
                        logits(s, ew2, 11, t + 1, 1 - j)

                pipelined(pe, prepare, attend, lambda t, j: None)
                end(pe)

            def slot_mixer():
                s = mx3
                begin(pe, 7)
                pe.wait_ge(s.w_in, 16 * len(slot_loads))
                mm, tr = nc.tensor.matmul, nc.tensor.transpose
                for c in range(2):
                    mm(bank[4][:, :], SIT[:, c, :], SWhh[:, c, 0:512], start=(c == 0), stop=(c == 1))
                for c in range(2):
                    mm(bank[5][:, 0:D], SIT[:, c, :], SWhh[:, c, 512:768], start=(c == 0), stop=(c == 1))
                pe.wait_ge(s.consts, 4)
                for c in range(2):
                    ins = mm(bank[6][:, 0:1], SW1[:, 2 + c, :], MEAN[:, c, :], start=(c == 0), stop=(c == 1))
                ins.then_inc(s.const_sums, 1)

                def prepare(t, j):
                    x_turn(s, t, j)

                def attend(t, j, more):
                    pe.wait_ge(s.x_copied, t + 1)
                    wait_count(pe, s.gelu, t - 1)
                    for c in range(2):
                        ins = mm(bank[1 + j][:, 0:T], SW1[:, c, :], FXT[j][:, c, :], start=(c == 0), stop=(c == 1))
                    ins.then_inc(s.hidden, 1)
                    if more:
                        prepare(t + 1, 1 - j)
                    pe.wait_ge(s.gelu, t + 1)
                    wait_count(pe, s.picked, 8 * (t - 1) + 2)
                    mm(bank[3][0:T, 0:NS], HG[j][:, :], SW2[:, :], start=True, stop=True).then_inc(s.logits, 1)

                pipelined(pe, prepare, attend, lambda t, j: None)

                def turn(src, k):
                    for c in range(2):
                        ins = tr(bank[4 * k][:, c * P:(c + 1) * P], src[:, c * P:(c + 1) * P], ident[:, :])
                    return ins

                def product(dst, lhs, w, lo, hi):
                    for c in range(2):
                        ins = mm(dst, lhs[:, c, :], w[:, c, lo:hi], start=(c == 0), stop=(c == 1))
                    return ins

                def sums(u, k):
                    pe.wait_ge(s.alpha, 3 * (u + 1))
                    for m in range(2):
                        ins = mm(bank[4 * k][:, 0:D + 1], pair[k].ALP[0:T, m, :],
                                 XS[0:T, bass.ds(2 * u + m, 1), :].rearrange("p o d -> p (o d)"), start=(m == 0), stop=(m == 1))
                    ins.then_inc(s.sums, 1)

                def alpha_turn(u, k):
                    for m in range(2):
                        ins = mm(bank[4 * k + 1][:, 0:T], pair[k].ALP[0:T, m, :], ident[0:T, 0:T], start=(m == 0), stop=(m == 1))
                    ins.then_inc(s.alpha_turned, 1)

                def pooled_turn(u, k):
                    pe.wait_ge(s.pooled, 3 * (u + 1))
                    turn(pair[k].SU, k).then_inc(s.pooled_turned, 1)

                def gru_in(u, k):
                    pe.wait_ge(s.pooled_copied, u + 1)
                    product(bank[4 * k + 2][:, :], pair[k].SUT, SWih, 0, 512)
                    product(bank[4 * k + 3][:, 0:D], pair[k].SUT, SWih, 512, 768).then_inc(s.gru_in, 1)

                def s_turn(u, k):
                    pe.wait_ge(s.slots_new, 3 * (u + 1))
                    turn(pair[k].S, k).then_inc(s.s_turned, 1)

                def qkv(u, k):
                    pe.wait_ge(s.s_copied, u + 1)
                    pe.wait_ge(s.alpha_copied, u + 1)
                    for m, w in ((0, SWq), (1, SWk)):
                        for c in range(2):
                            mm(bank[4 * k + 1][0:DQ, m * P:(m + 1) * P], w[:, c, :], pair[k].ST[:, c, :],
                               start=(c == 0), stop=(c == 1))
                    product(bank[4 * k + 3][:, 0:D], pair[k].ST, SWv, 0, D).then_inc(s.qkv, 1)

                def attn(u, k):
                    pe.wait_ge(s.qk_copied, u + 1)
                    mm(bank[4 * k + 2][:, 0:P], pair[k].QS[0:DQ, 0, :], pair[k].QS[0:DQ, 1, :], start=True, stop=True
                       ).then_inc(s.attn, 1)

                def attn_turn(u, k):
                    pe.wait_ge(s.attn_exped, u + 1)
                    pe.wait_ge(s.v_done, u + 1)
                    tr(bank[4 * k + 3][:, 0:P], pair[k].AT[:, :], ident[:, :]).then_inc(s.attn_turned, 1)

                def comm(u, k):
                    pe.wait_ge(s.attn_copied, 2 * (u + 1))
                    mm(bank[4 * k + 2][:, 0:D], pair[k].ATT[:, :], pair[k].VS[:, :], start=True, stop=True).then_inc(s.comm, 1)

                def y_turn(u, k):
                    pe.wait_ge(s.y_normed, u + 1)
                    turn(pair[k].Y, k).then_inc(s.y_turned, 1)

                def values(u, k):
                    pe.wait_ge(s.y_copied, u + 1)
                    product(bank[4 * k + 1][:, 0:D], pair[k].YT, SWvp, 0, D).then_inc(s.values, 1)

                def mixed(u, k):
                    pe.wait_ge(s.values_done, u + 1)
                    for m in range(2):
                        for c in range(2):
                            ins = mm(bank[4 * k + 3 * (1 - m)][:, c * T:(c + 1) * T],
                                     pair[k].SV[NS * m:NS * (m + 1), c * P:(c + 1) * P], pair[k].ALT[NS * m:NS * (m + 1), :],
                                     start=True, stop=True)
                    ins.then_inc(s.mixed, 1)

                def out_rows(u, k):
                    pe.wait_ge(s.mixed_copied, u + 1)
                    for m in range(2):
                        for c in range(2):
                            ins = mm(bank[4 * k + 2][0:T, m * D:(m + 1) * D], pair[k].MT[:, 2 * m + c, :], SWo[:, c, :],
                                     start=(c == 0), stop=(c == 1))
                    ins.then_inc(s.out, 1)

                with pe.Fori(0, B // 4) as i:
                    for stage in (sums, alpha_turn, pooled_turn, gru_in, s_turn, qkv, attn, attn_turn, comm, y_turn, values,
                                  mixed, out_rows):
                        stage(2 * i, 0)
                        stage(2 * i + 1, 1)
                end(pe)

            for p in phases:
                if p % 2 == 0:
                    attention(p // 2)
                else:
                    (routed_experts, squared_experts, linear_experts, slot_mixer)[p // 2]()


_OUTS = [((B, T, D), 'float32')]


def layout(inputs):
    import numpy as _np

    v = {k: _np.asarray(x) for k, x in inputs.items()}

    def column(x):
        return _np.pad(x, (0, -len(x) % P)).reshape(-1, P).T

    r = {"x": v["x"], "ctx": v["ctx_768"], "ctxT": v["ctx_768"].transpose(0, 2, 1), "mask": v["mask_BxS2_bk0"],
         "gates": _np.concatenate([v["g_xattn"], v["g_ffn"]]), "ident": _np.eye(P, dtype=_np.float32),
         "L0_WqT": v["L0_xattn_Wq"].T, "L0_WkvT": v["L0_xattn_Wkv"].T, "L0_WlkvT": v["L0_xattn_Wlkv"].T,
         "L0_WoT": v["L0_xattn_Wo"].T, "L2_WoT": v["L2_xattn_Wo"].T,
         "L0_qn_g2": column(_np.tile(v["L0_xattn_qn_g"], 2)), "L0_kn_g2": column(_np.tile(v["L0_xattn_kn_g"], 2))}
    for n in ("Wq", "Wk", "Wv"):
        r[f"L1_{n}"] = v[f"L1_xattn_{n}"]
        r[f"L2_{n}T"] = v[f"L2_xattn_{n}"].T
        r[f"L3_{n}"] = v[f"L3_xattn_{n}"]
    r["earlier"] = _np.triu(_np.ones((T, T), dtype=_np.float32), 1)
    r["tile_starts"] = P * _np.arange(STEPS0, dtype=_np.float32)
    r["tile_iota"] = _np.arange(TILES0, dtype=_np.float32)
    r["iota"] = _np.arange(8, dtype=_np.float32)
    for n in ("router_w", "router_b", "b2", "w1", "w2"):
        r[f"F0_{n}"] = v[f"L0_ffn_{n}"]
    r["F0_b1c"] = v["L0_ffn_b1"].reshape(E0, -1, P).transpose(0, 2, 1)
    r["F1_Wr"] = v["L1_ffn_Wr"]
    r["F1_up"] = _np.concatenate([v["L1_ffn_Ws1"][None], v["L1_ffn_W1"]]).transpose(1, 0, 2).reshape(D, -1)
    r["F1_down"] = _np.concatenate([v["L1_ffn_Ws2"][None], v["L1_ffn_W2"]]).reshape(-1, D)
    s = {k[7:]: x for k, x in v.items() if k.startswith("L3_ffn_")}
    for n in ("w1", "w2", "wq", "wk", "wv", "wvp", "wo", "b2", "bih", "bhh", "bv", "bvp", "bo", "tau"):
        r[f"F3_{n}"] = s[n]
    for n in ("b1", "bq", "bk", "ln_g", "ln_b"):
        r[f"F3_{n}"] = column(s[n])
    r["F3_WihT"], r["F3_WhhT"] = s["Wih"].T, s["Whh"].T
    r["F3_slot_init2"] = _np.tile(s["slot_init"], (2, 1))
    r["F3_slot_initT2"] = _np.tile(s["slot_init"].T, (1, 2))
    r["F3_apart"] = _np.kron(1 - _np.eye(2), _np.ones((NS, NS))).astype(_np.float32) * _np.float32(FAR)
    r["F2_gateT"], r["F2_weight"] = v["L2_ffn_gate_w"].T, v["L2_ffn_weight"]
    r["L1_Wo"], r["L3_Wo"] = v["L1_xattn_Wo"], v["L3_xattn_Wo"]
    for L in range(4):
        r[f"L{L}_bo"] = v[f"L{L}_xattn_bo"]
    for n in ("ln_x_g", "ln_x_b", "ln_l_g", "ln_l_b"):
        r[f"L0_{n}"] = column(v[f"L0_xattn_{n}"])
    for n in ("ln1_g", "ln1_b", "ln2_g", "ln2_b", "bq", "bk"):
        r[f"L3_{n}"] = column(v[f"L3_xattn_{n}"])
    r["L3_bv"] = v["L3_xattn_bv"]
    return r


def kernel(**inputs):
    import numpy as _np
    import concourse.bacc as _bacc
    from concourse import mybir as _mybir
    from concourse.bass_utils import run_bass_kernel_spmd as _run

    nc = _bacc.Bacc("TRN2", target_bir_lowering=False, num_devices=1)
    arrays, args = {}, {}
    for name, x in layout(inputs).items():
        x = _np.ascontiguousarray(x)
        arrays[f"in_{name}"] = x
        args[name] = nc.dram_tensor(f"in_{name}", x.shape, _mybir.dt.from_np(x.dtype), kind="ExternalInput").ap()
    out = nc.dram_tensor("out_0_dram", _OUTS[0][0], _mybir.dt.float32, kind="ExternalOutput").ap()
    flamingo_kernel(nc, args, out)
    r = _run(nc, [arrays], core_ids=[0])
    return r.results[0]["out_0_dram"]
```

```python
from contextlib import ExitStack

import concourse.bass as bass
from concourse import mybir

ALU = mybir.AluOpType
ACT = mybir.ActivationFunctionType
F32 = mybir.dt.float32
U8 = mybir.dt.uint8
U32 = mybir.dt.uint32
I32 = mybir.dt.int32
AXX = mybir.AxisListType.X

B, T, D = 16, 100, 256
NC, DC = 361, 192
P = 128
NCH = 3
LAST = NC - (NCH - 1) * P
NKP = NCH * P
CW = (P, DC - P)
LN_EPS = 1e-5
FAR = -1.0e30

HEADS = (4, 8, 4, 1)
HWID = (64, 64, 64, 256)
KEYS = (NKP + P, NC, NC, NC)
CHUNKS = (NCH + 1, NCH, NCH, NCH)
GROUPS = (
    ((0, 1, 2, 3, 4), (5, 6, 7), (), (8, 9, 10)),
    ((0, 1), (2,), (3,), (4,), (5,), (6,), (7,), (8,)),
    ((0, 1), (2, 3), (4, 5), (6,)),
    ((0, 1, 2, 3, 4),),
)
EARLY = (2, 1, 1, 3)
STEPS = tuple(sum(len(g) for g in gs) for gs in GROUPS)
NORMS = (2, 1, 1, 2)
MAXES = (2, 1, 1, 1)
E0, HID0 = 8, 1024
TILES0 = (B * T - E0) // P + E0
STEPS0 = -(-B * T // P)
E1, HID1 = 8, 128
E2 = 8
NS, TOPS, DQ = 64, 8, 64
BY_CHUNK = (4, 3, 0, 1, 2)
SQUARES_AT = (0, 3, 6, 11, 15)
PHASES = 8
PLACED = 29
WORK = 24600


class Named:

    def __init__(self, **by_name):
        self.by_name = by_name

    def __getattr__(self, name):
        return self.by_name[name]


def signals(nc, ctx, phase, names):
    return Named(**{n: ctx.enter_context(nc.semaphore(f"{phase}_{n}")) for n in names.split()})


class Signal:

    def __init__(self, sem, before):
        self.sem, self.before = sem, before


def raised_by_attention(L):
    H, own_ctx = HEADS[L], L in (0, 3)
    per_batch = {"ln_ctx": 10 * own_ctx, "rstd_ctx": own_ctx, "ln_x": 4 * NORMS[L], "rstd_x": NORMS[L],
                 "proj": STEPS[L], "copied": STEPS[L], "mask_row": L == 0, "qk_rms": 4 * 5 * (L == 0), "rqk": 5 * (L == 0),
                 "scores": H, "maxed": MAXES[L] * H, "exped": H, "probs_turned": H, "probs_copied": H, "pv": H,
                 "o_scaled": 2, "o_turned": 1, "o_copied": 1, "valued": L == 3, "v_copied": L == 3, "out": 1, "resid": 2,
                 "x_stats": 1}
    counts = {n: B * int(c) for n, c in per_batch.items()}
    counts.update(ctx_in0=16 * B, ctx_in1=16 * B, mask_in0=8 * B * (L == 0), mask_in1=8 * B * (L == 0), cleared=1)
    return counts


def two_follow(t, more):
    return more and not (isinstance(t, int) and t == B - 2)


def wait_for(eng, signal, count):
    if isinstance(count, int) and count <= 0:
        return
    eng.wait_ge(signal.sem, signal.before + count)


def apart(eng):
    eng.nop(nofuse=True)


def wait_count(eng, sem, count):
    if isinstance(count, int) and count <= 0:
        return
    eng.wait_ge(sem, count)


def pipelined(eng, prepare, attend, finish, n=B):
    prepare(0, 0)
    attend(0, 0, True)
    attend(1, 1, True)
    with eng.Fori(1, n // 2 - 1) as i:
        attend(2 * i, 0, True)
        attend(2 * i + 1, 1, True)
    attend(n - 2, 0, True)
    attend(n - 1, 1, False)
    finish(n - 1, 1)


def in_turn(eng, one, n=B):
    one(0, 0)
    one(1, 1)
    with eng.Fori(1, n // 2) as i:
        one(2 * i, 0)
        one(2 * i + 1, 1)


def flamingo_kernel(nc, a, out):
    ctx = ExitStack()
    with ctx:
        def sb(name, shape, dt=F32):
            return ctx.enter_context(nc.sbuf_tensor(name, shape, dt))

        def ps(name, shape):
            return ctx.enter_context(nc.psum_tensor(name, shape, F32))

        X = sb("X", [P, B, D])
        ident = sb("ident", [P, P])
        gates = sb("gates", [P, 8])
        x_st6 = sb("x_st6", [P, B, 6])
        neg_half = sb("neg_half", [P, 32])
        work = sb("work", [P, WORK])
        bank = [ps(f"bank{i}", [P, 512]) for i in range(8)]

        class Area:

            def __init__(self):
                self.at = 0

            def take(self, *shape, dt=F32):
                n = 1
                for s in shape:
                    n *= s
                words = n if dt in (F32, U32, I32) else (n + 3) // 4
                v = work[:, self.at:self.at + words]
                self.at += words
                assert self.at <= WORK, self.at
                if dt != F32:
                    v = v.bitcast(dt)[:, 0:n]
                names = " ".join("abcd"[:len(shape)])
                sizes = {"abcd"[i]: s for i, s in enumerate(shape)}
                return v.rearrange(f"p ({names}) -> p {names}", **sizes)

        loads = []

        def resident(phase, name, chunks, parts=P):
            src = a[name]
            n = src.shape[-1]
            w = sb(name, [P, chunks, n])
            full = src.shape[0] // P
            if full:
                loads.append((phase, w[:, 0:full, :], src[0:full * P, :].rearrange("(c p) n -> p c n", p=P)))
            if src.shape[0] % P:
                loads.append((phase, w[0:src.shape[0] % P, full, :], src[full * P:, :]))
            return w

        def column(phase, name, chunks=1):
            w = sb(name, [P, chunks])
            loads.append((phase, w[:, :], a[name]))
            return w

        def row(phase, name):
            n = a[name].shape[0]
            w = sb(name, [P, n])
            loads.append((phase, w[:, :], a[name].rearrange("(o n) -> o n", o=1).broadcast_to([P, n])))
            return w

        wq = [resident(2 * L, n, 2) for L, n in enumerate(("L0_WqT", "L1_Wq", "L2_WqT", "L3_Wq"))]
        wk = [None] + [resident(2 * L, n, 2) for L, n in ((1, "L1_Wk"), (2, "L2_WkT"))]
        wk3 = resident(6, "L3_WkT", 2)
        wv = [None] + [resident(2 * L, n, 2) for L, n in ((1, "L1_Wv"), (2, "L2_WvT"), (3, "L3_Wv"))]
        wkv0 = resident(0, "L0_WkvT", 2)
        wlkv0 = resident(0, "L0_WlkvT", 2)
        wo = [resident(2 * L, n, 4 if L == 1 else 2) for L, n in enumerate(("L0_WoT", "L1_Wo", "L2_WoT", "L3_Wo"))]
        bo = [row(2 * L, f"L{L}_bo") for L in range(4)]
        ctx_gain = {0: column(0, "L0_ln_x_g", 2), 3: column(6, "L3_ln2_g", 2)}
        ctx_bias = {0: column(0, "L0_ln_x_b", 2), 3: column(6, "L3_ln2_b", 2)}
        x_gain = {0: column(0, "L0_ln_l_g", 2), 3: column(6, "L3_ln1_g", 2)}
        x_bias = {0: column(0, "L0_ln_l_b", 2), 3: column(6, "L3_ln1_b", 2)}
        q_gain = column(0, "L0_qn_g2")
        k_gain = column(0, "L0_kn_g2")
        bq3, bv3 = column(6, "L3_bq", 2), column(6, "L3_bv", 2)
        bq3s = sb("bq3_scaled", [P, 2])
        qg0s = sb("q_gain_scaled", [P, 1])

        earlier = resident(1, "earlier", 1)
        tile_starts = row(1, "tile_starts")
        tile_iota = row(1, "tile_iota")
        ones = sb("ones", [P, P])
        zeros = sb("zeros", [P, D])
        iota = row(1, "iota")
        ew0 = resident(1, "F0_router_w", 2)
        eb0 = row(1, "F0_router_b")
        ew1 = resident(3, "F1_Wr", 2)
        up1 = resident(3, "F1_up", 2)
        down1 = resident(3, "F1_down", 1 + E1)
        ew2 = resident(5, "F2_gateT", 2)
        lin2 = sb("F2_weight", [P, 2, E2, D])
        for c in range(2):
            loads.append((5, lin2[:, c, :, :], a["F2_weight"][:, c * P:(c + 1) * P, :].rearrange("e p n -> p e n")))

        start = signals(nc, ctx, "start", "x_loaded consts gates gates_done neg_half scaled zeros")
        loaded = [ctx.enter_context(nc.semaphore(f"weights_loaded_{p}")) for p in range(8)]
        n_loads = [0] * 8
        for p, _, _ in loads:
            n_loads[p] += 1
        ended = ctx.enter_context(nc.semaphore("phase_ended"))
        stored = ctx.enter_context(nc.semaphore("stored"))
        shared = signals(nc, ctx, "attn", " ".join(raised_by_attention(0)))
        at = []
        for L in range(4):
            before = {n: sum(raised_by_attention(k)[n] for k in range(L)) for n in raised_by_attention(0)}
            at.append(Named(**{n: Signal(sem, before[n]) for n, sem in shared.by_name.items()}))
        mx0 = signals(nc, ctx, "routed", "ln_x rstd_x x_turned x_copied logits route "
                      "xr_copied ranks places zeroed scattered rows_in0 rows_in1 w1_in0 w1_in1 w2_in0 w2_in1 rows_turned rows_copied value gate sigmoid hidden out "
                      "y_copied y_stored0 y_stored1 gathered resid")
        mx1 = signals(nc, ctx, "squared", "ln_x rstd_x x_turned x_copied logits route exped ones hidden relu squared masked "
                      "h_turned h_copied out resid")
        mx2 = signals(nc, ctx, "linear", "ln_x rstd_x x_turned x_copied logits route exped out combined resid")
        mx3 = signals(nc, ctx, "slots", "w_in consts const_sums ln_x rstd_x x_turned x_copied hidden gelu logits picked "
                      "exped alpha sums alpha_turned alpha_copied pooled pooled_turned pooled_copied gru_in rz_in rz_tanh "
                      "rz_done n_tanh slots_new s_turned s_copied qkv qk_copied v_done attn masked attn_exped attn_turned "
                      "attn_copied comm y_stats rstd_y y_normed y_turned y_copied values values_done mixed mixed_copied "
                      "out resid")

        area = Area()
        C = [area.take(NCH, DC) for _ in range(2)]
        CNorm = [area.take(NCH, DC) for _ in range(2)]
        CT = [area.take(2, NKP) for _ in range(2)]
        XN = [area.take(D) for _ in range(2)]
        XN2 = [area.take(D) for _ in range(2)]
        XT = [area.take(2, P) for _ in range(2)]
        QT = [area.take(4, T) for _ in range(2)]
        PR = [area.take(4, P) for _ in range(2)]
        PT = [area.take(4, T) for _ in range(2)]
        O = area.take(512)
        OT = area.take(4, T)
        RO = area.take(D)
        st6 = [area.take(4, 6) for _ in range(2)]
        mv = [area.take(4, 2) for _ in range(2)]
        rs = [area.take(4) for _ in range(2)]
        ss = [area.take(20) for _ in range(2)]
        rr = [area.take(20) for _ in range(2)]
        nmax = [area.take(1) for _ in range(2)]
        pmax = [area.take(1) for _ in range(2)]
        rsum = [area.take(8) for _ in range(2)]
        rinv = area.take(8)
        unused_by_3 = area.at
        QK = [area.take(5, D) for _ in range(2)]
        QKsq = area.take(5, D)
        KT = [area.take(2048) for _ in range(2)]
        V = [area.take(2048) for _ in range(2)]
        M8 = [area.take(NC, dt=U8) for _ in range(2)]
        MR = [area.take(4, P) for _ in range(2)]
        S_bank = (bank[0], bank[1])
        PT_bank = (bank[2], bank[3])
        O_bank = bank[4]
        R_bank = bank[5]
        J_bank = (bank[6], bank[7])

        area = Area()
        FX = [area.take(D) for _ in range(2)]
        FXT = [area.take(2, T) for _ in range(2)]
        Fmv, Frs = area.take(B, 2), area.take(B)
        LG = [area.take(8) for _ in range(2)]
        V8 = [area.take(8) for _ in range(2)]
        I8 = [area.take(8, dt=U32) for _ in range(2)]
        IF = [area.take(2) for _ in range(2)]
        ED = [area.take(6) for _ in range(2)]
        WF = [area.take(9) for _ in range(2)]
        WB = [area.take(8) for _ in range(2)]
        mixture = area.at
        XR0 = area.take(B, D)
        OH = area.take(B, E0)
        LGA, V8A, I8A = area.take(B, E0), area.take(B, 8), area.take(B, 8, dt=U32)
        I1 = area.take(B)
        CUM = [area.take(B, E0) for _ in range(2)]
        PLACE = area.take(B, E0)
        GT = area.take(E0, STEPS0)
        NT = [area.take(E0) for _ in range(4)]
        TE = area.take(TILES0, E0)
        TX = [area.take(TILES0) for _ in range(2)]
        TXI = area.take(TILES0, dt=I32)
        PF = area.take(B)
        PI = area.take(B, dt=I32)
        W1 = [area.take(2, 2 * HID0) for _ in range(2)]
        W2 = [area.take(HID0 // P, D) for _ in range(2)]
        B1 = [area.take(2 * HID0 // P) for _ in range(2)]
        B2 = [area.take(D) for _ in range(2)]
        TR = [area.take(D) for _ in range(2)]
        TT = [area.take(2, P) for _ in range(2)]
        SG = [area.take(P) for _ in range(2)]
        AC = area.take(HID0 // P, P)
        YR = [area.take(D) for _ in range(2)]
        area.at = mixture
        RL = [area.take(3 * HID1) for _ in range(3)]
        SQ = [area.take(3 * HID1) for _ in range(3)]
        HT = [area.take(3, T) for _ in range(3)]
        area.at = mixture
        ACC = area.take(D)
        area.at = mixture
        XS = area.take(B, D + 1)
        ML = area.take(B, NS)
        MEAN = area.take(2, 1)
        GH = area.take(3 * D)
        HG = [area.take(T) for _ in range(2)]
        LV = area.take(B, 8)
        pair = [Named(AL=area.take(2, NS), ALP=area.take(2, P), AS=area.take(2), AR=area.take(2),
                                ALT=area.take(T), DEN=area.take(1), SU=area.take(D), SUT=area.take(2, P),
                                at=area.at, RZ=area.take(2 * D), NN=area.take(D), S=area.take(D), ST=area.take(2, P),
                                QS=area.take(2, P), VS=area.take(D), AT=area.take(P), AX=area.take(1), AU=area.take(1),
                                AI=area.take(1), ATT=area.take(P), Y=area.take(D), y6=area.take(6), ymv=area.take(2),
                                yrs=area.take(1), YT=area.take(2, P), SV=area.take(D), MT=area.take(4, T))
                for _ in range(2)]
        LS, LR = [work[:, w.at:w.at + B * NS].rearrange("p (b n) -> p b n", b=B) for w in pair]
        assert area.at >= unused_by_3
        SI, SIT = area.take(D), area.take(2, P)
        SW1, SW2 = area.take(4, P), area.take(NS)
        SWih, SWhh, Sbih, Sbhh = area.take(2, 3 * D), area.take(2, 3 * D), area.take(3 * D), area.take(3 * D)
        SWq, SWk, SWv, SWvp, SWo = area.take(2, DQ), area.take(2, DQ), area.take(2, D), area.take(2, D), area.take(2, D)
        Sb1, Sb2, Sbq, Sbk = area.take(1), area.take(NS), area.take(1), area.take(1)
        Sbv, Sbvp, Sbo, Sg, Sb = area.take(D), area.take(D), area.take(D), area.take(2), area.take(2)
        BD = area.take(P)
        TAU = area.take(2)
        slot_loads = []
        for dst, n in ((SI, "slot_init2"), (Sb1, "b1"), (Sbq, "bq"), (Sbk, "bk"), (Sg, "ln_g"), (Sb, "ln_b"), (BD, "apart"),
                       (SW2, "w2")):
            slot_loads.append((dst, a["F3_" + n]))
        for dst, n in ((SIT, "slot_initT2"), (SW1, "w1"), (SWih, "WihT"), (SWhh, "WhhT"), (SWq, "wq"), (SWk, "wk"),
                       (SWv, "wv"), (SWvp, "wvp"), (SWo, "wo")):
            slot_loads.append((dst, a["F3_" + n].rearrange("(c p) n -> p c n", p=P)))
        for dst, n in ((Sbih, "bih"), (Sbhh, "bhh"), (Sb2, "b2"), (Sbv, "bv"), (Sbvp, "bvp"), (Sbo, "bo"), (TAU[:, 0:1], "tau")):
            src = a["F3_" + n]
            slot_loads.append((dst, src.rearrange("(o n) -> o n", o=1).broadcast_to([P, src.shape[0]])))

        def kt(L, j):
            m = 4 if L == 1 else 2
            return KT[j][:, 0:m * 512].rearrange("p (m n) -> p m n", m=m)

        def vv(L, j):
            n = 512 if L == 1 else 256
            return V[j][:, 0:CHUNKS[L] * n].rearrange("p (c n) -> p c n", n=n)

        def begin(eng, p):
            if p > 0:
                eng.wait_ge(ended, 4 * p)

        def end(eng):
            eng.drain().then_inc(ended, 1)

        sorted_x = nc.dram_tensor("sorted_x", (TILES0 * P, D), F32, kind="Internal").ap()
        sorted_y = nc.dram_tensor("sorted_y", (TILES0 * P, D), F32, kind="Internal").ap()

        block = ctx.enter_context(nc.Block())

        @block.sync
        def _(sp):
            sp.dma_start(gates[:, :], a["gates"].rearrange("(o n) -> o n", o=1).broadcast_to([P, 8])).then_inc(start.gates, 16)
            sp.dma_start(ident[:, :], a["ident"]).then_inc(start.consts, 16)

            def first_loads():
                sp.dma_start(X[0:T, :, :], a["x"].rearrange("b t d -> t b d")).then_inc(start.x_loaded, 16)
                for q, dst, src in loads:
                    if q == 0:
                        sp.dma_start(dst, src).then_inc(loaded[q], 16)

            def later_loads():
                sp.wait_ge(start.zeros, 2)
                sp.dma_start(sorted_x.rearrange("(i p) d -> p i d", p=P),
                             zeros[:, :].rearrange("p (o d) -> p o d", o=1).broadcast_to([P, TILES0, D])).then_inc(mx0.zeroed, 16)
                for q, dst, src in loads:
                    if q > 0:
                        sp.dma_start(dst, src).then_inc(loaded[q], 16)

            def load_slot_weights():
                for dst, src in slot_loads:
                    sp.dma_start(dst, src).then_inc(mx3.w_in, 16)

            def attention(L):
                s = at[L]
                begin(sp, 2 * L)
                if L in (0, 3):
                    wait_for(sp, s.cleared, 1)

                def load(t, j):
                    bt = bass.ds(t, 1)
                    if L in (0, 3):
                        wait_for(sp, s.ln_ctx, 10 * (t - 1))
                        apart(sp)
                        src = a["ctx"][bt, :, :]
                        sp.dma_start(C[j][:, 0:NCH - 1, :],
                                     src[:, 0:(NCH - 1) * P, :].rearrange("o (c p) d -> p (o c) d", p=P)
                                     ).then_inc((s.ctx_in0, s.ctx_in1)[j].sem, 16)
                        sp.dma_start(C[j][0:LAST, NCH - 1, :],
                                     src[:, (NCH - 1) * P:NC, :].rearrange("o p d -> p (o d)")
                                     ).then_inc((s.ctx_in0, s.ctx_in1)[j].sem, 16)
                        if L == 0:
                            wait_for(sp, s.mask_row, t - 1)
                            apart(sp)
                            sp.dma_start(M8[j][0:T, :], a["mask"][bt, :].broadcast_to([T, NC])
                                         ).then_inc((s.mask_in0, s.mask_in1)[j].sem, 16)
                    else:
                        wait_for(sp, s.proj, STEPS[L] * (t - 1))
                        apart(sp)
                        src = a["ctxT"][bt, :, :]
                        for c in range(2):
                            sp.dma_start(CT[j][0:CW[c], c, 0:NC],
                                         src[:, c * P:c * P + CW[c], :].rearrange("o p n -> p (o n)")
                                         ).then_inc((s.ctx_in0, s.ctx_in1)[j].sem, 16)

                load(0, 0)
                load(1, 1)
                if L == 0:
                    first_loads()
                if L == 3:
                    load_slot_weights()
                with sp.Fori(1, B // 2) as i:
                    load(2 * i, 0)
                    load(2 * i + 1, 1)
                if L == 0:
                    later_loads()


            def routed_experts():
                begin(sp, 1)
                s = mx0

                sp.wait_ge(s.places, PLACED)

                def load(i, j):
                    e = sp.value_load(TXI[0:1, bass.ds(i, 1)], min_val=0, max_val=E0 - 1)
                    one = bass.ds(e, 1)
                    wait_count(sp, s.hidden, 8 * (i - 1))
                    apart(sp)
                    for c in range(2):
                        sp.dma_start(W1[j][:, c, :], a["F0_w1"][one, c * P:(c + 1) * P, :].rearrange("o p n -> p (o n)")
                                     ).then_inc((s.w1_in0, s.w1_in1)[j], 16)
                    sp.dma_start(B1[j][:, :], a["F0_b1c"][one, :, :].rearrange("o p n -> p (o n)")
                                 ).then_inc((s.w1_in0, s.w1_in1)[j], 16)
                    if isinstance(i, int) and i == 0:
                        sp.wait_ge(s.scattered, 16 * B)
                    sp.dma_start(TR[j][:, :], sorted_x[bass.ds(i * P, P), :]).then_inc((s.rows_in0, s.rows_in1)[j], 16)
                    wait_count(sp, s.y_copied, i - 1)
                    apart(sp)
                    sp.dma_start(W2[j][:, :, :], a["F0_w2"][one, :, :].rearrange("o (c p) n -> p (o c) n", p=P)
                                 ).then_inc((s.w2_in0, s.w2_in1)[j], 16)
                    sp.dma_start(B2[j][:, :], a["F0_b2"][one, :].broadcast_to([P, D])).then_inc((s.w2_in0, s.w2_in1)[j], 16)

                def store(i, j):
                    sp.wait_ge(s.y_copied, i + 1)
                    apart(sp)
                    sp.dma_start(sorted_y[bass.ds(i * P, P), :], YR[j][:, :]
                                 ).then_inc((s.y_stored0, s.y_stored1)[j], 16)

                load(0, 0)
                load(1, 1)
                with sp.Fori(1, TILES0 // 2) as i:
                    for j in range(2):
                        load(2 * i + j, j)
                        store(2 * i + j - 2, j)
                store(TILES0 - 2, 0)
                store(TILES0 - 1, 1)

            def squared_experts():
                begin(sp, 3)

            def linear_experts():
                begin(sp, 5)

            def slot_mixer():
                begin(sp, 7)

            for p in range(PHASES):
                if p % 2 == 0:
                    attention(p // 2)
                else:
                    (routed_experts, squared_experts, linear_experts, slot_mixer)[p // 2]()
            begin(sp, PHASES)
            for p in range(PHASES):
                if n_loads[p]:
                    sp.wait_ge(loaded[p], 16 * n_loads[p])
            sp.dma_start(out.rearrange("b t d -> t b d"), X[0:T, :, :]).then_inc(stored, 16)
            sp.wait_ge(stored, 16)

        @block.gpsimd
        def _(pool):
            nc.gpsimd.memset(zeros[:, :], 0.0).then_inc(start.zeros, 1)
            nc.gpsimd.memset(ones[:, :], 1.0).then_inc(start.zeros, 1)
            nc.gpsimd.memset(neg_half[:, :], -0.5).then_inc(start.neg_half, 1)
            pool.wait_ge(start.neg_half, 1)

            def attention(L):
                s = at[L]
                begin(pool, 2 * L)
                def norms(t, j):
                    if L in (0, 3):
                        wait_for(pool, s.ln_ctx, 10 * t + 7)
                        nc.gpsimd.tensor_tensor(rs[j][:, 0:3], rs[j][:, 0:3], neg_half[:, 0:3], ALU.pow
                                                ).then_inc(s.rstd_ctx.sem, 1)
                    for k in range(NORMS[L]):
                        wait_for(pool, s.ln_x, 4 * (NORMS[L] * t + k) + 3)
                        nc.gpsimd.tensor_tensor(rs[j][0:T, 3:4], rs[j][0:T, 3:4], neg_half[0:T, 0:1], ALU.pow
                                                ).then_inc(s.rstd_x.sem, 1)

                def rms(t, j):
                    for n, k in enumerate(BY_CHUNK):
                        wait_for(pool, s.qk_rms, 20 * t + SQUARES_AT[n] + 3)
                        nc.gpsimd.tensor_tensor(rr[j][:, 4 * k:4 * k + 4], rr[j][:, 4 * k:4 * k + 4], neg_half[:, 0:4],
                                                ALU.pow).then_inc(s.rqk.sem, 1)

                norms(0, 0)
                norms(1, 1)
                if L == 0:
                    rms(0, 0)
                with pool.Fori(0, B // 2 - 1) as i:
                    for j in range(2):
                        norms(2 * i + j + 2, j)
                        if L == 0:
                            rms(2 * i + j + 1, 1 - j)
                if L == 0:
                    rms(B - 1, 1)
                end(pool)


            def rstd_x(s, p, last=True):
                begin(pool, p)
                pool.wait_ge(s.ln_x, B + 1)
                nc.gpsimd.tensor_tensor(Frs[0:T, :], Frs[0:T, :], neg_half[0:T, 0:B], ALU.pow).then_inc(s.rstd_x, 1)
                if last:
                    end(pool)

            def routed_experts():
                s = mx0
                rstd_x(s, 1, last=False)
                pool.wait_ge(s.places, PLACED)
                pool.wait_ge(s.zeroed, 16)
                for t in range(B):
                    nc.gpsimd.indirect_dma_start(sorted_x, bass.IndirectOffsetOnAxis(PI[0:T, t:t + 1], 0), XR0[0:T, t, :],
                                                 None).then_inc(s.scattered, 16)
                pool.wait_ge(s.scattered, 16 * B)
                pool.wait_ge(s.y_stored0, 8 * TILES0)
                pool.wait_ge(s.y_stored1, 8 * TILES0)
                for t in range(B):
                    nc.gpsimd.indirect_dma_start(XR0[0:T, t, :], None, sorted_y,
                                                 bass.IndirectOffsetOnAxis(PI[0:T, t:t + 1], 0)).then_inc(s.gathered, 16)
                end(pool)

            def squared_experts():
                rstd_x(mx1, 3)

            def linear_experts():
                rstd_x(mx2, 5)

            def slot_mixer():
                s = mx3
                rstd_x(s, 7, last=False)

                def one(u, k):
                    pool.wait_ge(s.y_stats, 4 * (u + 1))
                    nc.gpsimd.tensor_tensor(pair[k].yrs[:, :], pair[k].yrs[:, :], neg_half[:, 0:1], ALU.pow
                                            ).then_inc(s.rstd_y, 1)

                with pool.Fori(0, B // 4) as i:
                    one(2 * i, 0)
                    one(2 * i + 1, 1)
                end(pool)

            for p in range(PHASES):
                if p % 2 == 0:
                    attention(p // 2)
                else:
                    (routed_experts, squared_experts, linear_experts, slot_mixer)[p // 2]()

        @block.scalar
        def _(act):
            act.wait_ge(start.gates, 16)
            nc.scalar.activation(gates[:, :], gates[:, :], ACT.Tanh).then_inc(start.gates_done, 1)
            act.wait_ge(loaded[0], 16 * n_loads[0])
            nc.scalar.mul(qg0s[:, :], q_gain[:, :], HWID[0] ** -0.5).then_inc(start.scaled, 1)
            act.wait_ge(start.scaled, 1)

            def attention(L):
                s = at[L]
                H, W, NK = HEADS[L], HWID[L], KEYS[L]
                scale = float(W) ** -0.5
                begin(act, 2 * L)
                wait_for(act, s.cleared, 1)
                if L == 3:
                    act.wait_ge(loaded[6], 16 * n_loads[6])
                    nc.scalar.mul(bq3s[:, :], bq3[:, :], scale).then_inc(start.scaled, 1)
                    act.wait_ge(start.scaled, 2)

                def step(t, j, n):
                    src = J_bank[(j * STEPS[L] + n) % 2]
                    wait_for(act, s.proj, STEPS[L] * t + n + 1)
                    if L == 3:
                        if n == 0:
                            for c in range(2):
                                ins = nc.scalar.activation(XT[j][:, c, 0:T], src[:, c * T:(c + 1) * T], ACT.Identity,
                                                           bias=x_bias[3][:, c:c + 1], scale=x_gain[3][:, c:c + 1])
                        elif n in (1, 2):
                            c, m = n - 1, CW[n - 1]
                            ins = nc.scalar.activation(CT[j][0:m, c, :], src[0:m, 0:NKP], ACT.Identity,
                                                       bias=ctx_bias[3][0:m, c:c + 1], scale=ctx_gain[3][0:m, c:c + 1])
                        elif n == 3:
                            for m in range(2):
                                ins = nc.scalar.activation(QT[j][:, m, :], src[:, m * T:(m + 1) * T], ACT.Identity,
                                                           bias=bq3s[:, m:m + 1], scale=scale)
                        else:
                            nc.scalar.copy(QT[j][:, 2, :], src[:, 0:T])
                            ins = nc.scalar.copy(QT[j][0:CW[1] + 1, 3, :], src[0:CW[1] + 1, T:2 * T])
                    elif L == 0:
                        if n in (0, 1):
                            m = CW[n]
                            ins = nc.scalar.activation(CT[j][0:m, n, :], src[0:m, 0:NKP], ACT.Identity,
                                                       bias=ctx_bias[0][0:m, n:n + 1], scale=ctx_gain[0][0:m, n:n + 1])
                        elif n == 2:
                            for c in range(2):
                                ins = nc.scalar.activation(XT[j][:, c, 0:T], src[:, c * T:(c + 1) * T], ACT.Identity,
                                                           bias=x_bias[0][:, c:c + 1], scale=x_gain[0][:, c:c + 1])
                        elif n in (4, 5, 6, 7):
                            k = BY_CHUNK[n - 3]
                            nc.scalar.copy(QK[j][:, k, :], src[:, 0:D])
                            ins = nc.scalar.copy(vv(0, j)[:, k, :], src[:, D:2 * D])
                        elif n == 3:
                            ins = nc.scalar.copy(QK[j][0:T, 4, :], src[0:T, 0:D])
                        elif n in (8, 9):
                            ins = nc.scalar.mul(kt(0, j)[:, n - 8, :], src[:, :], k_gain[:, 0:1])
                        else:
                            ins = nc.scalar.mul(QT[j][:, 0:2, :], src[:, 0:2 * T].rearrange("p (m t) -> p m t", m=2),
                                                qg0s[:, 0:1])
                    else:
                        MQ = 4 if L == 1 else 2
                        if n == 0:
                            ins = nc.scalar.copy(XT[j][:, :, 0:T], src[:, 0:2 * T].rearrange("p (c t) -> p c t", c=2))
                        elif n == 1:
                            ins = nc.scalar.mul(QT[j][:, 0:MQ, :], src[:, 0:MQ * T].rearrange("p (m t) -> p m t", m=MQ),
                                                scale)
                        elif n < 2 + MQ:
                            ins = nc.scalar.copy(kt(L, j)[:, n - 2, 0:NC], src[:, 0:NC])
                        else:
                            ins = nc.scalar.copy(vv(L, j)[:, n - 2 - MQ, :], src[:, 0:(512 if L == 1 else 256)])
                    ins.then_inc(s.copied.sem, 1)

                def exp(t, j, h):
                    n = H * t + h
                    k = (H * j + h) % 2
                    wait_for(act, s.maxed, MAXES[L] * (n + 1))
                    wait_for(act, s.probs_turned, n - 1)
                    pr = PR[k][0:T, :, :].rearrange("p c n -> p (c n)")
                    nc.scalar.activation(pr[:, 0:NK], S_bank[k][0:T, 0:NK], ACT.Exp, bias=nmax[k][0:T, :],
                                         accum_out=rsum[j][0:T, h:h + 1]).then_inc(s.exped.sem, 1)

                def o_copy(t, j):
                    wait_for(act, s.o_turned, t + 1)
                    wait_for(act, s.out, t)
                    if L == 3:
                        for c in range(2):
                            m = CW[c]
                            ins = nc.scalar.activation(OT[0:m, c, :], R_bank[0:m, c * T:(c + 1) * T], ACT.Identity,
                                                       bias=ctx_bias[3][0:m, c:c + 1], scale=ctx_gain[3][0:m, c:c + 1])
                        ins.then_inc(s.o_copied.sem, 1)
                    else:
                        m = 4 if L == 1 else 2
                        nc.scalar.copy(OT[:, 0:m, :], R_bank[:, 0:m * T].rearrange("p (m t) -> p m t", m=m)
                                       ).then_inc(s.o_copied.sem, 1)

                def v_copy(t, j):
                    wait_for(act, s.valued, t + 1)
                    for m in range(2):
                        ins = nc.scalar.activation(OT[:, 2 + m, :], R_bank[:, m * T:(m + 1) * T], ACT.Identity,
                                                   bias=bv3[:, m:m + 1])
                    ins.then_inc(s.v_copied.sem, 1)

                def prepare(t, j):
                    for n in range(STEPS[L]):
                        step(t, j, n)

                def attend(t, j, more):
                    started = not (isinstance(t, int) and t == 0)
                    if L == 3:
                        if started:
                            o_copy(t - 1, 1 - j)
                        if more:
                            step(t + 1, 1 - j, 0)
                        exp(t, j, 0)
                        if started:
                            v_copy(t - 1, 1 - j)
                    else:
                        exp(t, j, 0)
                        exp(t, j, 1)
                        if started:
                            o_copy(t - 1, 1 - j)
                    for h in range(H):
                        for n in GROUPS[L][h]:
                            if more and not (L == 3 and n == 0):
                                step(t + 1, 1 - j, n)
                        if h + 2 < H:
                            exp(t, j, h + 2)

                def finish(t, j):
                    o_copy(t, j)
                    if L == 3:
                        v_copy(t, j)

                pipelined(act, prepare, attend, finish)
                end(act)


            def x_copy(s, t, j):
                act.wait_ge(s.x_turned, t + 1)
                nc.scalar.copy(FXT[j][:, :, :], bank[0][:, 0:2 * T].rearrange("p (c t) -> p c t", c=2)
                               ).then_inc(s.x_copied, 1)

            def exp_difference(s, n_route, t, j):
                act.wait_ge(s.route, n_route * t + 4)
                nc.scalar.activation(ED[j][0:T, 1:2], ED[j][0:T, 0:1], ACT.Exp).then_inc(s.exped, 1)

            def routed_experts():
                s = mx0
                begin(act, 1)
                act.wait_ge(loaded[1], 16 * n_loads[1])

                in_turn(act, lambda t, j: x_copy(s, t, j))

                def rows_copy(i, j):
                    act.wait_ge(s.rows_turned, i + 1)
                    nc.scalar.copy(TT[j][:, :, :], bank[0][:, 0:2 * P].rearrange("p (c t) -> p c t", c=2)
                                   ).then_inc(s.rows_copied, 1)

                def tile(i, j, more):
                    for f in range(HID0 // P):
                        n = 8 * i + f
                        act.wait_ge(s.gate, n + 1)
                        wait_count(act, s.hidden, n - 1)
                        nc.scalar.activation(SG[f % 2][:, :], bank[2 + f % 2][:, 0:P], ACT.Sigmoid,
                                             bias=B1[j][:, 8 + f:9 + f]).then_inc(s.sigmoid, 1)
                    if more:
                        rows_copy(i + 1, 1 - j)

                pipelined(act, rows_copy, tile, lambda i, j: None, TILES0)
                end(act)

            def squared_experts():
                s = mx1
                begin(act, 3)

                def hidden(t, j, g):
                    act.wait_ge(s.hidden, 3 * t + g + 1)
                    nc.scalar.activation(RL[g][0:T, :], bank[2 + g][0:T, 0:3 * HID1], ACT.Relu).then_inc(s.relu, 1)
                    act.wait_ge(s.relu, 3 * t + g + 1)
                    nc.scalar.square(SQ[g][0:T, :], RL[g][0:T, :]).then_inc(s.squared, 1)

                def prepare(t, j):
                    x_copy(s, 0, 0)
                    x_copy(s, 1, 1)
                    exp_difference(s, 9, 0, 0)
                    for g in range(3):
                        hidden(0, 0, g)

                def attend(t, j, more):
                    if more:
                        exp_difference(s, 9, t + 1, 1 - j)
                    for g in range(3):
                        if g == 2 and two_follow(t, more):
                            x_copy(s, t + 2, j)
                        if more:
                            hidden(t + 1, 1 - j, g)

                pipelined(act, prepare, attend, lambda t, j: None)
                end(act)

            def linear_experts():
                s = mx2
                begin(act, 5)

                def prepare(t, j):
                    x_copy(s, 0, 0)
                    x_copy(s, 1, 1)
                    exp_difference(s, 11, 0, 0)

                def attend(t, j, more):
                    if more:
                        exp_difference(s, 11, t + 1, 1 - j)
                    if two_follow(t, more):
                        x_copy(s, t + 2, j)

                pipelined(act, prepare, attend, lambda t, j: None)
                end(act)

            def slot_mixer():
                s = mx3
                begin(act, 7)
                act.wait_ge(s.w_in, 16 * len(slot_loads))

                def prepare(t, j):
                    x_copy(s, t, j)

                def attend(t, j, more):
                    act.wait_ge(s.hidden, t + 1)
                    if isinstance(t, int) and t == 0:
                        act.wait_ge(s.consts, 9)
                    nc.scalar.activation(HG[j][:, :], bank[1 + j][:, 0:T], ACT.Gelu, bias=Sb1[:, 0:1]).then_inc(s.gelu, 1)
                    if more:
                        prepare(t + 1, 1 - j)

                pipelined(act, prepare, attend, lambda t, j: None)

                def weights(u, k):
                    w = pair[k]
                    for m in range(2):
                        ins = nc.scalar.activation(w.AL[0:T, m, :], ML[0:T, bass.ds(2 * u + m, 1), :], ACT.Exp,
                                                   accum_out=w.AS[0:T, m:m + 1])
                    ins.then_inc(s.exped, 1)

                def pooled(u, k):
                    act.wait_ge(s.pooled_turned, u + 1)
                    nc.scalar.copy(pair[k].SUT[:, :, :], bank[4 * k][:, 0:2 * P].rearrange("p (c n) -> p c n", c=2)
                                   ).then_inc(s.pooled_copied, 1)

                def rz_tanh(u, k):
                    act.wait_ge(s.rz_in, 2 * u + 1)
                    nc.scalar.activation(pair[k].RZ[:, :], pair[k].RZ[:, :], ACT.Tanh, scale=0.5).then_inc(s.rz_tanh, 1)

                def n_tanh(u, k):
                    act.wait_ge(s.rz_done, 3 * (u + 1))
                    nc.scalar.activation(pair[k].NN[:, :], pair[k].NN[:, :], ACT.Tanh).then_inc(s.n_tanh, 1)

                def slots_copy(u, k):
                    act.wait_ge(s.s_turned, u + 1)
                    nc.scalar.copy(pair[k].ST[:, :, :], bank[4 * k][:, 0:2 * P].rearrange("p (c n) -> p c n", c=2)
                                   ).then_inc(s.s_copied, 1)

                def qk_copy(u, k):
                    act.wait_ge(s.qkv, u + 1)
                    for m, b in ((0, Sbq), (1, Sbk)):
                        ins = nc.scalar.activation(pair[k].QS[0:DQ, m, :], bank[4 * k + 1][0:DQ, m * P:(m + 1) * P],
                                                   ACT.Identity, bias=b[0:DQ, 0:1])
                    ins.then_inc(s.qk_copied, 1)

                def attn_exp(u, k):
                    act.wait_ge(s.masked, 2 * (u + 1))
                    nc.scalar.activation(pair[k].AT[:, :], pair[k].AT[:, :], ACT.Exp, bias=pair[k].AX[:, 0:1],
                                         accum_out=pair[k].AU[:, 0:1]).then_inc(s.attn_exped, 1)

                def y_copy(u, k):
                    act.wait_ge(s.y_turned, u + 1)
                    for c in range(2):
                        ins = nc.scalar.activation(pair[k].YT[:, c, :], bank[4 * k][:, c * P:(c + 1) * P], ACT.Identity,
                                                   bias=Sb[:, c:c + 1], scale=Sg[:, c:c + 1])
                    ins.then_inc(s.y_copied, 1)

                def mixed_copy(u, k):
                    act.wait_ge(s.mixed, u + 1)
                    for m in range(2):
                        ins = nc.scalar.copy(pair[k].MT[:, 2 * m:2 * m + 2, :],
                                             bank[4 * k + 3 * (1 - m)][:, 0:2 * T].rearrange("p (c t) -> p c t", c=2))
                    ins.then_inc(s.mixed_copied, 1)

                act.wait_ge(s.picked, 4 * B + 4)
                with act.Fori(0, B // 4) as i:
                    for stage in (weights, pooled, rz_tanh, n_tanh, slots_copy, qk_copy, attn_exp, y_copy, mixed_copy):
                        stage(2 * i, 0)
                        stage(2 * i + 1, 1)
                end(act)

            for p in range(PHASES):
                if p % 2 == 0:
                    attention(p // 2)
                else:
                    (routed_experts, squared_experts, linear_experts, slot_mixer)[p // 2]()

        @block.vector
        def _(dve):
            def x_in():
                dve.wait_ge(start.x_loaded, 16)
                dve.wait_ge(start.gates_done, 1)

            def attention(L):
                s = at[L]
                H, W, NK, CH = HEADS[L], HWID[L], KEYS[L], CHUNKS[L]
                begin(dve, 2 * L)
                for j in range(2):
                    if L in (0, 3):
                        nc.vector.memset(C[j][96:P, NCH - 1, :], 0.0)
                    if L == 0:
                        nc.vector.memset(XT[j][:, :, T:P], 0.0)
                        nc.vector.memset(QK[j][96:P, 4, :], 1.0)
                        nc.vector.memset(MR[j][0:T, NCH - 1, LAST:P], FAR)
                        nc.vector.memset(MR[j][0:T, NCH, 0:T], 0.0)
                        nc.vector.memset(MR[j][0:T, NCH, T:P], FAR)
                    if L in (1, 2):
                        nc.vector.memset(CT[j][:, :, NC:NKP], 0.0)
                    if L == 3:
                        nc.vector.memset(CT[j][CW[1]:CW[1] + 1, 1, :], 1.0)
                    if L > 0:
                        nc.vector.memset(PR[j][0:T, NCH - 1, LAST:P], 0.0)
                dve.drain().then_inc(s.cleared.sem, 1)
                wait_for(dve, s.cleared, 1)
                if L > 0:
                    dve.wait_ge(loaded[2 * L], 16 * n_loads[2 * L])

                def ln_ctx_stats(t, j):
                    wait_for(dve, (s.ctx_in0, s.ctx_in1)[j], 32 * (t // 2 + 1))
                    b = 10 * t
                    for c in range(NCH):
                        nc.vector.bn_stats(st6[j][:, c, :], C[j][:, c, :]).then_inc(s.ln_ctx.sem, 1)
                    wait_for(dve, s.ln_ctx, b + 3)
                    apart(dve)
                    for c in range(NCH):
                        nc.vector.bn_aggr(mv[j][:, c, :], st6[j][:, c, :]).then_inc(s.ln_ctx.sem, 1)
                    wait_for(dve, s.ln_ctx, b + 6)
                    nc.vector.tensor_scalar(rs[j][:, 0:3], mv[j][:, 0:3, 1], LN_EPS, None, ALU.add).then_inc(s.ln_ctx.sem, 1)

                def ln_ctx_norm(t, j):
                    wait_for(dve, s.rstd_ctx, t + 1)
                    for c in range(NCH):
                        nc.vector.tensor_scalar(CNorm[j][:, c, :], C[j][:, c, :], mv[j][:, c, 0:1], rs[j][:, c:c + 1],
                                                ALU.subtract, ALU.mult).then_inc(s.ln_ctx.sem, 1)

                def ln_x(t, j, k):
                    b = 4 * (NORMS[L] * t + k)
                    src = X[0:T, bass.ds(t, 1), :] if k == 0 else XN[j][0:T, :]
                    if L == 0 and k == 0 and isinstance(t, int) and t == 0:
                        x_in()
                        dve.wait_ge(loaded[0], 16 * n_loads[0])
                    if k:
                        wait_for(dve, s.ln_x, b)
                    nc.vector.bn_stats(st6[j][0:T, 3, :], src).then_inc(s.ln_x.sem, 1)
                    wait_for(dve, s.ln_x, b + 1)
                    apart(dve)
                    nc.vector.bn_aggr(mv[j][0:T, 3, :], st6[j][0:T, 3, :]).then_inc(s.ln_x.sem, 1)
                    wait_for(dve, s.ln_x, b + 2)
                    nc.vector.tensor_scalar(rs[j][0:T, 3:4], mv[j][0:T, 3, 1:2], LN_EPS, None, ALU.add).then_inc(s.ln_x.sem, 1)

                def ln_x_norm(t, j, k):
                    src = X[0:T, bass.ds(t, 1), :] if k == 0 else XN[j][0:T, :]
                    dst = XN[j] if k == 0 else XN2[j]
                    wait_for(dve, s.rstd_x, NORMS[L] * t + k + 1)
                    nc.vector.tensor_scalar(dst[0:T, :], src, mv[j][0:T, 3, 0:1], rs[j][0:T, 3:4],
                                            ALU.subtract, ALU.mult).then_inc(s.ln_x.sem, 1)

                def mask_row(t, j):
                    wait_for(dve, (s.mask_in0, s.mask_in1)[j], 16 * (t // 2 + 1))
                    mr = MR[j][0:T, :, :].rearrange("p c n -> p (c n)")
                    nc.vector.tensor_scalar(mr[:, 0:NC], M8[j][0:T, :], -FAR, FAR, ALU.mult, ALU.add
                                            ).then_inc(s.mask_row.sem, 1)

                def rms(t, j, n):
                    wait_for(dve, s.copied, STEPS[L] * t + 4 + n)
                    b = 20 * t + SQUARES_AT[n]
                    k = BY_CHUNK[n]
                    cols = slice(4 * k, 4 * k + 4)
                    nc.vector.tensor_tensor(QKsq[:, k, :], QK[j][:, k, :], QK[j][:, k, :], ALU.mult).then_inc(s.qk_rms.sem, 1)
                    wait_for(dve, s.qk_rms, b + 1)
                    nc.vector.reduce_sum(ss[j][:, cols], QKsq[:, k, :].rearrange("p (h w) -> p h w", w=W), axis=AXX
                                         ).then_inc(s.qk_rms.sem, 1)
                    wait_for(dve, s.qk_rms, b + 2)
                    nc.vector.tensor_scalar(rr[j][:, cols], ss[j][:, cols], 1.0 / W, 1e-16, ALU.mult, ALU.max
                                            ).then_inc(s.qk_rms.sem, 1)

                def rms_scale(t, j, n):
                    wait_for(dve, s.rqk, 5 * t + n + 1)
                    k = BY_CHUNK[n]
                    v = QK[j][:, k, :].rearrange("p (h w) -> p h w", w=W)
                    r = rr[j][:, 4 * k:4 * k + 4].rearrange("p (n o) -> p n o", o=1).broadcast_to([P, 4, W])
                    nc.vector.tensor_tensor(v, v, r, ALU.mult).then_inc(s.qk_rms.sem, 1)

                def maximum(t, j, h):
                    n = H * t + h
                    k = (H * j + h) % 2
                    wait_for(dve, s.scores, n + 1)
                    if L == 0:
                        if h == 0:
                            wait_for(dve, s.mask_row, t + 1)
                        sc = S_bank[k][0:T, 0:NK]
                        apart(dve)
                        nc.vector.tensor_tensor_reduce(out=sc, in0=sc, in1=MR[j][0:T, :, :].rearrange("p c n -> p (c n)"),
                                                       scale=1.0, scalar=-3.0e38, op0=ALU.add, op1=ALU.max,
                                                       accum_out=pmax[k][0:T, :]).then_inc(s.maxed.sem, 1)
                        wait_for(dve, s.maxed, 2 * n + 1)
                        nc.vector.tensor_scalar(nmax[k][0:T, :], pmax[k][0:T, :], -1.0, None, ALU.mult).then_inc(s.maxed.sem, 1)
                    else:
                        nc.vector.tensor_reduce(nmax[k][0:T, :], S_bank[k][0:T, 0:NK], axis=AXX, op=ALU.max,
                                                negate=True).then_inc(s.maxed.sem, 1)

                def probs_copy(t, j, h):
                    n = H * t + h
                    k = (H * j + h) % 2
                    wait_for(dve, s.probs_turned, n + 1)
                    wait_for(dve, s.pv, n - 1)
                    nc.vector.tensor_copy(PT[k][:, 0:CH, :], PT_bank[k][:, 0:CH * T].rearrange("p (c t) -> p c t", c=CH)
                                          ).then_inc(s.probs_copied.sem, 1)

                def o_scale(t, j):
                    wait_for(dve, s.pv, H * (t + 1))
                    wait_for(dve, s.o_turned, t)
                    nc.vector.reciprocal(rinv[0:T, 0:H], rsum[j][0:T, 0:H]).then_inc(s.o_scaled.sem, 1)
                    wait_for(dve, s.o_scaled, 2 * t + 1)
                    if H == 1:
                        nc.vector.tensor_scalar(O[0:T, 0:DC], O_bank[0:T, 0:DC], rinv[0:T, 0:1], None, ALU.mult
                                                ).then_inc(s.o_scaled.sem, 1)
                    else:
                        nc.vector.tensor_tensor(O[0:T, 0:H * W].rearrange("p (h w) -> p h w", h=H),
                                                O_bank[0:T, 0:H * W].rearrange("p (h w) -> p h w", h=H),
                                                rinv[0:T, 0:H].rearrange("p (h o) -> p h o", o=1).broadcast_to([T, H, W]),
                                                ALU.mult).then_inc(s.o_scaled.sem, 1)

                def residual(t, j):
                    wait_for(dve, s.out, t + 1)
                    nc.vector.tensor_tensor(RO[0:T, :], R_bank[0:T, 0:D], bo[L][0:T, :], ALU.add).then_inc(s.resid.sem, 1)
                    wait_for(dve, s.resid, 2 * t + 1)
                    xt = X[0:T, bass.ds(t, 1), :].rearrange("p o d -> p (o d)")
                    nc.vector.scalar_tensor_tensor(xt, RO[0:T, :], gates[0:T, L:L + 1], xt, ALU.mult, ALU.add
                                                   ).then_inc(s.resid.sem, 1)
                    wait_for(dve, s.resid, 2 * t + 2)
                    apart(dve)
                    nc.vector.bn_stats(x_st6[0:T, bass.ds(t, 1), :].rearrange("p o n -> p (o n)"), xt).then_inc(s.x_stats.sem, 1)

                def norms(t, j):
                    if L in (0, 3):
                        ln_ctx_stats(t, j)
                    ln_x(t, j, 0)
                    if L == 0 or (L == 3 and isinstance(t, int) and t == 0):
                        ln_ctx_norm(t, j)
                    ln_x_norm(t, j, 0)
                    if NORMS[L] == 2:
                        ln_x(t, j, 1)
                        ln_x_norm(t, j, 1)

                def rms_1(t, j):
                    rms(t, j, 0)
                    rms(t, j, 1)

                def rms_2(t, j):
                    rms(t, j, 2)
                    rms_scale(t, j, 0)
                    rms_scale(t, j, 1)
                    rms(t, j, 3)
                    rms_scale(t, j, 2)
                    rms(t, j, 4)
                    rms_scale(t, j, 3)

                def rms_3(t, j):
                    rms_scale(t, j, 4)

                rms_parts = (rms_1, rms_2, rms_3)

                def prepare(t, j):
                    norms(0, 0)
                    norms(1, 1)
                    if L == 0:
                        mask_row(0, 0)
                        mask_row(1, 1)
                        for part in rms_parts:
                            part(0, 0)

                def attend(t, j, more):
                    two_more = two_follow(t, more)
                    maximum(t, j, 0)
                    if H > 1:
                        maximum(t, j, 1)
                    if L == 3 and more:
                        wait_for(dve, s.pv, t)
                        ln_ctx_norm(t + 1, 1 - j)
                    if two_more:
                        norms(t + 2, j)
                    for h in range(H):
                        probs_copy(t, j, h)
                        if h + 2 < H:
                            maximum(t, j, h + 2)
                        if h == 0 and not (isinstance(t, int) and t == 0):
                            residual(t - 1, 1 - j)
                        if L == 0 and more and h < 3:
                            rms_parts[h](t + 1, 1 - j)
                    if L == 0 and two_more:
                        mask_row(t + 2, j)
                    o_scale(t, j)

                pipelined(dve, prepare, attend, residual)
                end(dve)


            def x_stats(s, L):
                wait_for(dve, at[L].x_stats, B)
                for t in range(B):
                    nc.vector.bn_aggr(Fmv[0:T, t, :], x_st6[0:T, t, :]).then_inc(s.ln_x, 1)
                dve.wait_ge(s.ln_x, B)
                nc.vector.tensor_scalar(Frs[0:T, :], Fmv[0:T, :, 1], LN_EPS, None, ALU.add).then_inc(s.ln_x, 1)
                dve.wait_ge(s.rstd_x, 1)

            def x_norm(s, t, j):
                wait_count(dve, s.x_turned, t - 1)
                nc.vector.tensor_scalar(FX[j][0:T, :], X[0:T, bass.ds(t, 1), :].rearrange("p o d -> p (o d)"),
                                        Fmv[0:T, bass.ds(t, 1), 0:1].rearrange("p o n -> p (o n)"),
                                        Frs[0:T, bass.ds(t, 1)], ALU.subtract, ALU.mult).then_inc(s.ln_x, 1)

            def choose(s, n, t, j, bias=None):
                b = n * t
                dve.wait_ge(s.logits, t + 1)
                if bias is None:
                    nc.vector.tensor_copy(LG[j][0:T, :], bank[1][0:T, 0:8]).then_inc(s.route, 1)
                else:
                    nc.vector.tensor_tensor(LG[j][0:T, :], bank[1][0:T, 0:8], bias[0:T, :], ALU.add).then_inc(s.route, 1)
                dve.wait_ge(s.route, b + 1)
                apart(dve)
                nc.vector.max(V8[j][0:T, :], LG[j][0:T, :]).then_inc(s.route, 1)
                dve.wait_ge(s.route, b + 2)
                apart(dve)
                nc.vector.max_index(I8[j][0:T, :], V8[j][0:T, :], LG[j][0:T, :]).then_inc(s.route, 1)
                nc.vector.tensor_tensor(ED[j][0:T, 0:1], V8[j][0:T, 1:2], V8[j][0:T, 0:1], ALU.subtract).then_inc(s.route, 1)
                dve.wait_ge(s.route, b + 3)
                nc.vector.tensor_copy(IF[j][0:T, :], I8[j][0:T, 0:2]).then_inc(s.route, 1)

            def first_weight(s, n, t, j):
                dve.wait_ge(s.exped, t + 1)
                nc.vector.tensor_scalar(ED[j][0:T, 2:3], ED[j][0:T, 1:2], 1.0, None, ALU.add).then_inc(s.route, 1)
                dve.wait_ge(s.route, n * t + 6)
                nc.vector.reciprocal(ED[j][0:T, 3:4], ED[j][0:T, 2:3]).then_inc(s.route, 1)
                dve.wait_ge(s.route, n * t + 7)

            def routed_experts():
                s = mx0
                begin(dve, 1)
                dve.wait_ge(loaded[1], 16 * n_loads[1])

                x_stats(s, 0)

                def prepare(t, j):
                    x_norm(s, t, j)
                    dve.wait_ge(s.ln_x, B + 1 + t + 1)
                    nc.vector.tensor_copy(XR0[0:T, bass.ds(t, 1), :].rearrange("p o d -> p (o d)"), FX[j][0:T, :]
                                          ).then_inc(s.xr_copied, 1)

                def attend(t, j, more):
                    if more:
                        prepare(t + 1, 1 - j)
                    dve.wait_ge(s.logits, t + 1)
                    nc.vector.tensor_tensor(LGA[0:T, bass.ds(t, 1), :].rearrange("p o e -> p (o e)"), bank[1][0:T, 0:E0],
                                            eb0[0:T, :], ALU.add).then_inc(s.route, 1)

                pipelined(dve, prepare, attend, lambda t, j: None)
                dve.wait_ge(s.route, B)
                for t in range(B):
                    nc.vector.max(V8A[0:T, t, :], LGA[0:T, t, :]).then_inc(s.route, 1)
                dve.wait_ge(s.route, 2 * B)
                for t in range(B):
                    nc.vector.max_index(I8A[0:T, t, :], V8A[0:T, t, :], LGA[0:T, t, :]).then_inc(s.route, 1)
                dve.wait_ge(s.route, 3 * B)
                nc.vector.tensor_copy(I1[0:T, :], I8A[0:T, :, 0]).then_inc(s.route, 1)
                dve.wait_ge(s.route, 3 * B + 1)
                nc.vector.tensor_tensor(OH[0:T, :, :], iota[0:T, :].rearrange("p (o e) -> p o e", o=1).broadcast_to([T, B, E0]),
                                        I1[0:T, :].rearrange("p (b o) -> p b o", o=1).broadcast_to([T, B, E0]),
                                        ALU.is_equal).then_inc(s.route, 1)

                def wide(v, dims):
                    return v.broadcast_to([P, *dims])

                dve.wait_ge(s.ranks, 1)
                dve.wait_ge(s.route, 3 * B + 2)
                nc.vector.tensor_copy(CUM[0][:, :, :], bank[3][:, 0:B * E0].rearrange("p (b e) -> p b e", b=B)
                                      ).then_inc(s.places, 1)
                n = 1
                for k, d in enumerate((1, 2, 4, 8)):
                    src, dst = CUM[k % 2], CUM[1 - k % 2]
                    dve.wait_ge(s.places, n)
                    nc.vector.tensor_copy(dst[:, 0:d, :], src[:, 0:d, :]).then_inc(s.places, 1)
                    nc.vector.tensor_tensor(dst[:, d:B, :], src[:, d:B, :], src[:, 0:B - d, :], ALU.add).then_inc(s.places, 1)
                    n += 2
                dve.wait_ge(s.places, 9)
                nc.vector.tensor_tensor(GT[:, :, :], wide(CUM[0][:, B - 1:B, :].rearrange("p o e -> p e o"), (E0, STEPS0)),
                                        wide(tile_starts[:, :].rearrange("p (o k) -> p o k", o=1), (E0, STEPS0)),
                                        ALU.is_gt).then_inc(s.places, 1)
                dve.wait_ge(s.places, 10)
                nc.vector.reduce_sum(NT[0][:, :], GT[:, :, :], axis=AXX).then_inc(s.places, 1)
                n = 11
                for k, d in enumerate((1, 2, 4)):
                    src, dst = NT[k], NT[k + 1]
                    dve.wait_ge(s.places, n)
                    nc.vector.tensor_copy(dst[:, 0:d], src[:, 0:d]).then_inc(s.places, 1)
                    nc.vector.tensor_tensor(dst[:, d:E0], src[:, d:E0], src[:, 0:E0 - d], ALU.add).then_inc(s.places, 1)
                    n += 2
                dve.wait_ge(s.places, 17)
                nc.vector.tensor_tensor(TE[:, :, :], wide(NT[3][:, :].rearrange("p (o e) -> p o e", o=1), (TILES0, E0)),
                                        wide(tile_iota[:, :].rearrange("p (i o) -> p i o", o=1), (TILES0, E0)),
                                        ALU.is_le).then_inc(s.places, 1)
                nc.vector.tensor_tensor(NT[1][:, :], NT[3][:, :], NT[0][:, :], ALU.subtract).then_inc(s.places, 1)
                nc.vector.tensor_tensor(CUM[1][:, :, :], CUM[0][:, :, :], bank[3][:, 0:B * E0].rearrange("p (b e) -> p b e", b=B),
                                        ALU.subtract).then_inc(s.places, 1)
                dve.wait_ge(s.places, 20)
                nc.vector.reduce_sum(TX[0][:, :], TE[:, :, :], axis=AXX).then_inc(s.places, 1)
                nc.vector.tensor_scalar(NT[2][:, :], NT[1][:, :], float(P), None, ALU.mult).then_inc(s.places, 1)
                nc.vector.tensor_tensor(PLACE[0:T, :, :], CUM[1][0:T, :, :],
                                        bank[2][0:T, 0:B * E0].rearrange("p (b e) -> p b e", b=B), ALU.add).then_inc(s.places, 1)
                dve.wait_ge(s.places, 23)
                nc.vector.tensor_scalar(TX[1][:, :], TX[0][:, :], float(E0 - 1), None, ALU.min).then_inc(s.places, 1)
                nc.vector.tensor_tensor(PLACE[0:T, :, :], PLACE[0:T, :, :],
                                        NT[2][0:T, :].rearrange("p (o e) -> p o e", o=1).broadcast_to([T, B, E0]),
                                        ALU.add).then_inc(s.places, 1)
                dve.wait_ge(s.places, 25)
                nc.vector.tensor_copy(TXI[:, :], TX[1][:, :]).then_inc(s.places, 1)
                nc.vector.tensor_tensor(PLACE[0:T, :, :], PLACE[0:T, :, :], OH[0:T, :, :], ALU.mult).then_inc(s.places, 1)
                dve.wait_ge(s.places, 27)
                nc.vector.reduce_sum(PF[0:T, :], PLACE[0:T, :, :], axis=AXX).then_inc(s.places, 1)
                dve.wait_ge(s.places, 28)
                dve.wait_ge(s.xr_copied, B)
                nc.vector.tensor_copy(PI[0:T, :], PF[0:T, :]).then_inc(s.places, 1)

                def tile(i, j):
                    for f in range(HID0 // P):
                        n = 8 * i + f
                        dve.wait_ge(s.value, n + 1)
                        dve.wait_ge(s.sigmoid, n + 1)
                        if f == 0:
                            wait_count(dve, s.out, i)
                        nc.vector.scalar_tensor_tensor(AC[:, f, :], bank[4 + f % 2][:, 0:P], B1[j][:, f:f + 1],
                                                       SG[f % 2][:, :], ALU.add, ALU.mult).then_inc(s.hidden, 1)
                    dve.wait_ge(s.out, i + 1)
                    wait_count(dve, (s.y_stored0, s.y_stored1)[j], 16 * (i // 2))
                    nc.vector.tensor_tensor(YR[j][:, :], bank[6 + j][:, 0:D], B2[j][:, :], ALU.add).then_inc(s.y_copied, 1)

                in_turn(dve, tile, TILES0)
                dve.wait_ge(s.gathered, 16 * B)
                nc.vector.scalar_tensor_tensor(X[0:T, :, :], XR0[0:T, :, :], gates[0:T, 4:5], X[0:T, :, :], ALU.mult, ALU.add
                                               ).then_inc(s.resid, 1)
                end(dve)

            def squared_experts():
                s = mx1
                begin(dve, 3)
                for j in range(2):
                    nc.vector.memset(WF[j][0:T, 0:1], 1.0).then_inc(s.ones, 1)
                dve.wait_ge(loaded[3], 16 * n_loads[3])
                dve.wait_ge(loaded[1], 16 * n_loads[1])
                dve.wait_ge(s.ones, 2)
                x_stats(s, 1)

                def route(t, j):
                    first_weight(s, 9, t, j)
                    nc.vector.tensor_scalar(ED[j][0:T, 4:5], ED[j][0:T, 3:4], 1.0, None, ALU.is_ge).then_inc(s.route, 1)
                    dve.wait_ge(s.route, 9 * t + 8)
                    nc.vector.tensor_scalar(WF[j][0:T, 1:9], iota[0:T, :], IF[j][0:T, 0:1], ED[j][0:T, 4:5],
                                            ALU.is_equal, ALU.mult).then_inc(s.route, 1)
                    dve.wait_ge(s.route, 9 * t + 9)

                def mask(t, j, g):
                    dve.wait_ge(s.squared, 3 * t + g + 1)
                    v = SQ[g][0:T, :].rearrange("p (e n) -> p e n", e=3)
                    w = WF[j][0:T, 3 * g:3 * g + 3].rearrange("p (e o) -> p e o", o=1).broadcast_to([T, 3, HID1])
                    nc.vector.tensor_tensor(v, v, w, ALU.mult).then_inc(s.masked, 1)

                def h_copy(t, j, g):
                    dve.wait_ge(s.h_turned, 3 * t + g + 1)
                    nc.vector.tensor_copy(HT[g][:, :, :], bank[5 + (3 * j + g) % 2][:, 0:3 * T].rearrange("p (c t) -> p c t", c=3)
                                          ).then_inc(s.h_copied, 1)

                def residual(t, j):
                    dve.wait_ge(s.out, t + 1)
                    xt = X[0:T, bass.ds(t, 1), :].rearrange("p o d -> p (o d)")
                    nc.vector.scalar_tensor_tensor(xt, bank[7][0:T, 0:D], gates[0:T, 5:6], xt, ALU.mult, ALU.add
                                                   ).then_inc(s.resid, 1)

                def prepare(t, j):
                    x_norm(s, 0, 0)
                    x_norm(s, 1, 1)
                    choose(s, 9, t, j)
                    route(t, j)
                    for g in range(3):
                        mask(t, j, g)

                def attend(t, j, more):
                    h_copy(t, j, 0)
                    if more:
                        choose(s, 9, t + 1, 1 - j)
                    h_copy(t, j, 1)
                    if more:
                        route(t + 1, 1 - j)
                    h_copy(t, j, 2)
                    if more:
                        mask(t + 1, 1 - j, 0)
                    residual(t, j)
                    if two_follow(t, more):
                        x_norm(s, t + 2, j)
                    if more:
                        mask(t + 1, 1 - j, 1)
                        mask(t + 1, 1 - j, 2)

                pipelined(dve, prepare, attend, lambda t, j: None)
                end(dve)

            def linear_experts():
                s = mx2
                begin(dve, 5)
                dve.wait_ge(loaded[5], 16 * n_loads[5])
                dve.wait_ge(loaded[1], 16 * n_loads[1])
                x_stats(s, 2)

                def route(t, j):
                    first_weight(s, 11, t, j)
                    nc.vector.tensor_tensor(ED[j][0:T, 4:5], ED[j][0:T, 1:2], ED[j][0:T, 3:4], ALU.mult).then_inc(s.route, 1)
                    nc.vector.tensor_scalar(WF[j][0:T, 0:8], iota[0:T, :], IF[j][0:T, 0:1], ED[j][0:T, 3:4],
                                            ALU.is_equal, ALU.mult).then_inc(s.route, 1)
                    dve.wait_ge(s.route, 11 * t + 8)
                    nc.vector.tensor_scalar(WB[j][0:T, :], iota[0:T, :], IF[j][0:T, 1:2], ED[j][0:T, 4:5],
                                            ALU.is_equal, ALU.mult).then_inc(s.route, 1)
                    dve.wait_ge(s.route, 11 * t + 10)
                    nc.vector.tensor_tensor(WF[j][0:T, 0:8], WF[j][0:T, 0:8], WB[j][0:T, :], ALU.add).then_inc(s.route, 1)
                    dve.wait_ge(s.route, 11 * t + 11)

                def combine(t, j, g):
                    dve.wait_ge(s.out, 4 * t + g + 1)
                    for k in range(2):
                        e = 2 * g + k
                        y, w = bank[2 + g][0:T, k * D:(k + 1) * D], WF[j][0:T, e:e + 1]
                        if e == 0:
                            wait_count(dve, s.resid, t)
                            nc.vector.tensor_scalar(ACC[0:T, :], y, w, None, ALU.mult).then_inc(s.combined, 1)
                        else:
                            dve.wait_ge(s.combined, 8 * t + e)
                            nc.vector.scalar_tensor_tensor(ACC[0:T, :], y, w, ACC[0:T, :], ALU.mult, ALU.add
                                                           ).then_inc(s.combined, 1)

                def prepare(t, j):
                    x_norm(s, 0, 0)
                    x_norm(s, 1, 1)
                    choose(s, 11, t, j)
                    route(t, j)

                def attend(t, j, more):
                    if more:
                        choose(s, 11, t + 1, 1 - j)
                    if two_follow(t, more):
                        x_norm(s, t + 2, j)
                    for g in range(4):
                        combine(t, j, g)
                        if g == 1 and more:
                            route(t + 1, 1 - j)
                    dve.wait_ge(s.combined, 8 * (t + 1))
                    xt = X[0:T, bass.ds(t, 1), :].rearrange("p o d -> p (o d)")
                    nc.vector.scalar_tensor_tensor(xt, ACC[0:T, :], gates[0:T, 6:7], xt, ALU.mult, ALU.add
                                                   ).then_inc(s.resid, 1)

                pipelined(dve, prepare, attend, lambda t, j: None)
                end(dve)

            def slot_mixer():
                s = mx3
                begin(dve, 7)
                x_stats(s, 3)
                for k in range(2):
                    nc.vector.memset(pair[k].ALP[0:T, 0, NS:P], 0.0)
                    nc.vector.memset(pair[k].ALP[0:T, 1, 0:NS], 0.0)
                nc.vector.memset(XS[0:T, :, D:D + 1], 1.0).then_inc(s.consts, 1)
                dve.wait_ge(s.w_in, 16 * len(slot_loads))
                nc.vector.reduce_sum(MEAN[:, :, :].rearrange("p c o -> p (c o)"), SIT[:, :, 0:NS], axis=AXX
                                     ).then_inc(s.consts, 1)
                nc.vector.tensor_scalar(TAU[:, 1:2], TAU[:, 0:1], -1.0, None, ALU.mult).then_inc(s.consts, 1)
                dve.wait_ge(s.consts, 3)
                nc.vector.tensor_scalar(MEAN[:, :, :], MEAN[:, :, :], 1.0 / NS, None, ALU.mult).then_inc(s.consts, 1)
                nc.vector.tensor_tensor(TAU[:, 0:1], TAU[:, 0:1], TAU[:, 1:2], ALU.max).then_inc(s.consts, 1)
                dve.wait_ge(s.consts, 5)
                nc.vector.tensor_scalar(TAU[:, 1:2], TAU[:, 0:1], 0.1, None, ALU.add).then_inc(s.consts, 1)
                dve.wait_ge(s.consts, 6)
                nc.vector.reciprocal(TAU[:, 0:1], TAU[:, 1:2]).then_inc(s.consts, 1)
                dve.wait_ge(s.const_sums, 1)
                nc.vector.tensor_tensor(GH[:, 0:512], bank[4][:, :], Sbhh[:, 0:512], ALU.add).then_inc(s.consts, 1)
                nc.vector.tensor_tensor(Sb1[:, :], bank[6][:, 0:1], Sb1[:, :], ALU.add).then_inc(s.consts, 1)
                dve.wait_ge(s.consts, 9)
                nc.vector.tensor_tensor(GH[:, 512:768], bank[5][:, 0:D], Sbhh[:, 512:768], ALU.add).then_inc(s.consts, 1)
                nc.vector.tensor_tensor(GH[:, 0:512], GH[:, 0:512], Sbih[:, 0:512], ALU.add).then_inc(s.consts, 1)
                dve.wait_ge(s.consts, 11)

                def prepare(t, j):
                    wait_count(dve, s.picked, 2 * (t - 1))
                    x_norm(s, t, j)

                def attend(t, j, more):
                    if more:
                        prepare(t + 1, 1 - j)
                    dve.wait_ge(s.ln_x, B + 1 + t + 1)
                    nc.vector.tensor_copy(XS[0:T, bass.ds(t, 1), 0:D].rearrange("p o d -> p (o d)"), FX[j][0:T, :]
                                          ).then_inc(s.picked, 1)
                    dve.wait_ge(s.logits, t + 1)
                    nc.vector.tensor_tensor(LS[0:T, bass.ds(t, 1), :].rearrange("p o n -> p (o n)"), bank[3][0:T, 0:NS],
                                            Sb2[0:T, :], ALU.add).then_inc(s.picked, 1)

                pipelined(dve, prepare, attend, lambda t, j: None)
                dve.wait_ge(s.picked, 2 * B)
                nc.vector.tensor_scalar(LS[0:T, :, :], LS[0:T, :, :], TAU[0:T, 0:1], None, ALU.mult).then_inc(s.picked, 1)
                dve.wait_ge(s.picked, 2 * B + 1)
                for t in range(B):
                    nc.vector.max(LV[0:T, t, :], LS[0:T, t, :]).then_inc(s.picked, 1)
                dve.wait_ge(s.picked, 3 * B + 1)
                for t in range(B):
                    nc.vector.match_replace(out=LR[0:T, t, :], in_to_replace=LV[0:T, t, :], in_values=LS[0:T, t, :],
                                            imm_value=-3.0e38).then_inc(s.picked, 1)
                dve.wait_ge(s.picked, 4 * B + 1)
                nc.vector.tensor_tensor(LR[0:T, :, :], LR[0:T, :, :], LS[0:T, :, :], ALU.is_equal).then_inc(s.picked, 1)
                dve.wait_ge(s.picked, 4 * B + 2)
                nc.vector.tensor_tensor(LS[0:T, :, :], LS[0:T, :, :], LV[0:T, :, 0:1].broadcast_to([T, B, NS]), ALU.subtract
                                        ).then_inc(s.picked, 1)
                dve.wait_ge(s.picked, 4 * B + 3)
                nc.vector.scalar_tensor_tensor(ML[0:T, :, :], LR[0:T, :, :], FAR, LS[0:T, :, :], ALU.mult, ALU.add
                                               ).then_inc(s.picked, 1)
                dve.wait_ge(s.picked, 4 * B + 4)

                def alpha(u, k):
                    w = pair[k]
                    dve.wait_ge(s.exped, u + 1)
                    nc.vector.reciprocal(w.AR[0:T, :], w.AS[0:T, :]).then_inc(s.alpha, 1)
                    dve.wait_ge(s.alpha, 3 * u + 1)
                    for m in range(2):
                        nc.vector.tensor_scalar(w.ALP[0:T, m, m * NS:(m + 1) * NS], w.AL[0:T, m, :], w.AR[0:T, m:m + 1],
                                                None, ALU.mult).then_inc(s.alpha, 1)

                def pooled(u, k):
                    w = pair[k]
                    dve.wait_ge(s.sums, u + 1)
                    nc.vector.tensor_scalar(w.DEN[:, :], bank[4 * k][:, D:D + 1], 1e-8, None, ALU.add).then_inc(s.pooled, 1)
                    dve.wait_ge(s.pooled, 3 * u + 1)
                    nc.vector.reciprocal(w.DEN[:, :], w.DEN[:, :]).then_inc(s.pooled, 1)
                    dve.wait_ge(s.pooled, 3 * u + 2)
                    nc.vector.tensor_scalar(w.SU[:, :], bank[4 * k][:, 0:D], w.DEN[:, 0:1], None, ALU.mult
                                            ).then_inc(s.pooled, 1)

                def alpha_copy(u, k):
                    dve.wait_ge(s.alpha_turned, u + 1)
                    nc.vector.tensor_copy(pair[k].ALT[:, :], bank[4 * k + 1][:, 0:T]).then_inc(s.alpha_copied, 1)

                def rz_in(u, k):
                    dve.wait_ge(s.gru_in, u + 1)
                    nc.vector.tensor_tensor(pair[k].RZ[:, :], bank[4 * k + 2][:, :], GH[:, 0:512], ALU.add).then_inc(s.rz_in, 1)
                    nc.vector.tensor_tensor(pair[k].NN[:, :], bank[4 * k + 3][:, 0:D], Sbih[:, 512:768], ALU.add
                                            ).then_inc(s.rz_in, 1)

                def rz_done(u, k):
                    w = pair[k]
                    dve.wait_ge(s.rz_tanh, u + 1)
                    nc.vector.tensor_scalar(w.RZ[:, :], w.RZ[:, :], 0.5, 0.5, ALU.mult, ALU.add).then_inc(s.rz_done, 1)
                    dve.wait_ge(s.rz_done, 3 * u + 1)
                    nc.vector.tensor_tensor(w.RZ[:, 0:D], w.RZ[:, 0:D], GH[:, 512:768], ALU.mult).then_inc(s.rz_done, 1)
                    dve.wait_ge(s.rz_done, 3 * u + 2)
                    nc.vector.tensor_tensor(w.NN[:, :], w.NN[:, :], w.RZ[:, 0:D], ALU.add).then_inc(s.rz_done, 1)

                def slots_new(u, k):
                    w = pair[k]
                    dve.wait_ge(s.n_tanh, u + 1)
                    nc.vector.tensor_tensor(w.S[:, :], SI[:, :], w.NN[:, :], ALU.subtract).then_inc(s.slots_new, 1)
                    dve.wait_ge(s.slots_new, 3 * u + 1)
                    nc.vector.tensor_tensor(w.S[:, :], w.S[:, :], w.RZ[:, D:2 * D], ALU.mult).then_inc(s.slots_new, 1)
                    dve.wait_ge(s.slots_new, 3 * u + 2)
                    nc.vector.tensor_tensor(w.S[:, :], w.S[:, :], w.NN[:, :], ALU.add).then_inc(s.slots_new, 1)

                def v_done(u, k):
                    dve.wait_ge(s.qkv, u + 1)
                    nc.vector.tensor_tensor(pair[k].VS[:, :], bank[4 * k + 3][:, 0:D], Sbv[:, :], ALU.add
                                            ).then_inc(s.v_done, 1)

                def masked(u, k):
                    w = pair[k]
                    dve.wait_ge(s.attn, u + 1)
                    nc.vector.scalar_tensor_tensor(w.AT[:, :], bank[4 * k + 2][:, 0:P], float(DQ) ** -0.5, BD[:, :],
                                                   ALU.mult, ALU.add).then_inc(s.masked, 1)
                    dve.wait_ge(s.masked, 2 * u + 1)
                    nc.vector.tensor_reduce(w.AX[:, :], w.AT[:, :], axis=AXX, op=ALU.max, negate=True).then_inc(s.masked, 1)

                def attn_copy(u, k):
                    w = pair[k]
                    dve.wait_ge(s.attn_turned, u + 1)
                    nc.vector.tensor_copy(w.ATT[:, :], bank[4 * k + 3][:, 0:P]).then_inc(s.attn_copied, 1)
                    nc.vector.reciprocal(w.AI[:, :], w.AU[:, :]).then_inc(s.attn_copied, 1)

                def y_stats(u, k):
                    w = pair[k]
                    dve.wait_ge(s.comm, u + 1)
                    dve.wait_ge(s.attn_copied, 2 * (u + 1))
                    nc.vector.scalar_tensor_tensor(w.Y[:, :], bank[4 * k + 2][:, 0:D], w.AI[:, 0:1], w.S[:, :],
                                                   ALU.mult, ALU.add).then_inc(s.y_stats, 1)
                    dve.wait_ge(s.y_stats, 4 * u + 1)
                    nc.vector.bn_stats(w.y6[:, :], w.Y[:, :]).then_inc(s.y_stats, 1)
                    dve.wait_ge(s.y_stats, 4 * u + 2)
                    apart(dve)
                    nc.vector.bn_aggr(w.ymv[:, :], w.y6[:, :]).then_inc(s.y_stats, 1)
                    dve.wait_ge(s.y_stats, 4 * u + 3)
                    nc.vector.tensor_scalar(w.yrs[:, :], w.ymv[:, 1:2], LN_EPS, None, ALU.add).then_inc(s.y_stats, 1)

                def y_norm(u, k):
                    w = pair[k]
                    dve.wait_ge(s.rstd_y, u + 1)
                    nc.vector.tensor_scalar(w.Y[:, :], w.Y[:, :], w.ymv[:, 0:1], w.yrs[:, :], ALU.subtract, ALU.mult
                                            ).then_inc(s.y_normed, 1)

                def values_done(u, k):
                    dve.wait_ge(s.values, u + 1)
                    nc.vector.tensor_tensor(pair[k].SV[:, :], bank[4 * k + 1][:, 0:D], Sbvp[:, :], ALU.add
                                            ).then_inc(s.values_done, 1)

                def residual(u, k):
                    dve.wait_ge(s.out, u + 1)
                    r = pair[k].RZ[0:T, :].rearrange("p (m d) -> p m d", m=2)
                    nc.vector.tensor_tensor(r, bank[4 * k + 2][0:T, :].rearrange("p (m d) -> p m d", m=2),
                                            Sbo[0:T, :].rearrange("p (o d) -> p o d", o=1).broadcast_to([T, 2, D]), ALU.add
                                            ).then_inc(s.resid, 1)
                    dve.wait_ge(s.resid, 2 * u + 1)
                    xt = X[0:T, bass.ds(2 * u, 2), :]
                    nc.vector.scalar_tensor_tensor(xt, r, gates[0:T, 7:8], xt, ALU.mult, ALU.add).then_inc(s.resid, 1)

                with dve.Fori(0, B // 4) as i:
                    for stage in (alpha, pooled, alpha_copy, rz_in, rz_done, slots_new, v_done, masked, attn_copy, y_stats,
                                  y_norm, values_done, residual):
                        stage(2 * i, 0)
                        stage(2 * i + 1, 1)
                end(dve)

            for p in range(PHASES):
                if p % 2 == 0:
                    attention(p // 2)
                else:
                    (routed_experts, squared_experts, linear_experts, slot_mixer)[p // 2]()

        @block.tensor
        def _(pe):
            pe.wait_ge(start.consts, 16)

            def attention(L):
                s = at[L]
                H, W, NK, CH = HEADS[L], HWID[L], KEYS[L], CHUNKS[L]
                VN = 512 if L == 1 else 256
                MQ = 4 if L == 1 else 2
                begin(pe, 2 * L)
                wait_for(pe, s.cleared, 1)
                pe.wait_ge(loaded[2 * L], 16 * n_loads[2 * L])

                def step(t, j, n):
                    dst = J_bank[(j * STEPS[L] + n) % 2]
                    wait_for(pe, s.copied, STEPS[L] * t + n - 1)
                    done = STEPS[L] * t
                    mm, tr = nc.tensor.matmul, nc.tensor.transpose

                    def ctx_turn(c):
                        if c == 0:
                            wait_for(pe, s.ln_ctx, 10 * (t + 1))
                        else:
                            apart(pe)
                        for k in range(NCH):
                            ins = tr(dst[0:CW[c], k * P:(k + 1) * P], CNorm[j][:, k, c * P:c * P + CW[c]], ident[:, :])
                        return ins

                    def x_turn():
                        wait_for(pe, s.ln_x, 4 * NORMS[L] * (t + 1))
                        src = XN2[j] if NORMS[L] == 2 else XN[j]
                        for c in range(2):
                            ins = tr(dst[:, c * T:(c + 1) * T], src[0:T, c * P:(c + 1) * P], ident[0:T, 0:T])
                        return ins

                    def rows(lhs, parts, w, n_out, m_out):
                        for c in range(2):
                            ins = mm(dst[0:m_out, 0:n_out], lhs(c), w[0:parts[c], c, 0:n_out], start=(c == 0), stop=(c == 1))
                        return ins

                    if L == 0:
                        if n in (0, 1):
                            ins = ctx_turn(n)
                        elif n == 2:
                            ins = x_turn()
                        elif n in (5, 6, 7):
                            k = BY_CHUNK[n - 3]
                            ins = rows(lambda c: CT[j][0:CW[c], c, k * P:(k + 1) * P], CW, wkv0, 512, P)
                        elif n == 4:
                            ins = rows(lambda c: XT[j][:, c, :], (P, P), wlkv0, 512, P)
                        elif n == 3:
                            wait_for(pe, s.copied, done + 3)
                            ins = rows(lambda c: XT[j][:, c, 0:T], (P, P), wq[0], D, T)
                        elif n in (8, 9):
                            m = n - 8
                            wait_for(pe, s.qk_rms, 20 * (t + 1))
                            for k in range(4):
                                ins = tr(dst[:, k * P:(k + 1) * P], QK[j][:, k, m * P:(m + 1) * P], ident[:, :])
                        else:
                            for m in range(2):
                                ins = tr(dst[:, m * T:(m + 1) * T], QK[j][0:T, 4, m * P:(m + 1) * P], ident[0:T, 0:T])
                    elif L == 3:
                        if n == 0:
                            ins = x_turn()
                        elif n in (1, 2):
                            ins = ctx_turn(n - 1)
                        elif n == 3:
                            wait_for(pe, s.copied, done + 1)
                            for m in range(2):
                                for c in range(2):
                                    ins = mm(dst[:, m * T:(m + 1) * T], wq[3][:, c, m * P:(m + 1) * P], XT[j][:, c, 0:T],
                                             start=(c == 0), stop=(c == 1))
                        else:
                            wait_for(pe, s.copied, done + 4)
                            for c, (lo, m) in enumerate(((0, P), (P, CW[1] + 1))):
                                for e in range(2):
                                    ins = mm(dst[0:m, c * T:(c + 1) * T], wk3[:, e, lo:lo + m], QT[j][:, e, :],
                                             start=(e == 0), stop=(e == 1))
                    else:
                        if n == 0:
                            ins = x_turn()
                        elif n == 1:
                            wait_for(pe, s.copied, done + 1)
                            for m in range(MQ):
                                for c in range(2):
                                    ins = mm(dst[:, m * T:(m + 1) * T], wq[L][:, c, m * P:(m + 1) * P], XT[j][:, c, 0:T],
                                             start=(c == 0), stop=(c == 1))
                        elif n < 2 + MQ:
                            m = n - 2
                            if m == 0:
                                wait_for(pe, (s.ctx_in0, s.ctx_in1)[j], 32 * (t // 2 + 1))
                            for c in range(2):
                                ins = mm(dst[:, 0:NC], wk[L][0:CW[c], c, m * P:(m + 1) * P], CT[j][0:CW[c], c, 0:NC],
                                         start=(c == 0), stop=(c == 1))
                        else:
                            k = n - 2 - MQ
                            ins = rows(lambda c: CT[j][0:CW[c], c, k * P:(k + 1) * P], CW, wv[L], VN, P)
                    ins.then_inc(s.proj.sem, 1)

                def scores(t, j, h):
                    n = H * t + h
                    k = (H * j + h) % 2
                    wait_for(pe, s.exped, n - 1)
                    if h == 0:
                        wait_for(pe, s.copied, STEPS[L] * (t + 1))
                    if H == 1:
                        for c, m in ((0, P), (1, CW[1] + 1)):
                            ins = nc.tensor.matmul(S_bank[k][0:T, 0:NK], QT[j][0:m, 2 + c, :], CT[j][0:m, c, 0:NK],
                                                   start=(c == 0), stop=(c == 1))
                    else:
                        m, b = h // 2, W * (h % 2)
                        ins = nc.tensor.matmul(S_bank[k][0:T, 0:NK], QT[j][b:b + W, m, :], kt(L, j)[b:b + W, m, 0:NK],
                                               start=True, stop=True)
                    ins.then_inc(s.scores.sem, 1)

                def probs_turn(t, j, h):
                    n = H * t + h
                    k = (H * j + h) % 2
                    wait_for(pe, s.exped, n + 1)
                    wait_for(pe, s.probs_copied, n - 1)
                    for c in range(CH):
                        ins = nc.tensor.transpose(PT_bank[k][:, c * T:(c + 1) * T], PR[k][0:T, c, :], ident[0:T, 0:T])
                    ins.then_inc(s.probs_turned.sem, 1)

                def weigh(t, j, h):
                    n = H * t + h
                    k = (H * j + h) % 2
                    wait_for(pe, s.probs_copied, n + 1)
                    if h == 0:
                        wait_for(pe, s.o_scaled, 2 * t)
                    for c in range(CH):
                        if H == 1:
                            to, values = O_bank[0:T, 0:DC], CNorm[j][:, c, :]
                        else:
                            to, values = O_bank[0:T, h * W:(h + 1) * W], vv(L, j)[:, c, h * W:(h + 1) * W]
                        ins = nc.tensor.matmul(to, PT[k][:, c, :], values, start=(c == 0), stop=(c == CH - 1))
                    ins.then_inc(s.pv.sem, 1)

                def o_turn(t, j):
                    wait_for(pe, s.o_scaled, 2 * (t + 1))
                    wait_for(pe, s.resid, 2 * t)
                    for m in range(H * W // P):
                        n = CW[m] if L == 3 else P
                        ins = nc.tensor.transpose(R_bank[0:n, m * T:(m + 1) * T], O[0:T, m * P:m * P + n], ident[0:T, 0:T])
                    ins.then_inc(s.o_turned.sem, 1)

                def value(t, j):
                    wait_for(pe, s.o_copied, t + 1)
                    for m in range(2):
                        for c in range(2):
                            ins = nc.tensor.matmul(R_bank[:, m * T:(m + 1) * T], wv[3][0:CW[c], c, m * P:(m + 1) * P],
                                                   OT[0:CW[c], c, :], start=(c == 0), stop=(c == 1))
                    ins.then_inc(s.valued.sem, 1)

                def project(t, j):
                    if L == 3:
                        wait_for(pe, s.v_copied, t + 1)
                    else:
                        wait_for(pe, s.o_copied, t + 1)
                    M = H * W // P
                    for m in range(M):
                        ins = nc.tensor.matmul(R_bank[0:T, 0:D], OT[:, (2 if L == 3 else 0) + m, :], wo[L][:, m, :],
                                               start=(m == 0), stop=(m == M - 1))
                    ins.then_inc(s.out.sem, 1)

                def prepare(t, j):
                    for n in range(STEPS[L]):
                        step(t, j, n)

                def attend(t, j, more):
                    started = not (isinstance(t, int) and t == 0)
                    scores(t, j, 0)
                    if H > 1:
                        scores(t, j, 1)
                    if started:
                        o_turn(t - 1, 1 - j)
                    for n in range(EARLY[L]):
                        if more:
                            step(t + 1, 1 - j, n)
                        if L == 3 and n == 0 and started:
                            value(t - 1, 1 - j)
                    if L == 3 and started:
                        project(t - 1, 1 - j)
                    probs_turn(t, j, 0)
                    for h in range(H):
                        if h + 2 < H:
                            scores(t, j, h + 2)
                        if h == 0 and L != 3 and started:
                            project(t - 1, 1 - j)
                        if L == 0 and h + 1 < H:
                            probs_turn(t, j, h + 1)
                        for n in GROUPS[L][h]:
                            if more and n >= EARLY[L]:
                                step(t + 1, 1 - j, n)
                        weigh(t, j, h)
                        if L != 0 and h + 1 < H:
                            probs_turn(t, j, h + 1)

                def finish(t, j):
                    o_turn(t, j)
                    if L == 3:
                        value(t, j)
                    project(t, j)

                pipelined(pe, prepare, attend, finish)
                end(pe)


            def x_turn(s, t, j):
                pe.wait_ge(s.ln_x, B + 1 + t + 1)
                wait_count(pe, s.x_copied, t)
                for c in range(2):
                    ins = nc.tensor.transpose(bank[0][:, c * T:(c + 1) * T], FX[j][0:T, c * P:(c + 1) * P], ident[0:T, 0:T])
                ins.then_inc(s.x_turned, 1)

            def logits(s, w, n_route, t, j):
                pe.wait_ge(s.x_copied, t + 1)
                wait_count(pe, s.route, n_route * (t - 1) + 1)
                for c in range(2):
                    ins = nc.tensor.matmul(bank[1][0:T, 0:8], FXT[j][:, c, :], w[:, c, :], start=(c == 0), stop=(c == 1))
                ins.then_inc(s.logits, 1)

            def routed_experts():
                s = mx0
                begin(pe, 1)
                pe.wait_ge(loaded[1], 16 * n_loads[1])

                def attend(t, j, more):
                    pe.wait_ge(s.x_copied, t + 1)
                    if more:
                        x_turn(s, t + 1, 1 - j)
                    logits(s, ew0, 1, t, j)

                pipelined(pe, lambda t, j: x_turn(s, t, j), attend, lambda t, j: None)
                pe.wait_ge(start.zeros, 2)
                pe.wait_ge(s.route, 3 * B + 2)
                choices = OH[0:T, :, :].rearrange("p b e -> p (b e)")
                nc.tensor.matmul(bank[2][0:T, 0:B * E0], earlier[0:T, 0, :], choices, start=True, stop=True)
                nc.tensor.matmul(bank[3][:, 0:B * E0], ones[0:T, :], choices, start=True, stop=True).then_inc(s.ranks, 1)
                pe.wait_ge(s.places, PLACED)

                def rows_turn(i, j):
                    pe.wait_ge((s.rows_in0, s.rows_in1)[j], 16 * (i // 2 + 1))
                    wait_count(pe, s.rows_copied, i)
                    for c in range(2):
                        ins = nc.tensor.transpose(bank[0][:, c * P:(c + 1) * P], TR[j][:, c * P:(c + 1) * P], ident[:, :])
                    ins.then_inc(s.rows_turned, 1)

                def tile(i, j, more):
                    pe.wait_ge(s.rows_copied, i + 1)
                    pe.wait_ge((s.w1_in0, s.w1_in1)[j], 48 * (i // 2 + 1))
                    for f in range(HID0 // P):
                        n = 8 * i + f
                        for half, to, sig, used in ((1, 2, s.gate, s.sigmoid), (0, 4, s.value, s.hidden)):
                            wait_count(pe, used, n - 1)
                            for c in range(2):
                                col = half * HID0 + f * P
                                ins = nc.tensor.matmul(bank[to + f % 2][:, 0:P], W1[j][:, c, col:col + P], TT[j][:, c, :],
                                                       start=(c == 0), stop=(c == 1))
                            ins.then_inc(sig, 1)
                    if more:
                        rows_turn(i + 1, 1 - j)
                    pe.wait_ge(s.hidden, 8 * (i + 1))
                    wait_count(pe, s.y_copied, i - 1)
                    pe.wait_ge((s.w2_in0, s.w2_in1)[j], 32 * (i // 2 + 1))
                    for f in range(HID0 // P):
                        ins = nc.tensor.matmul(bank[6 + j][:, 0:D], AC[:, f, :], W2[j][:, f, :],
                                               start=(f == 0), stop=(f == HID0 // P - 1))
                    ins.then_inc(s.out, 1)

                pipelined(pe, rows_turn, tile, lambda i, j: None, TILES0)
                end(pe)

            def squared_experts():
                s = mx1
                begin(pe, 3)
                pe.wait_ge(loaded[3], 16 * n_loads[3])

                def hidden(t, j, g):
                    wait_count(pe, s.relu, 3 * (t - 1) + g + 1)
                    for c in range(2):
                        ins = nc.tensor.matmul(bank[2 + g][0:T, 0:3 * HID1], FXT[j][:, c, :],
                                               up1[:, c, 3 * HID1 * g:3 * HID1 * (g + 1)], start=(c == 0), stop=(c == 1))
                    ins.then_inc(s.hidden, 1)

                def turn(t, j, g):
                    pe.wait_ge(s.masked, 3 * t + g + 1)
                    wait_count(pe, s.h_copied, 3 * t + g - 1)
                    for k in range(3):
                        ins = nc.tensor.transpose(bank[5 + (3 * j + g) % 2][:, k * T:(k + 1) * T],
                                                  SQ[g][0:T, k * HID1:(k + 1) * HID1], ident[0:T, 0:T])
                    ins.then_inc(s.h_turned, 1)

                def down(t, j, g):
                    pe.wait_ge(s.h_copied, 3 * t + g + 1)
                    if g == 0:
                        wait_count(pe, s.resid, t)
                    for k in range(3):
                        ins = nc.tensor.matmul(bank[7][0:T, 0:D], HT[g][:, k, :], down1[:, 3 * g + k, :],
                                               start=(g == 0 and k == 0), stop=(g == 2 and k == 2))
                    if g == 2:
                        ins.then_inc(s.out, 1)

                def prepare(t, j):
                    x_turn(s, 0, 0)
                    x_turn(s, 1, 1)
                    logits(s, ew1, 9, t, j)
                    for g in range(3):
                        hidden(t, j, g)

                def attend(t, j, more):
                    turn(t, j, 0)
                    if more:
                        logits(s, ew1, 9, t + 1, 1 - j)
                    turn(t, j, 1)
                    down(t, j, 0)
                    down(t, j, 1)
                    turn(t, j, 2)
                    if more:
                        hidden(t + 1, 1 - j, 0)
                    down(t, j, 2)
                    if more:
                        hidden(t + 1, 1 - j, 1)
                    if two_follow(t, more):
                        x_turn(s, t + 2, j)
                    if more:
                        hidden(t + 1, 1 - j, 2)

                pipelined(pe, prepare, attend, lambda t, j: None)
                end(pe)

            def linear_experts():
                s = mx2
                begin(pe, 5)
                pe.wait_ge(loaded[5], 16 * n_loads[5])

                def experts(t, j, g):
                    wait_count(pe, s.combined, 8 * (t - 1) + 2 * g + 2)
                    for c in range(2):
                        ins = nc.tensor.matmul(bank[2 + g][0:T, :], FXT[j][:, c, :],
                                               lin2[:, c, 2 * g:2 * g + 2, :].rearrange("p e n -> p (e n)"),
                                               start=(c == 0), stop=(c == 1))
                    ins.then_inc(s.out, 1)

                def prepare(t, j):
                    x_turn(s, 0, 0)
                    x_turn(s, 1, 1)
                    logits(s, ew2, 11, t, j)

                def attend(t, j, more):
                    if more:
                        logits(s, ew2, 11, t + 1, 1 - j)
                    for g in range(4):
                        experts(t, j, g)
                    if two_follow(t, more):
                        x_turn(s, t + 2, j)

                pipelined(pe, prepare, attend, lambda t, j: None)
                end(pe)

            def slot_mixer():
                s = mx3
                begin(pe, 7)
                pe.wait_ge(s.w_in, 16 * len(slot_loads))
                mm, tr = nc.tensor.matmul, nc.tensor.transpose
                for c in range(2):
                    mm(bank[4][:, :], SIT[:, c, :], SWhh[:, c, 0:512], start=(c == 0), stop=(c == 1))
                for c in range(2):
                    mm(bank[5][:, 0:D], SIT[:, c, :], SWhh[:, c, 512:768], start=(c == 0), stop=(c == 1))
                pe.wait_ge(s.consts, 4)
                for c in range(2):
                    ins = mm(bank[6][:, 0:1], SW1[:, 2 + c, :], MEAN[:, c, :], start=(c == 0), stop=(c == 1))
                ins.then_inc(s.const_sums, 1)

                def prepare(t, j):
                    x_turn(s, t, j)

                def attend(t, j, more):
                    pe.wait_ge(s.x_copied, t + 1)
                    wait_count(pe, s.gelu, t - 1)
                    for c in range(2):
                        ins = mm(bank[1 + j][:, 0:T], SW1[:, c, :], FXT[j][:, c, :], start=(c == 0), stop=(c == 1))
                    ins.then_inc(s.hidden, 1)
                    if more:
                        prepare(t + 1, 1 - j)
                    pe.wait_ge(s.gelu, t + 1)
                    wait_count(pe, s.picked, 2 * t)
                    mm(bank[3][0:T, 0:NS], HG[j][:, :], SW2[:, :], start=True, stop=True).then_inc(s.logits, 1)

                pipelined(pe, prepare, attend, lambda t, j: None)

                def turn(src, k):
                    for c in range(2):
                        ins = tr(bank[4 * k][:, c * P:(c + 1) * P], src[:, c * P:(c + 1) * P], ident[:, :])
                    return ins

                def product(dst, lhs, w, lo, hi):
                    for c in range(2):
                        ins = mm(dst, lhs[:, c, :], w[:, c, lo:hi], start=(c == 0), stop=(c == 1))
                    return ins

                def sums(u, k):
                    pe.wait_ge(s.alpha, 3 * (u + 1))
                    for m in range(2):
                        ins = mm(bank[4 * k][:, 0:D + 1], pair[k].ALP[0:T, m, :],
                                 XS[0:T, bass.ds(2 * u + m, 1), :].rearrange("p o d -> p (o d)"), start=(m == 0), stop=(m == 1))
                    ins.then_inc(s.sums, 1)

                def alpha_turn(u, k):
                    for m in range(2):
                        ins = mm(bank[4 * k + 1][:, 0:T], pair[k].ALP[0:T, m, :], ident[0:T, 0:T], start=(m == 0), stop=(m == 1))
                    ins.then_inc(s.alpha_turned, 1)

                def pooled_turn(u, k):
                    pe.wait_ge(s.pooled, 3 * (u + 1))
                    turn(pair[k].SU, k).then_inc(s.pooled_turned, 1)

                def gru_in(u, k):
                    pe.wait_ge(s.pooled_copied, u + 1)
                    product(bank[4 * k + 2][:, :], pair[k].SUT, SWih, 0, 512)
                    product(bank[4 * k + 3][:, 0:D], pair[k].SUT, SWih, 512, 768).then_inc(s.gru_in, 1)

                def s_turn(u, k):
                    pe.wait_ge(s.slots_new, 3 * (u + 1))
                    turn(pair[k].S, k).then_inc(s.s_turned, 1)

                def qkv(u, k):
                    pe.wait_ge(s.s_copied, u + 1)
                    pe.wait_ge(s.alpha_copied, u + 1)
                    for m, w in ((0, SWq), (1, SWk)):
                        for c in range(2):
                            mm(bank[4 * k + 1][0:DQ, m * P:(m + 1) * P], w[:, c, :], pair[k].ST[:, c, :],
                               start=(c == 0), stop=(c == 1))
                    product(bank[4 * k + 3][:, 0:D], pair[k].ST, SWv, 0, D).then_inc(s.qkv, 1)

                def attn(u, k):
                    pe.wait_ge(s.qk_copied, u + 1)
                    mm(bank[4 * k + 2][:, 0:P], pair[k].QS[0:DQ, 0, :], pair[k].QS[0:DQ, 1, :], start=True, stop=True
                       ).then_inc(s.attn, 1)

                def attn_turn(u, k):
                    pe.wait_ge(s.attn_exped, u + 1)
                    pe.wait_ge(s.v_done, u + 1)
                    tr(bank[4 * k + 3][:, 0:P], pair[k].AT[:, :], ident[:, :]).then_inc(s.attn_turned, 1)

                def comm(u, k):
                    pe.wait_ge(s.attn_copied, 2 * (u + 1))
                    mm(bank[4 * k + 2][:, 0:D], pair[k].ATT[:, :], pair[k].VS[:, :], start=True, stop=True).then_inc(s.comm, 1)

                def y_turn(u, k):
                    pe.wait_ge(s.y_normed, u + 1)
                    turn(pair[k].Y, k).then_inc(s.y_turned, 1)

                def values(u, k):
                    pe.wait_ge(s.y_copied, u + 1)
                    product(bank[4 * k + 1][:, 0:D], pair[k].YT, SWvp, 0, D).then_inc(s.values, 1)

                def mixed(u, k):
                    pe.wait_ge(s.values_done, u + 1)
                    for m in range(2):
                        for c in range(2):
                            ins = mm(bank[4 * k + 3 * (1 - m)][:, c * T:(c + 1) * T],
                                     pair[k].SV[NS * m:NS * (m + 1), c * P:(c + 1) * P], pair[k].ALT[NS * m:NS * (m + 1), :],
                                     start=True, stop=True)
                    ins.then_inc(s.mixed, 1)

                def out_rows(u, k):
                    pe.wait_ge(s.mixed_copied, u + 1)
                    for m in range(2):
                        for c in range(2):
                            ins = mm(bank[4 * k + 2][0:T, m * D:(m + 1) * D], pair[k].MT[:, 2 * m + c, :], SWo[:, c, :],
                                     start=(c == 0), stop=(c == 1))
                    ins.then_inc(s.out, 1)

                with pe.Fori(0, B // 4) as i:
                    for stage in (sums, alpha_turn, pooled_turn, gru_in, s_turn, qkv, attn, attn_turn, comm, y_turn, values,
                                  mixed, out_rows):
                        stage(2 * i, 0)
                        stage(2 * i + 1, 1)
                end(pe)

            for p in range(PHASES):
                if p % 2 == 0:
                    attention(p // 2)
                else:
                    (routed_experts, squared_experts, linear_experts, slot_mixer)[p // 2]()


_OUTS = [((B, T, D), 'float32')]


def layout(inputs):
    import numpy as _np

    v = {k: _np.asarray(x) for k, x in inputs.items()}

    def column(x):
        return _np.pad(x, (0, -len(x) % P)).reshape(-1, P).T

    r = {"x": v["x"], "ctx": v["ctx_768"], "ctxT": v["ctx_768"].transpose(0, 2, 1), "mask": v["mask_BxS2_bk0"],
         "gates": _np.concatenate([v["g_xattn"], v["g_ffn"]]), "ident": _np.eye(P, dtype=_np.float32),
         "L0_WqT": v["L0_xattn_Wq"].T, "L0_WkvT": v["L0_xattn_Wkv"].T, "L0_WlkvT": v["L0_xattn_Wlkv"].T,
         "L0_WoT": v["L0_xattn_Wo"].T, "L2_WoT": v["L2_xattn_Wo"].T,
         "L0_qn_g2": column(_np.tile(v["L0_xattn_qn_g"], 2)), "L0_kn_g2": column(_np.tile(v["L0_xattn_kn_g"], 2))}
    for n in ("Wq", "Wk", "Wv"):
        r[f"L1_{n}"] = v[f"L1_xattn_{n}"]
        r[f"L2_{n}T"] = v[f"L2_xattn_{n}"].T
    for n in ("Wq", "Wv"):
        r[f"L3_{n}"] = v[f"L3_xattn_{n}"]
    r["L3_WkT"] = _np.concatenate([v["L3_xattn_Wk"].T, v["L3_xattn_bk"][:, None]], axis=1)
    r["earlier"] = _np.triu(_np.ones((T, T), dtype=_np.float32), 1)
    r["tile_starts"] = P * _np.arange(STEPS0, dtype=_np.float32)
    r["tile_iota"] = _np.arange(TILES0, dtype=_np.float32)
    r["iota"] = _np.arange(8, dtype=_np.float32)
    for n in ("router_w", "router_b", "b2", "w1", "w2"):
        r[f"F0_{n}"] = v[f"L0_ffn_{n}"]
    r["F0_b1c"] = v["L0_ffn_b1"].reshape(E0, -1, P).transpose(0, 2, 1)
    r["F1_Wr"] = v["L1_ffn_Wr"]
    r["F1_up"] = _np.concatenate([v["L1_ffn_Ws1"][None], v["L1_ffn_W1"]]).transpose(1, 0, 2).reshape(D, -1)
    r["F1_down"] = _np.concatenate([v["L1_ffn_Ws2"][None], v["L1_ffn_W2"]]).reshape(-1, D)
    s = {k[7:]: x for k, x in v.items() if k.startswith("L3_ffn_")}
    for n in ("w1", "w2", "wq", "wk", "wv", "wvp", "wo", "b2", "bih", "bhh", "bv", "bvp", "bo", "tau"):
        r[f"F3_{n}"] = s[n]
    for n in ("b1", "bq", "bk", "ln_g", "ln_b"):
        r[f"F3_{n}"] = column(s[n])
    r["F3_WihT"], r["F3_WhhT"] = s["Wih"].T, s["Whh"].T
    r["F3_slot_init2"] = _np.tile(s["slot_init"], (2, 1))
    r["F3_slot_initT2"] = _np.tile(s["slot_init"].T, (1, 2))
    r["F3_apart"] = _np.kron(1 - _np.eye(2), _np.ones((NS, NS))).astype(_np.float32) * _np.float32(FAR)
    r["F2_gateT"], r["F2_weight"] = v["L2_ffn_gate_w"].T, v["L2_ffn_weight"]
    r["L1_Wo"], r["L3_Wo"] = v["L1_xattn_Wo"], v["L3_xattn_Wo"]
    for L in range(4):
        r[f"L{L}_bo"] = v[f"L{L}_xattn_bo"]
    for n in ("ln_x_g", "ln_x_b", "ln_l_g", "ln_l_b"):
        r[f"L0_{n}"] = column(v[f"L0_xattn_{n}"])
    for n in ("ln1_g", "ln1_b", "ln2_g", "ln2_b", "bq", "bv"):
        r[f"L3_{n}"] = column(v[f"L3_xattn_{n}"])
    return r


def kernel(**inputs):
    import numpy as _np
    import concourse.bacc as _bacc
    from concourse import mybir as _mybir
    from concourse.bass_utils import run_bass_kernel_spmd as _run

    nc = _bacc.Bacc("TRN2", target_bir_lowering=False, num_devices=1)
    arrays, args = {}, {}
    for name, x in layout(inputs).items():
        x = _np.ascontiguousarray(x)
        arrays[f"in_{name}"] = x
        args[name] = nc.dram_tensor(f"in_{name}", x.shape, _mybir.dt.from_np(x.dtype), kind="ExternalInput").ap()
    out = nc.dram_tensor("out_0_dram", _OUTS[0][0], _mybir.dt.float32, kind="ExternalOutput").ap()
    flamingo_kernel(nc, args, out)
    r = _run(nc, [arrays], core_ids=[0])
    return r.results[0]["out_0_dram"]
```
